# Optimizing a Trainium2 kernel written in Bass

```python
import numpy as np
import jax
import jax.numpy as jnp

def _softmax(x, axis=-1):
    return jax.nn.softmax(x, axis=axis)

def _gelu(x):
    return jax.nn.gelu(x, approximate=True)

def _silu(x):
    return jax.nn.silu(x)

def _sigmoid(x):
    return jax.nn.sigmoid(x)

def _layernorm(x, axis=-1, eps=1e-05):
    m = jnp.mean(x, axis=axis, keepdims=True)
    v = jnp.var(x, axis=axis, keepdims=True)
    return (x - m) / jnp.sqrt(v + eps)

def _scatter_add(tgt, idx, src, axis=0):
    return tgt.at[idx].add(src)

def _segment_sum(src, seg, n):
    return jax.ops.segment_sum(src, seg, n)
kernel_name = 'mk_prb_d1_jaxref_r4_e25643'

def setup_inputs(seed: int=0):
    np.random.seed(seed)
    _w = jnp.asarray

    def _L0_attn_setup():
        import jax, jax.numpy as jnp
        import numpy as np
        HID = 256
        NH = 4
        HD = HID // NH
        KS = 4
        C = 64
        EPS = 1e-05
        B = 4
        L = 1024

        def _causal_dwconv(x, w):
            xc = jnp.moveaxis(x, 1, 2)
            y = jax.lax.conv_general_dilated(xc, w, window_strides=(1,), padding=[(w.shape[-1] - 1, 0)], dimension_numbers=('NCH', 'OIH', 'NCH'), feature_group_count=w.shape[0])
            return jnp.moveaxis(jax.nn.silu(y), 1, 2)

        def _forward(x, Wq, Wk, Wv, Wb, conv_q, conv_k, conv_v, g, Wo):
            Bx, Lx, _ = x.shape
            N = Lx // C
            q = _causal_dwconv(x @ Wq, conv_q).reshape(Bx, Lx, NH, HD)
            k = _causal_dwconv(x @ Wk, conv_k).reshape(Bx, Lx, NH, HD)
            v = _causal_dwconv(x @ Wv, conv_v).reshape(Bx, Lx, NH, HD)
            q = q / jnp.linalg.norm(q, axis=-1, keepdims=True)
            k = k / jnp.linalg.norm(k, axis=-1, keepdims=True)
            beta = jax.nn.sigmoid(x @ Wb)
            Q = q.reshape(Bx, N, C, NH, HD)
            K = k.reshape(Bx, N, C, NH, HD)
            V = v.reshape(Bx, N, C, NH, HD)
            bta = beta.reshape(Bx, N, C, NH, 1)
            Kb = K * bta
            Vb = V * bta
            A = jnp.einsum('bnihd,bnjhd->bnij', Kb, K)
            T0 = jnp.eye(C, dtype=x.dtype) - jnp.tril(A, -1)
            col = jnp.arange(C)

            def body(i, T):
                row = jax.lax.dynamic_slice_in_dim(T, i, 1, axis=2)[:, :, 0]
                acc = jnp.einsum('bnj,bnjc->bnc', row, T)
                new_row = jnp.where(col < i, row + acc, row)
                return jax.lax.dynamic_update_slice_in_dim(T, new_row[:, :, None, :], i, axis=2)
            T = jax.lax.fori_loop(1, C, body, T0)
            W = jnp.einsum('bnij,bnjhd->bnihd', T, Kb)
            U = jnp.einsum('bnij,bnjhd->bnihd', T, Vb)

            def chunk_step(S, inp):
                q_i, k_i, w_i, u0 = inp
                Sd = jnp.diagonal(S, axis1=-2, axis2=-1)
                u_i = u0 - w_i * Sd[:, None]
                o_inter = q_i * Sd[:, None]
                A_i = jnp.tril(jnp.einsum('bchd,bchd->bc', q_i, k_i))
                o_intra = A_i[:, :, None, None] * u_i
                S = S + jnp.einsum('bchd,bche->bhde', k_i, u_i)
                return (S, o_inter + o_intra)
            xs = tuple((jnp.moveaxis(a, 1, 0) for a in (Q, K, W, U)))
            S0 = jnp.zeros((Bx, NH, HD, HD), x.dtype)
            S, O = jax.lax.scan(chunk_step, S0, xs)
            o = jnp.moveaxis(O, 0, 1).reshape(Bx, Lx, NH, HD)
            o = o * jax.lax.rsqrt(jnp.mean(o * o, axis=-1, keepdims=True) + EPS) * g
            out = o.reshape(Bx, Lx, NH * HD) @ Wo
            return (out, S)

        def _reference_tuple_inner(x, Wq, Wk, Wv, Wb, conv_q, conv_k, conv_v, g, Wo):
            return _forward(x, Wq, Wk, Wv, Wb, conv_q, conv_k, conv_v, g, Wo)
        key = jax.random.key(seed)
        ks = jax.random.split(key, 9)
        return {'x': jax.random.normal(ks[0], (B, L, HID), jnp.float32), 'Wq': jax.random.normal(ks[1], (HID, HID), jnp.float32) * 0.02, 'Wk': jax.random.normal(ks[2], (HID, HID), jnp.float32) * 0.02, 'Wv': jax.random.normal(ks[3], (HID, HID), jnp.float32) * 0.02, 'Wb': jax.random.normal(ks[4], (HID, NH), jnp.float32) * 0.02, 'conv_q': jax.random.normal(ks[5], (HID, 1, KS), jnp.float32) * 0.5, 'conv_k': jax.random.normal(ks[6], (HID, 1, KS), jnp.float32) * 0.5, 'conv_v': jax.random.normal(ks[7], (HID, 1, KS), jnp.float32) * 0.5, 'g': jnp.ones((HD,), jnp.float32), 'Wo': jax.random.normal(ks[8], (HID, HID), jnp.float32) * 0.02}
    _L0_attn_in = _L0_attn_setup()

    def _L0_ffn_setup():
        import jax, jax.numpy as jnp
        import numpy as np
        B, S, D, F, E = (8, 256, 256, 1024, 8)
        EPS = 1e-05
        key = jax.random.key(seed)
        ks = jax.random.split(key, 4)
        s = 0.02
        return {'input_features': jax.random.normal(ks[0], (B, S, D), jnp.float32), 'centroids': jax.random.normal(ks[1], (E, D), jnp.float32) * 0.1, 'ln_g': jnp.ones((E, D), jnp.float32), 'ln_b': jnp.zeros((E, D), jnp.float32), 'w1': jax.random.normal(ks[2], (E, D, F), jnp.float32) * s, 'b1': jnp.zeros((E, F), jnp.float32), 'w2': jax.random.normal(ks[3], (E, F, D), jnp.float32) * s, 'b2': jnp.zeros((E, D), jnp.float32)}
    _L0_ffn_in = _L0_ffn_setup()
    _d = {'L0_attn_x': _L0_attn_in['x'], 'L0_attn_Wq': _L0_attn_in['Wq'], 'L0_attn_Wk': _L0_attn_in['Wk'], 'L0_attn_Wv': _L0_attn_in['Wv'], 'L0_attn_Wb': _L0_attn_in['Wb'], 'L0_attn_conv_q': _L0_attn_in['conv_q'], 'L0_attn_conv_k': _L0_attn_in['conv_k'], 'L0_attn_conv_v': _L0_attn_in['conv_v'], 'L0_attn_g': _L0_attn_in['g'], 'L0_attn_Wo': _L0_attn_in['Wo'], 'L0_ffn_centroids': _L0_ffn_in['centroids'], 'L0_ffn_ln_g': _L0_ffn_in['ln_g'], 'L0_ffn_ln_b': _L0_ffn_in['ln_b'], 'L0_ffn_w1': _L0_ffn_in['w1'], 'L0_ffn_b1': _L0_ffn_in['b1'], 'L0_ffn_w2': _L0_ffn_in['w2'], 'L0_ffn_b2': _L0_ffn_in['b2']}
    _x0 = _d['L0_attn_x']
    _d['L0_attn_x'] = jax.random.normal(jax.random.fold_in(jax.random.key(seed), 1), (8, 512, 256), dtype=_x0.dtype)
    del _x0
    return _d

def reference(L0_attn_x, L0_attn_Wq, L0_attn_Wk, L0_attn_Wv, L0_attn_Wb, L0_attn_conv_q, L0_attn_conv_k, L0_attn_conv_v, L0_attn_g, L0_attn_Wo, L0_ffn_centroids, L0_ffn_ln_g, L0_ffn_ln_b, L0_ffn_w1, L0_ffn_b1, L0_ffn_w2, L0_ffn_b2):

    def _L0_attn_ref(x, Wq, Wk, Wv, Wb, conv_q, conv_k, conv_v, g, Wo):
        import jax, jax.numpy as jnp
        import numpy as np
        HID = 256
        NH = 4
        HD = HID // NH
        KS = 4
        C = 64
        EPS = 1e-05
        B = 4
        L = 1024

        def _causal_dwconv(x, w):
            xc = jnp.moveaxis(x, 1, 2)
            y = jax.lax.conv_general_dilated(xc, w, window_strides=(1,), padding=[(w.shape[-1] - 1, 0)], dimension_numbers=('NCH', 'OIH', 'NCH'), feature_group_count=w.shape[0])
            return jnp.moveaxis(jax.nn.silu(y), 1, 2)

        def _forward(x, Wq, Wk, Wv, Wb, conv_q, conv_k, conv_v, g, Wo):
            Bx, Lx, _ = x.shape
            N = Lx // C
            q = _causal_dwconv(x @ Wq, conv_q).reshape(Bx, Lx, NH, HD)
            k = _causal_dwconv(x @ Wk, conv_k).reshape(Bx, Lx, NH, HD)
            v = _causal_dwconv(x @ Wv, conv_v).reshape(Bx, Lx, NH, HD)
            q = q / jnp.linalg.norm(q, axis=-1, keepdims=True)
            k = k / jnp.linalg.norm(k, axis=-1, keepdims=True)
            beta = jax.nn.sigmoid(x @ Wb)
            Q = q.reshape(Bx, N, C, NH, HD)
            K = k.reshape(Bx, N, C, NH, HD)
            V = v.reshape(Bx, N, C, NH, HD)
            bta = beta.reshape(Bx, N, C, NH, 1)
            Kb = K * bta
            Vb = V * bta
            A = jnp.einsum('bnihd,bnjhd->bnij', Kb, K)
            T0 = jnp.eye(C, dtype=x.dtype) - jnp.tril(A, -1)
            col = jnp.arange(C)

            def body(i, T):
                row = jax.lax.dynamic_slice_in_dim(T, i, 1, axis=2)[:, :, 0]
                acc = jnp.einsum('bnj,bnjc->bnc', row, T)
                new_row = jnp.where(col < i, row + acc, row)
                return jax.lax.dynamic_update_slice_in_dim(T, new_row[:, :, None, :], i, axis=2)
            T = jax.lax.fori_loop(1, C, body, T0)
            W = jnp.einsum('bnij,bnjhd->bnihd', T, Kb)
            U = jnp.einsum('bnij,bnjhd->bnihd', T, Vb)

            def chunk_step(S, inp):
                q_i, k_i, w_i, u0 = inp
                Sd = jnp.diagonal(S, axis1=-2, axis2=-1)
                u_i = u0 - w_i * Sd[:, None]
                o_inter = q_i * Sd[:, None]
                A_i = jnp.tril(jnp.einsum('bchd,bchd->bc', q_i, k_i))
                o_intra = A_i[:, :, None, None] * u_i
                S = S + jnp.einsum('bchd,bche->bhde', k_i, u_i)
                return (S, o_inter + o_intra)
            xs = tuple((jnp.moveaxis(a, 1, 0) for a in (Q, K, W, U)))
            S0 = jnp.zeros((Bx, NH, HD, HD), x.dtype)
            S, O = jax.lax.scan(chunk_step, S0, xs)
            o = jnp.moveaxis(O, 0, 1).reshape(Bx, Lx, NH, HD)
            o = o * jax.lax.rsqrt(jnp.mean(o * o, axis=-1, keepdims=True) + EPS) * g
            out = o.reshape(Bx, Lx, NH * HD) @ Wo
            return (out, S)

        def _reference_tuple_inner(x, Wq, Wk, Wv, Wb, conv_q, conv_k, conv_v, g, Wo):
            return _forward(x, Wq, Wk, Wv, Wb, conv_q, conv_k, conv_v, g, Wo)
        return _reference_tuple_inner(x, Wq, Wk, Wv, Wb, conv_q, conv_k, conv_v, g, Wo)[0]

    def _L0_ffn_ref(input_features, centroids, ln_g, ln_b, w1, b1, w2, b2):
        import jax, jax.numpy as jnp
        import numpy as np
        B, S, D, F, E = (8, 256, 256, 1024, 8)
        EPS = 1e-05
        x = input_features.reshape(-1, D)
        aff = jax.lax.stop_gradient(x @ centroids.T)
        eid = jnp.argmax(aff, axis=-1)
        alpha = jax.nn.sigmoid(jnp.sum(x * centroids[eid], axis=-1, keepdims=True))
        mu = jnp.mean(x, axis=-1, keepdims=True)
        var = jnp.mean((x - mu) ** 2, axis=-1, keepdims=True)
        xn = (x - mu) * jax.lax.rsqrt(var + EPS)
        xln = xn * ln_g[eid] + ln_b[eid]
        onehot = jax.nn.one_hot(eid, E, dtype=x.dtype)
        ffn = jnp.zeros_like(x)
        for e in range(E):
            h = jax.nn.relu(xln @ w1[e] + b1[e])
            ffn = ffn + onehot[:, e:e + 1] * (h @ w2[e] + b2[e])
        out = x + alpha * ffn
        return out.reshape(input_features.shape)
    x = L0_attn_x
    xn = _layernorm(x, axis=-1)
    x = x + _L0_attn_ref(xn, L0_attn_Wq, L0_attn_Wk, L0_attn_Wv, L0_attn_Wb, L0_attn_conv_q, L0_attn_conv_k, L0_attn_conv_v, L0_attn_g, L0_attn_Wo) + _L0_ffn_ref(xn, L0_ffn_centroids, L0_ffn_ln_g, L0_ffn_ln_b, L0_ffn_w1, L0_ffn_b1, L0_ffn_w2, L0_ffn_b2)
    return x

_drawn_inputs = setup_inputs


def setup_inputs(seed=0):
    import zlib

    import numpy as np

    out = dict(_drawn_inputs(seed))
    spreads = {'L0_attn_g': (1.0, 0.562),
     'L0_ffn_ln_g': (1.0, 0.6),
     'L0_ffn_ln_b': (0.0, 0.8),
     'L0_ffn_b1': (0.0, 0.404),
     'L0_ffn_b2': (0.0, 0.1)}
    factors = {}
    for name, (base, spread) in spreads.items():
        noise = np.random.default_rng([zlib.crc32(name.encode()), seed]).standard_normal(out[name].shape)
        drawn = base * np.exp(spread * noise) if base else spread * noise
        out[name] = jnp.asarray(drawn.astype(out[name].dtype))
    for name, factor in factors.items():
        out[name] = (out[name] * factor).astype(out[name].dtype)
    return out
```

```python
import concourse.bass as bass
from concourse import mybir
from contextlib import ExitStack

P = 128
D = 256
B, L = 8, 512
T = B * L
NT = T // P
TB = L // P
NH, HD = 4, 64
C = 64
NC = L // C
KS = 4
E, F = 8, 1024
FC = F // P
NBLK = NT + E - 1
EPS = 1e-5
LEVELS = [2, 4, 8, 16, 32]
NL = len(LEVELS)
CORR = B
BW = D + 1

CON = {}
_at = 0
for _n, _w in (("ident", P), ("ones", P), ("head_ones", P), ("head_mean", P), ("head_eps", P),
               ("head_cols", 2), ("neg_strict", 2 * P), ("first_merge", 2 * P),
               ("merge", NL * P), ("minus_2i", P), ("tril_rows", B * CORR), ("earlier", P),
               ("rank8", E), ("thresholds", E * NT), ("block_ids", NBLK * E), ("not_first", E * NT),
               ("eps", 1)):
    CON[_n] = (_at, _w)
    _at += _w
CON_W = _at
PRM = {}
_at = 0
for _n, _w in (("taps", 6 * KS), ("ln_g", E * 2), ("ln_b", E * 2), ("b1", E * FC), ("g", 1), ("cw", 2 * (E + NH))):
    PRM[_n] = (_at, _w)
    _at += _w
PRM_W = _at


def block_kernel(nc, x, con, ids, prm, wqkv, wo, w1, w2, b2, out):
    fp32, i32 = mybir.dt.float32, mybir.dt.int32
    ALU, ACT, AX = mybir.AluOpType, mybir.ActivationFunctionType, mybir.AxisListType.X
    ctx = ExitStack()
    with ctx:
        def sb(name, shape, dt=fp32):
            return ctx.enter_context(nc.sbuf_tensor(name, shape, dt))

        def sem(name):
            return ctx.enter_context(nc.semaphore(name))

        ffn_rows = nc.dram_tensor("ffn_rows", (T, D), fp32, kind="Internal").ap()
        base_rows = nc.dram_tensor("base_rows", (T, BW), fp32, kind="Internal").ap()
        slot_token = nc.dram_tensor("slot_token", (NBLK * P, 1), i32, kind="Internal").ap()

        WE = 2 * F + FC * D
        W = sb("W", [P, E * WE])

        def w1_of(e, k, h):
            return W[:, bass.ds(e * WE + k * F + h * 512, 512)]

        def w2_of(e, c):
            return W[:, bass.ds(e * WE + 2 * F + c * D, D)]

        XNT = W[:, 6 * WE:8 * WE].rearrange("p (k t) -> p k t", k=2)
        XX = W[:, 4 * WE:6 * WE].rearrange("p (t d) -> p t d", d=D)
        QKV = W[:, 2 * WE:2 * WE + 6 * L].rearrange("p (m t) -> p m t", m=6)
        KK = W[:, 2 * WE + 6 * L:2 * WE + 12 * L].rearrange("p (t c) -> p t c", t=TB)
        KTT = W[:, 2 * WE + 12 * L:2 * WE + 16 * L].rearrange("p (c t) -> p c t", c=4)
        XN = [W[:, h * 2 * TB * D:h * 2 * TB * D + TB * D].rearrange("p (t d) -> p t d", d=D) for h in range(2)]
        XN2 = [W[:, (2 * h + 1) * TB * D:(2 * h + 2) * TB * D].rearrange("p (t d) -> p t d", d=D)
               for h in range(2)]

        CO = sb("CO", [P, CON_W])
        PR = sb("PR", [P, PRM_W])
        IDS = sb("IDS", [P, NT + NBLK], i32)
        WQKV = sb("WQKV", [P, 2, 3 * D])
        WOG = sb("WOG", [P, 2, D])

        def con_(name, lo=0, n=None):
            a, w = CON[name]
            return CO[:, a + lo:a + lo + (w if n is None else n)]

        def prm_(name, lo=0, n=None):
            a, w = PRM[name]
            return PR[:, a + lo:a + lo + (w if n is None else n)]

        ident, ones = con_("ident"), con_("ones")
        eps = con_("eps")
        CW = prm_("cw").rearrange("p (k n) -> p k n", k=2)

        ST = [sb(f"ST{h}", [P, TB, 6]) for h in range(2)]
        MV = [sb(f"MV{h}", [P, TB, 2]) for h in range(2)]
        MW = [sb(f"MW{h}", [P, TB, 2]) for h in range(2)]
        RS = [sb(f"RS{h}", [P, 4, TB]) for h in range(2)]
        AF = [sb(f"AF{h}", [E + NH, L]) for h in range(2)]
        AB = sb("AB", [P, NT, E + NH])
        MX = sb("MX", [P, NT])
        ALPHA = sb("ALPHA", [P, NT])
        BETA = sb("BETA", [P, NT, NH])
        SLOT = sb("SLOT", [P, NT], i32)
        EBLK = sb("EBLK", [P, NBLK], i32)
        IDX = sb("IDX", [P, NBLK], i32)
        RAW = [sb(f"RAW{i}", [P, KS - 1 + L]) for i in range(4)]
        SY = sb("SY", [P, 4, L])
        SQ, YS = SY[:, 0:2, :], SY[:, 2:4, :]
        RK = sb("RK", [P, TB, NH])
        CF = sb("CF", [P, TB, 2, NH])
        LL = sb("LL", [P, 2, L])
        XY = sb("XY", [P, 2, L])
        WV = sb("WV", [P, 2, L // 2])
        WU8 = sb("WU8", [P, 4, NC, CORR])
        QT = sb("QT", [P, L])
        KWU = sb("KWU", [P, 4, NC])
        KEEP = sb("KEEP", [P, 2, NC])
        SD = sb("SD", [P, 2, NC + 1])
        Y2 = sb("Y2", [P, 2, L])
        BASE = sb("BASE", [P, TB, BW])
        Q8 = [sb(f"Q8_{i}", [P, 2, NC, CORR]) for i in range(6)]
        A8 = sb("A8", [P, NC, CORR])
        PP = LL[:, :, :].rearrange("p a (c t) -> p a c t", t=P)
        TT = WV[:, :, :].rearrange("p a b -> p (a b)")
        XG = sb("XG", [P, D])
        XGT = sb("XGT", [P, 2, P])
        H = XY[:, :, :]
        HT = Y2[:, :, :].rearrange("p a (c t) -> p (a c) t", t=P)
        BG = sb("BG", [P, BW])
        YO = sb("YO", [P, D])
        B2 = SY[:, :, :].rearrange("p a b -> p (a b)").rearrange("p (e d) -> p e d", e=E)
        CUR = [sb(f"CUR{i}", [P, 1], i32) for i in range(3)]
        RT = [Y2[:, 0, 0:256], Y2[:, 0, 256:512], Y2[:, 1, 0:256], Y2[:, 1, 256:512], YS[:, 0, 0:256],
              YS[:, 0, 256:512], YS[:, 1, 0:256], YS[:, 1, 256:512]]
        RB = SQ[:, :, :].rearrange("p a b -> p (a b)")
        RSM = sb("RSM", [P, 4, E])
        SCR = sb("SCR", [P, 2, NT])

        PS = [ctx.enter_context(nc.psum_tensor(f"PS{i}", [P, 512], fp32)) for i in range(8)]

        s_ld_con = sem("ld_con")
        s_ld_ids = sem("ld_ids")
        s_ld_prm = sem("ld_prm")
        s_ld_wqkv = sem("ld_wqkv")
        s_ld_wo = sem("ld_wo")
        s_ld_b2 = sem("ld_b2")
        s_x_ready = sem("x_ready")
        s_stats1 = sem("stats1")
        s_rstd1_ln = sem("rstd1_ln")
        s_rstd1 = sem("rstd1")
        s_shift1 = sem("shift1")
        s_xn_ready = sem("xn_ready")
        s_stats2 = sem("stats2")
        s_rstd2_ln = sem("rstd2_ln")
        s_rstd2 = sem("rstd2")
        s_shift2 = sem("shift2")
        s_xn2_ready = sem("xn2_ready")
        s_xx_ready = sem("xx_ready")
        s_xn_t = sem("xn_t")
        s_xnt_ready = sem("xnt_ready")
        s_aff_t = sem("aff_t")
        s_aff_sb = sem("aff_sb")
        s_aff_back = sem("aff_back")
        s_ab_ready = sem("ab_ready")
        s_route_a = sem("route_a")
        s_alpha_exp = sem("alpha_exp")
        s_counts = sem("counts")
        s_slots_ready = sem("slots_ready")
        s_eblk_ready = sem("eblk_ready")
        s_wog_ready = sem("wog_ready")
        s_route_chain = sem("route_chain")
        s_gates_ready = sem("gates_ready")
        s_slot_filled = sem("slot_filled")
        s_slot_scattered = sem("slot_scattered")
        s_idx_loaded = sem("idx_loaded")
        s_pads_zeroed = sem("pads_zeroed")
        s_proj_done = sem("proj_done")
        s_proj_read_kv = sem("proj_read_kv")
        s_proj_read_q = sem("proj_read_q")
        s_conv_kv = sem("conv_kv")
        s_conv_q = sem("conv_q")
        s_silu_kv = sem("silu_kv")
        s_silu_q = sem("silu_q")
        s_ksq_ready = sem("ksq_ready")
        s_ssk_done = sem("ssk_done")
        s_k_ln = sem("k_ln")
        s_k_rn = sem("k_rn")
        s_coef = sem("coef")
        s_t1_done = sem("t1_done")
        s_t1_read = sem("t1_read")
        s_t2_done = sem("t2_done")
        s_t2_read = sem("t2_read")
        s_a_done = sem("a_done")
        s_ll_half = sem("ll_half")
        s_ll_ready = sem("ll_ready")
        s_xy_init = sem("xy_init")
        s_lv1_done = sem("lv1_done")
        s_lv1_read = sem("lv1_read")
        s_lv2_done = sem("lv2_done")
        s_lv2_read = sem("lv2_read")
        s_tt_ready = sem("tt_ready")
        s_wu_done = sem("wu_done")
        s_wu_read = sem("wu_read")
        s_pp_ready = sem("pp_ready")
        s_kwu_ready = sem("kwu_ready")
        s_keep_ready = sem("keep_ready")
        s_scan_ready = sem("scan_ready")
        s_sd_zero = sem("sd_zero")
        s_y_ready = sem("y_ready")
        s_q8_sq = sem("q8_sq")
        s_q8_ss = sem("q8_ss")
        s_q8_ln = sem("q8_ln")
        s_q8_r = sem("q8_r")
        s_q8_n = sem("q8_n")
        s_q8_k = sem("q8_k")
        s_q8_kr = sem("q8_kr")
        s_a8_done = sem("a8_done")
        s_a8_masked = sem("a8_masked")
        s_u8_a = sem("u8_a")
        s_u8_b = sem("u8_b")
        s_u8_c = sem("u8_c")
        s_y_fixed = sem("y_fixed")
        s_qsq_ready = sem("qsq_ready")
        s_ysq_ready = sem("ysq_ready")
        s_yn_done = sem("yn_done")
        s_yn_ln = sem("yn_ln")
        s_yn_r = sem("yn_r")
        s_o_ready = sem("o_ready")
        s_wo_done = sem("wo_done")
        s_base_ready = sem("base_ready")
        s_base_stored = sem("base_stored")
        s_attention_done = sem("attention_done")
        s_rows_in = sem("rows_in")
        s_base_in = sem("base_in")
        s_xgt_ps = sem("xgt_ps")
        s_xgt_ready = sem("xgt_ready")
        s_h_ps = sem("h_ps")
        s_h_act = sem("h_act")
        s_h_dve = sem("h_dve")
        s_ht_ps = sem("ht_ps")
        s_ht_act = sem("ht_act")
        s_ht_dve = sem("ht_dve")
        s_wait_carrier = sem("wait_carrier")
        s_y_ps = sem("y_ps")
        s_y_bias = sem("y_bias")
        s_y_ready2 = sem("y_ready2")
        s_y_out = sem("y_out")
        s_w_ready = sem("w_ready")
        s_bg_zero = sem("bg_zero")
        s_xg_zero = sem("xg_zero")
        s_idx_cur = [sem(f"idx_cur{i}") for i in range(3)]
        s_xn2_stored = [sem(f"xn2_stored{h}") for h in range(2)]
        s_x = [sem(f"ld_x{g}") for g in range(B)]
        s_w = [sem(f"ld_w{e}") for e in range(E)]

        block = ctx.enter_context(nc.Block())
        rows = "(t p) d -> p t d"

        def chunks(ap, k=NC):
            return ap.rearrange("p h (n c) -> p h n c", n=k)

        def cols(half, s, tile):
            v = XY[:, half, tile * P:(tile + 1) * P].rearrange("p (n c) -> p n c", c=2 * s)
            return v[:, :, half * s:half * s + s]

        @block.sync
        def _(sp):
            sp.dma_start(CO[:, :], con).then_inc(s_ld_con, 16)
            for g in range(B):
                sp.dma_start(XX[:, g * TB:(g + 1) * TB, :],
                             x[g * L:(g + 1) * L, :].rearrange(rows, p=P)).then_inc(s_x[g], 16)
            sp.dma_start(PR[:, :], prm).then_inc(s_ld_prm, 16)
            sp.dma_start(IDS[:, :], ids).then_inc(s_ld_ids, 16)
            sp.dma_start(WQKV[:, :, :], wqkv.rearrange("(k p) n -> p k n", p=P)).then_inc(s_ld_wqkv, 16)
            sp.dma_start(WOG[:, :, :], wo.rearrange("(k p) n -> p k n", p=P)).then_inc(s_ld_wo, 16)
            for g in range(B):
                sp.wait_ge(s_x[g], 16)
                sp.sem_inc(s_x_ready, 1)

            def store_rows(i, h):
                sp.wait_ge(s_xn2_ready, 2 * i + h + 1)
                sp.dma_start(ffn_rows[bass.ds((2 * i + h) * L, L), :].rearrange(rows, p=P),
                             XN2[h]).then_inc(s_xn2_stored[h], 16)

            with sp.Fori(0, B // 2) as i:
                for h in range(2):
                    store_rows(i, h)
            sp.wait_ge(s_ld_ids, 16)
            sp.dma_start(slot_token.rearrange("(p j) a -> p (j a)", p=P), IDS[:, NT:NT + NBLK]
                         ).then_inc(s_slot_filled, 16)

            def load_w(e):
                sp.dma_start(W[:, e * WE:e * WE + 2 * F].rearrange("p (k f) -> p k f", k=2),
                             w1[e].rearrange("(k p) f -> p k f", p=P)).then_inc(s_w[e], 16)
                sp.dma_start(W[:, e * WE + 2 * F:(e + 1) * WE].rearrange("p (c d) -> p c d", d=D),
                             w2[e].rearrange("(c p) d -> p c d", p=P)).then_inc(s_w[e], 16)

            for h in range(2):
                sp.wait_ge(s_xn2_stored[h], 16 * (B // 2))
            sp.wait_ge(s_xn_t, B)
            sp.wait_ge(s_xx_ready, B)
            load_w(0)
            load_w(1)
            sp.wait_ge(s_slot_scattered, 16 * NT)
            sp.dma_start(IDX[:, :], slot_token.rearrange("(j p) a -> p (j a)", p=P),
                         allow_slow_non_contiguous=True).then_inc(s_idx_loaded, 16)
            with sp.Fori(0, B) as b:
                sp.wait_ge(s_base_ready, 2 * b + 2)
                sp.dma_start(base_rows[bass.ds(b * L, L), :].rearrange(rows, p=P), BASE[:, :, :]
                             ).then_inc(s_base_stored, 16)
            sp.wait_ge(s_attention_done, 1)
            sp.dma_start(SY[:, :, :].rearrange("p a b -> p (a b)"), b2.partition_broadcast(P)
                         ).then_inc(s_ld_b2, 16)
            for e in range(2, E):
                load_w(e)
            for e in range(E):
                sp.wait_ge(s_w[e], 32)
                sp.sem_inc(s_w_ready, 1)
            sp.wait_ge(s_base_stored, 16 * B)
            sp.wait_ge(s_idx_loaded, 16)

        @block.gpsimd
        def _(pool):
            for i in range(4):
                last = pool.memset(RAW[i][:, 0:KS - 1], 0.0)
            last.then_inc(s_pads_zeroed, 1)
            pool.memset(SD[:, :, 0:1], 0.0).then_inc(s_sd_zero, 1)
            pool.memset(XG[:, :], 0.0).then_inc(s_xg_zero, 1)
            pool.memset(BG[:, :], 0.0).then_inc(s_bg_zero, 1)

            def residual(i, h):
                pool.wait_ge(s_xn_ready, 2 * i + h + 1)
                pool.sem_inc(s_wait_carrier, 1)
                v = XX[:, bass.ds((2 * i + h) * TB, TB), :]
                pool.tensor_tensor(v, v, XN[h], ALU.add).then_inc(s_xx_ready, 1)

            with pool.Fori(0, B // 2) as i:
                for h in range(2):
                    residual(i, h)

            def conv_q(f):
                for m in range(2):
                    pool.wait_ge(s_proj_read_q, 2 * f + m + 1)
                    pool.sem_inc(s_wait_carrier, 1)
                    if m == 0:
                        pool.wait_ge(s_y_ready, f)
                        pool.sem_inc(s_wait_carrier, 1)
                        pool.wait_ge(s_q8_k, f)
                        pool.sem_inc(s_wait_carrier, 1)
                        pool.wait_ge(s_q8_sq, f)
                        pool.sem_inc(s_wait_carrier, 1)
                        pool.wait_ge(s_qsq_ready, f)
                        pool.sem_inc(s_wait_carrier, 1)
                        pool.wait_ge(s_silu_q, f)
                        pool.sem_inc(s_wait_carrier, 1)
                    q = QKV[:, 4 + m, :]
                    for j in range(KS):
                        src = RAW[2 + m][:, j:j + L]
                        tap = prm_("taps", (4 + m) * KS + j, 1)
                        n = (2 * f + m) * 7
                        if j == 0:
                            pool.tensor_scalar(q, src, tap, 0.0, ALU.mult, ALU.add).then_inc(s_conv_q, 1)
                        else:
                            pool.wait_ge(s_conv_q, n + 2 * j - 1)
                            pool.sem_inc(s_wait_carrier, 1)
                            pool.tensor_scalar(QT[:, :], src, tap, 0.0, ALU.mult, ALU.add
                                               ).then_inc(s_conv_q, 1)
                            pool.wait_ge(s_conv_q, n + 2 * j)
                            pool.sem_inc(s_wait_carrier, 1)
                            pool.tensor_tensor(q, q, QT[:, :], ALU.add).then_inc(s_conv_q, 1)

            pool.wait_ge(s_ld_prm, 16)
            conv_q(0)
            pool.wait_ge(s_slots_ready, 1)
            pool.wait_ge(s_slot_filled, 16)
            for t in range(NT):
                pool.indirect_dma_start(out=slot_token, out_offset=bass.IndirectOffsetOnAxis(ap=SLOT[:, t:t + 1], axis=0),
                                        in_=IDS[:, t:t + 1], in_offset=None).then_inc(s_slot_scattered, 16)
            conv_q(1)
            with pool.Fori(2, B) as f:
                conv_q(f)

            def index(i, j):
                pool.tensor_copy(CUR[i][:, :], IDX[:, bass.ds(j, 1)]).then_inc(s_idx_cur[i], 1)
                pool.wait_ge(s_idx_cur[i], j + 1)
                pool.sem_inc(s_wait_carrier, 1)

            def rows_of(j):
                pool.wait_ge(s_rows_in, 16 * j)
                pool.sem_inc(s_wait_carrier, 1)
                index(0, j)
                pool.wait_ge(s_xgt_ps, j)
                pool.sem_inc(s_wait_carrier, 1)
                pool.indirect_dma_start(out=XG[:, :], out_offset=None, in_=ffn_rows,
                                        in_offset=bass.IndirectOffsetOnAxis(ap=CUR[0][:, 0:1], axis=0),
                                        bounds_check=T - 1, oob_is_err=False).then_inc(s_rows_in, 16)

            def base_of(j):
                pool.wait_ge(s_base_in, 16 * j)
                pool.sem_inc(s_wait_carrier, 1)
                index(1, j)
                pool.wait_ge(s_y_ready2, j)
                pool.sem_inc(s_wait_carrier, 1)
                pool.indirect_dma_start(out=BG[:, :], out_offset=None, in_=base_rows,
                                        in_offset=bass.IndirectOffsetOnAxis(ap=CUR[1][:, 0:1], axis=0),
                                        bounds_check=T - 1, oob_is_err=False).then_inc(s_base_in, 16)

            def put(j):
                pool.wait_ge(s_y_out, 16 * j)
                pool.sem_inc(s_wait_carrier, 1)
                index(2, j)
                pool.wait_ge(s_y_ready2, j + 1)
                pool.sem_inc(s_wait_carrier, 1)
                pool.indirect_dma_start(out=out, out_offset=bass.IndirectOffsetOnAxis(ap=CUR[2][:, 0:1], axis=0),
                                        in_=YO[:, :], in_offset=None,
                                        bounds_check=T - 1, oob_is_err=False).then_inc(s_y_out, 16)

            pool.wait_ge(s_idx_loaded, 16)
            pool.wait_ge(s_xg_zero, 1)
            pool.wait_ge(s_bg_zero, 1)
            for h in range(2):
                pool.wait_ge(s_xn2_stored[h], 16 * (B // 2))
            rows_of(0)
            rows_of(1)
            pool.wait_ge(s_base_stored, 16 * B)
            base_of(0)
            rows_of(2)
            with pool.Fori(1, NBLK - 2) as j:
                rows_of(j + 2)
                put(j - 1)
                base_of(j)
            put(NBLK - 3)
            base_of(NBLK - 2)
            put(NBLK - 2)
            base_of(NBLK - 1)
            put(NBLK - 1)
            pool.wait_ge(s_y_out, 16 * NBLK)

        @block.vector
        def _(dve):
            n_chain = [0]

            def chain(ins):
                n_chain[0] += 1
                ins.then_inc(s_route_chain, 1)
                dve.wait_ge(s_route_chain, n_chain[0])

            def norm(i):
                first = isinstance(i, int)
                for h in range(2):
                    g = 2 * i + h
                    dve.wait_ge(s_x_ready, g + 1)
                    if not first:
                        dve.wait_ge(s_rstd1_ln, g - 1)
                        dve.wait_ge(s_shift1, g - 1)
                    for t in range(TB):
                        ins = dve.bn_stats(ST[h][:, t, :], XX[:, bass.ds(g * TB + t, 1), :].rearrange("p a d -> p (a d)"))
                    ins.then_inc(s_stats1, 1)
                    dve.wait_ge(s_stats1, 2 * g + 1)
                    dve.sem_inc(s_wait_carrier, 1)
                    for t in range(TB):
                        ins = dve.bn_aggr(MV[h][:, t, :], ST[h][:, t, :])
                    ins.then_inc(s_stats1, 1)
                for h in range(2):
                    g = 2 * i + h
                    dve.wait_ge(s_rstd1, g + 1)
                    dve.wait_ge(s_stats1, 2 * g + 2)
                    dve.scalar_tensor_tensor(RS[h][:, 1, :], MV[h][:, :, 0], -1.0, RS[h][:, 0, :],
                                             ALU.mult, ALU.mult).then_inc(s_shift1, 1)
                    dve.wait_ge(s_shift1, g + 1)
                    if not first:
                        dve.wait_ge(s_xn_t, g - 1)
                        dve.wait_ge(s_xn2_ready, g - 1)
                        dve.wait_ge(s_xx_ready, g - 1)
                    for t in range(TB):
                        ins = dve.tensor_scalar(XN[h][:, t, :], XX[:, bass.ds(g * TB + t, 1), :].rearrange("p a d -> p (a d)"),
                                                RS[h][:, 0, t:t + 1], RS[h][:, 1, t:t + 1], ALU.mult, ALU.add)
                    ins.then_inc(s_xn_ready, 1)
                    dve.wait_ge(s_xn_ready, g + 1)
                    for t in range(TB):
                        ins = dve.bn_stats(ST[h][:, t, :], XN[h][:, t, :])
                    ins.then_inc(s_stats2, 1)
                    dve.wait_ge(s_stats2, 2 * g + 1)
                    dve.sem_inc(s_wait_carrier, 1)
                    for t in range(TB):
                        ins = dve.bn_aggr(MW[h][:, t, :], ST[h][:, t, :])
                    ins.then_inc(s_stats2, 1)
                for h in range(2):
                    g = 2 * i + h
                    dve.wait_ge(s_rstd2, g + 1)
                    dve.wait_ge(s_stats2, 2 * g + 2)
                    dve.scalar_tensor_tensor(RS[h][:, 3, :], MW[h][:, :, 0], -1.0, RS[h][:, 2, :],
                                             ALU.mult, ALU.mult).then_inc(s_shift2, 1)

            norm(0)
            with dve.Fori(1, B // 2) as i:
                norm(i)

            dve.wait_ge(s_ab_ready, B)
            dve.wait_ge(s_ld_con, 16)
            aff, betaz = AB[:, :, 0:E], AB[:, :, E:E + NH]
            te = [r.rearrange("p (t e) -> p t e", e=E) for r in RT]
            et = [r.rearrange("p (e t) -> p e t", e=E) for r in RT]
            dve.tensor_reduce(MX[:, :], aff, AX, ALU.max).then_inc(s_route_a, 1)
            dve.wait_ge(s_route_a, 1)
            chain(dve.tensor_tensor(te[0], aff, MX[:, :].unsqueeze(2).to_broadcast([P, NT, E]), ALU.is_ge))
            rank8 = con_("rank8").unsqueeze(1).to_broadcast([P, NT, E])
            chain(dve.tensor_tensor(te[1], te[0], rank8, ALU.mult))
            chain(dve.tensor_reduce(SCR[:, 0, :], te[1], AX, ALU.max))
            dve.tensor_tensor(te[2], rank8, SCR[:, 0, :].unsqueeze(2).to_broadcast([P, NT, E]), ALU.is_equal
                              ).then_inc(s_route_a, 1)
            dve.wait_ge(s_alpha_exp, 2)
            chain(dve.tensor_scalar(ALPHA[:, :], ALPHA[:, :], 1.0, None, ALU.add))
            dve.reciprocal(ALPHA[:, :], ALPHA[:, :]).then_inc(s_gates_ready, 1)
            chain(dve.tensor_scalar(BETA[:, :, :], BETA[:, :, :], 1.0, None, ALU.add))
            dve.reciprocal(BETA[:, :, :], BETA[:, :, :]).then_inc(s_gates_ready, 1)
            dve.wait_ge(s_ld_prm, 16)
            dve.wait_ge(s_ld_wo, 16)
            for k in range(2):
                dve.tensor_scalar(WOG[:, k, :], WOG[:, k, :], prm_("g"), None, ALU.mult).then_inc(s_wog_ready, 1)
            dve.wait_ge(s_counts, 1)
            chain(dve.tensor_copy(et[3], PS[7][:, 0:256].rearrange("p (t e) -> p e t", e=E)))
            chain(dve.tensor_tensor_scan(RT[4], con_("not_first"), RT[3], 0.0, ALU.mult, ALU.add))
            total = et[4][:, :, NT - 1:NT]
            chain(dve.tensor_tensor(et[5], total.to_broadcast([P, E, NT]),
                                    con_("thresholds").rearrange("p (e k) -> p e k", e=E), ALU.is_gt))
            chain(dve.tensor_reduce(RSM[:, 0, :], et[5], AX, ALU.add))
            chain(dve.tensor_tensor_scan(RSM[:, 1, :], ones[:, 0:E], RSM[:, 0, :], 0.0, ALU.mult, ALU.add))
            chain(dve.tensor_tensor(RSM[:, 2, :], RSM[:, 1, :], RSM[:, 0, :], ALU.subtract))
            chain(dve.tensor_scalar(RSM[:, 2, :], RSM[:, 2, :], float(P), None, ALU.mult))
            jb = RB[:, 0:NBLK * E].rearrange("p (j e) -> p j e", e=E)
            chain(dve.tensor_tensor(jb, con_("block_ids").rearrange("p (j e) -> p j e", e=E),
                                    RSM[:, 1, :].unsqueeze(1).to_broadcast([P, NBLK, E]), ALU.is_ge))
            chain(dve.tensor_reduce(RB[:, 512:512 + NBLK], jb, AX, ALU.add))
            chain(dve.tensor_scalar(EBLK[:, :], RB[:, 512:512 + NBLK], float(E - 1), None, ALU.min))
            chain(dve.tensor_tensor(et[5], et[4], et[3], ALU.subtract))
            chain(dve.tensor_tensor(et[5], et[5], RSM[:, 2, :].unsqueeze(2).to_broadcast([P, E, NT]), ALU.add))
            chain(dve.tensor_tensor(te[6], PS[6][:, 0:256].rearrange("p (t e) -> p t e", e=E),
                                    RT[5].rearrange("p (e t) -> p t e", e=E), ALU.add))
            chain(dve.tensor_tensor(te[7], te[6], te[2], ALU.mult))
            chain(dve.tensor_reduce(SCR[:, 1, :], te[7], AX, ALU.add))
            dve.tensor_copy(SLOT[:, :], SCR[:, 1, :]).then_inc(s_slots_ready, 1)

            def tap(f, m, j):
                n = (4 * f + m) * 3
                if j == 0:
                    dve.wait_ge(s_proj_read_kv, 4 * f + m + 1)
                else:
                    dve.wait_ge(s_conv_kv, n + j)
                kv = QKV[:, m, :]
                dve.scalar_tensor_tensor(kv, RAW[m % 2][:, j:j + L], prm_("taps", m * KS + j, 1), kv,
                                         ALU.mult, ALU.add).then_inc(s_conv_kv, 1)

            def back(b, more):
                f = b + 1
                first = isinstance(b, int) and b == 0
                dve.wait_ge(s_k_rn, b + 1)
                if first:
                    dve.wait_ge(s_gates_ready, 2)
                beta = BETA[:, bass.ds(b * TB, TB), :]
                dve.tensor_tensor(CF[:, :, 1, :], CF[:, :, 0, :], beta, ALU.mult).then_inc(s_coef, 1)
                dve.wait_ge(s_coef, b + 1)
                dve.wait_ge(s_wu_done, 4 * b)
                for t in range(TB):
                    dve.wait_ge(s_t1_done, 4 * b + t + 1)
                    ps = PS[2 + t % 2]
                    kk = KK[:, t, 0:2 * D].rearrange("p (a h d) -> p a h d", a=2, h=NH)
                    for a in range(2):
                        dve.tensor_tensor(kk[:, a], ps[:, 0:D].rearrange("p (h d) -> p h d", h=NH),
                                          CF[:, t, a, :].unsqueeze(2).to_broadcast([P, NH, HD]), ALU.mult)
                    dve.tensor_tensor(KK[:, t, 2 * D:3 * D].rearrange("p (h d) -> p h d", h=NH),
                                      ps[:, D:2 * D].rearrange("p (h d) -> p h d", h=NH),
                                      BETA[:, bass.ds(b * TB + t, 1), :].rearrange("p a h -> p (a h)")
                                      .unsqueeze(2).to_broadcast([P, NH, HD]), ALU.mult
                                      ).then_inc(s_t1_read, 1)
                dve.wait_ge(s_kwu_ready, 4 * b)
                for u in range(2):
                    dve.wait_ge(s_a_done, 2 * b + u + 1)
                    dve.tensor_tensor(
                        LL[:, :, u * 2 * P:(u + 1) * 2 * P].rearrange("p x (t c) -> p t x c", t=2),
                        PS[2 + u][:, :].rearrange("p (t x c) -> p t x c", t=2, x=2),
                        con_("neg_strict").rearrange("p (x c) -> p x c", x=2).unsqueeze(1)
                        .to_broadcast([P, 2, 2, P]), ALU.mult).then_inc(s_ll_half, 1)
                dve.wait_ge(s_ll_half, 2 * b + 2)
                l8 = LL[:, :, :].rearrange("p x (t c) -> p (x t) c", c=P)
                dve.tensor_tensor(l8, l8, ident.unsqueeze(1).to_broadcast([P, 8, P]), ALU.add
                                  ).then_inc(s_ll_ready, 1)
                dve.wait_ge(s_ll_ready, b + 1)
                dve.wait_ge(s_wu_done, 4 * b)
                dve.tensor_tensor(XY[:, :, :].rearrange("p x (t c) -> p x t c", c=P),
                                  LL[:, :, :].rearrange("p x (t c) -> p x t c", c=P),
                                  con_("first_merge").rearrange("p (x c) -> p x c", x=2).unsqueeze(2)
                                  .to_broadcast([P, 2, TB, P]), ALU.mult).then_inc(s_xy_init, 1)
                dve.wait_ge(s_silu_q, b + 1)
                dve.wait_ge(s_y_fixed, b)
                q8 = [chunks(QKV[:, 4:6, :])[:, h, :, 0:CORR] for h in range(2)]
                k8 = [chunks(KTT[:, 0:2, :])[:, h, :, 0:CORR] for h in range(2)]
                for h in range(2):
                    ins = dve.tensor_tensor(Q8[0][:, h], q8[h], q8[h], ALU.mult)
                ins.then_inc(s_q8_sq, 1)
                for h in range(2):
                    ins = dve.tensor_tensor(Q8[1][:, h], q8[h], k8[h], ALU.mult)
                ins.then_inc(s_q8_k, 1)
                for l, s in enumerate(LEVELS):
                    dve.wait_ge(s_lv1_done, NL * b + l + 1)
                    dve.tensor_tensor(WV[:, :, :].rearrange("p x (t c) -> p x t c", t=TB),
                                      PS[4][:, :].rearrange("p (x t c) -> p x t c", x=2, t=TB),
                                      con_("merge", l * P, P).rearrange("p (x c) -> p x c", x=2).unsqueeze(2)
                                      .to_broadcast([P, 2, TB, P // 2]), ALU.mult).then_inc(s_lv1_read, 1)
                    if l == 0:
                        dve.wait_ge(s_q8_r, b + 1)
                        dve.wait_ge(s_q8_k, b + 1)
                        dve.tensor_tensor(Q8[1][:, :, :, :], Q8[1][:, :, :, :], Q8[2][:, :, :, :], ALU.mult
                                          ).then_inc(s_q8_kr, 1)
                    if l == 1:
                        dve.wait_ge(s_a8_done, b + 1)
                        dve.tensor_tensor(A8[:, :, :], PS[6][:, 128:192].rearrange("p (n c) -> p n c", c=CORR),
                                          con_("tril_rows").rearrange("p (b c) -> p b c", b=B)
                                          [:, bass.ds(b, 1), :].to_broadcast([P, NC, CORR]), ALU.mult
                                          ).then_inc(s_a8_masked, 1)
                        dve.wait_ge(s_a8_masked, b + 1)
                        dve.wait_ge(s_q8_n, b + 1)
                        for h in range(2):
                            ins = dve.tensor_tensor(Q8[4][:, h], Q8[3][:, h], A8[:, :, :], ALU.mult)
                        ins.then_inc(s_u8_a, 1)
                    if more and l:
                        for j in range(KS - 1):
                            tap(f, l - 1, j)
                dve.wait_ge(s_lv2_read, NL * b + NL)
                dve.scalar_tensor_tensor(TT.rearrange("p (t c) -> p t c", c=P),
                                         XY[:, 1, :].rearrange("p (t c) -> p t c", c=P), 3.0,
                                         con_("minus_2i").unsqueeze(1).to_broadcast([P, TB, P]),
                                         ALU.mult, ALU.add).then_inc(s_tt_ready, 1)
                for t in range(TB):
                    dve.wait_ge(s_wu_done, 4 * b + t + 1)
                    ps = PS[6 + t % 2][:, :]
                    if t or not first:
                        dve.wait_ge(s_kwu_ready, 4 * b + t - 1)
                    pp = PP[:, t % 2]
                    for a in range(2):
                        ins = dve.tensor_tensor(pp[:, 2 * a:2 * a + 2, :],
                                                ps[:, a * D:(a + 1) * D].rearrange("p (h c) -> p h c", h=2),
                                                KTT[:, 0:2, t * P:(t + 1) * P], ALU.mult)
                    ins.then_inc(s_pp_ready, 1)
                    dve.tensor_copy(WU8[:, :, 2 * t:2 * t + 2, :],
                                    ps.rearrange("p (c n k) -> p c n k", c=4, n=2)[:, :, :, 0:CORR]
                                    ).then_inc(s_wu_read, 1)
                    dve.wait_ge(s_pp_ready, 4 * b + t + 1)
                    dve.tensor_reduce(KWU[:, :, 2 * t:2 * t + 2], pp.rearrange("p c (n k) -> p c n k", n=2),
                                      AX, ALU.add).then_inc(s_kwu_ready, 1)
                dve.wait_ge(s_kwu_ready, 4 * b + 4)
                dve.tensor_scalar(KEEP[:, :, :], KWU[:, 0:2, :], -1.0, 1.0, ALU.mult, ALU.add
                                  ).then_inc(s_keep_ready, 1)
                dve.wait_ge(s_keep_ready, b + 1)
                if first:
                    dve.wait_ge(s_sd_zero, 1)
                for h in range(2):
                    ins = dve.tensor_tensor_scan(SD[:, h, 1:NC + 1], KEEP[:, h, :], KWU[:, 2 + h, :], 0.0,
                                                 ALU.mult, ALU.add)
                ins.then_inc(s_scan_ready, 1)
                dve.wait_ge(s_scan_ready, b + 1)
                dve.wait_ge(s_wo_done, 2 * b)
                for h in range(2):
                    ins = dve.tensor_tensor(chunks(Y2[:, :, :])[:, h], chunks(QKV[:, 4:6, :])[:, h],
                                            SD[:, h, 0:NC].unsqueeze(2).to_broadcast([P, NC, C]), ALU.mult)
                ins.then_inc(s_y_ready, 1)
                sd8 = SD[:, :, 0:NC].unsqueeze(3).to_broadcast([P, 2, NC, CORR])
                dve.wait_ge(s_wu_read, 4 * b + 4)
                dve.tensor_tensor(Q8[5][:, :, :, :], WU8[:, 0:2], sd8, ALU.mult).then_inc(s_u8_b, 1)
                dve.wait_ge(s_u8_b, 3 * b + 1)
                dve.tensor_tensor(Q8[5][:, :, :, :], WU8[:, 2:4], Q8[5][:, :, :, :], ALU.subtract
                                  ).then_inc(s_u8_b, 1)
                dve.wait_ge(s_u8_b, 3 * b + 2)
                dve.wait_ge(s_u8_a, b + 1)
                dve.tensor_tensor(Q8[5][:, :, :, :], Q8[5][:, :, :, :], Q8[4][:, :, :, :], ALU.mult
                                  ).then_inc(s_u8_b, 1)
                dve.wait_ge(s_u8_b, 3 * b + 3)
                dve.wait_ge(s_y_ready, b + 1)
                y8 = chunks(Y2[:, :, :])
                for h in range(2):
                    ins = dve.tensor_tensor(y8[:, h, :, 0:CORR], y8[:, h, :, 0:CORR], Q8[5][:, h], ALU.add)
                ins.then_inc(s_y_fixed, 1)
                dve.wait_ge(s_ysq_ready, b + 1)
                for h in range(2):
                    dve.wait_ge(s_yn_r, 2 * b + h + 1)
                    dve.tensor_tensor(Y2[:, h, :], Y2[:, h, :], YS[:, h, :], ALU.mult).then_inc(s_o_ready, 1)
                dve.wait_ge(s_base_stored, 16 * b)
                if first:
                    dve.wait_ge(s_xx_ready, B)
                for u in range(2):
                    dve.wait_ge(s_wo_done, 2 * b + u + 1)
                    dve.tensor_copy(BASE[:, 2 * u:2 * u + 2, D:BW],
                                    ALPHA[:, bass.ds(b * TB + 2 * u, 2)].unsqueeze(2))
                    dve.tensor_tensor(BASE[:, 2 * u:2 * u + 2, 0:D],
                                      PS[6 + u][:, :].rearrange("p (t d) -> p t d", t=2),
                                      XX[:, bass.ds(b * TB + 2 * u, 2), :], ALU.add).then_inc(s_base_ready, 1)

            dve.wait_ge(s_pads_zeroed, 1)
            for m in range(4):
                for j in range(KS - 1):
                    tap(0, m, j)
            back(0, True)
            with dve.Fori(1, B - 1) as b:
                back(b, True)
            back(B - 1, False)
            dve.wait_ge(s_base_ready, 2 * B)
            dve.sem_inc(s_attention_done, 1)

            def expert(j):
                return dve.value_load(EBLK[0:1, bass.ds(j, 1)], min_val=0, max_val=E - 1)

            def rows_in(j, e):
                dve.wait_ge(s_xgt_ps, j + 1)
                dve.wait_ge(s_h_ps, 2 * j)
                for k in range(2):
                    ins = dve.tensor_scalar(XGT[:, k, :], PS[0][:, k * P:(k + 1) * P],
                                            PR[:, bass.ds(e * 2 + (PRM["ln_g"][0] + k), 1)],
                                            PR[:, bass.ds(e * 2 + (PRM["ln_b"][0] + k), 1)], ALU.mult, ALU.add)
                ins.then_inc(s_xgt_ready, 1)

            def hidden(j):
                dve.wait_ge(s_h_ps, 2 * j + 2)
                dve.wait_ge(s_ht_ps, 2 * j)
                dve.tensor_copy(H[:, 1, :], PS[2][:, :]).then_inc(s_h_dve, 1)

            def relu(j, e):
                dve.wait_ge(s_ht_ps, 2 * j + 2)
                dve.wait_ge(s_y_ps, j)
                for c in range(4, FC):
                    ins = dve.tensor_scalar(HT[:, c, :], PS[4][:, (c - 4) * P:(c - 3) * P],
                                            PR[:, bass.ds(e * FC + (PRM["b1"][0] + c), 1)], 0.0, ALU.add, ALU.max)
                ins.then_inc(s_ht_dve, 1)

            def finish(j, e):
                dve.wait_ge(s_y_ps, j + 1)
                dve.wait_ge(s_y_out, 16 * j)
                dve.tensor_tensor(YO[:, :], PS[5][:, 0:D], B2[:, bass.ds(e, 1), :].rearrange("p a d -> p (a d)"),
                                  ALU.add).then_inc(s_y_bias, 1)
                dve.wait_ge(s_y_bias, j + 1)
                dve.wait_ge(s_base_in, 16 * j + 16)
                dve.scalar_tensor_tensor(YO[:, :], YO[:, :], BG[:, D:BW], BG[:, 0:D], ALU.mult, ALU.add
                                         ).then_inc(s_y_ready2, 1)

            rows_in(0, expert(0))
            hidden(0)
            rows_in(1, expert(1))
            relu(0, expert(0))
            hidden(1)
            dve.wait_ge(s_ld_b2, 16)
            with dve.Fori(1, NBLK - 1) as j:
                before, this, nxt = expert(j - 1), expert(j), expert(j + 1)
                rows_in(j + 1, nxt)
                finish(j - 1, before)
                relu(j, this)
                hidden(j + 1)
            finish(NBLK - 2, expert(NBLK - 2))
            relu(NBLK - 1, expert(NBLK - 1))
            finish(NBLK - 1, expert(NBLK - 1))

        @block.scalar
        def _(act):
            log_exp = "natural_log_exp_and_others"
            act.preload_act_table_set(log_exp)
            act.wait_ge(s_ld_con, 16)

            def rsqrt(out, in_, s_ln, ln_n, s_done):
                act.activation(out, in_, ACT.Ln, bias=eps).then_inc(s_ln, 1)
                act.wait_ge(s_ln, ln_n)
                return act.activation(out, out, ACT.Exp, scale=-0.5).then_inc(s_done, 1)

            def norm(i):
                first = isinstance(i, int)
                for h in range(2):
                    g = 2 * i + h
                    act.wait_ge(s_stats1, 2 * g + 2)
                    if not first:
                        act.wait_ge(s_xn_ready, g - 1)
                    rsqrt(RS[h][:, 0, :], MV[h][:, :, 1], s_rstd1_ln, g + 1, s_rstd1)
                for h in range(2):
                    g = 2 * i + h
                    act.wait_ge(s_stats2, 2 * g + 2)
                    rsqrt(RS[h][:, 2, :], MW[h][:, :, 1], s_rstd2_ln, g + 1, s_rstd2)
                for h in range(2):
                    g = 2 * i + h
                    act.wait_ge(s_shift2, g + 1)
                    act.wait_ge(s_rstd2, g + 1)
                    if not first:
                        act.wait_ge(s_xn2_stored[h], 16 * i)
                    for t in range(TB):
                        ins = act.activation(XN2[h][:, t, :], XN[h][:, t, :], ACT.Identity,
                                             scale=RS[h][:, 2, t:t + 1], bias=RS[h][:, 3, t:t + 1])
                    ins.then_inc(s_xn2_ready, 1)
                for h in range(2):
                    g = 2 * i + h
                    act.wait_ge(s_xn_t, g + 1)
                    for k in range(2):
                        ins = act.activation(XNT[:, k, bass.ds(g * L, L)], PS[2 * h + k][:, :], ACT.Copy)
                    ins.then_inc(s_xnt_ready, 1)
                for h in range(2):
                    g = 2 * i + h
                    act.wait_ge(s_aff_t, g + 1)
                    if not first:
                        act.wait_ge(s_aff_back, g - 1)
                    act.activation(AF[h][:, :], PS[4 + h][0:E + NH, :], ACT.Copy).then_inc(s_aff_sb, 1)
                for h in range(2):
                    g = 2 * i + h
                    act.wait_ge(s_aff_back, g + 1)
                    act.activation(AB[:, bass.ds(g * TB, TB), :],
                                   PS[6 + h][:, 0:TB * (E + NH)].rearrange("p (t n) -> p t n", t=TB), ACT.Copy
                                   ).then_inc(s_ab_ready, 1)

            norm(0)
            with act.Fori(1, B // 2) as i:
                norm(i)
            act.wait_ge(s_route_a, 1)
            act.wait_ge(s_ab_ready, B)
            act.activation(ALPHA[:, :], MX[:, :], ACT.Exp, scale=-1.0).then_inc(s_alpha_exp, 1)
            act.activation(BETA[:, :, :], AB[:, :, E:E + NH], ACT.Exp, scale=-1.0).then_inc(s_alpha_exp, 1)

            def project_kv(f, m):
                n = 4 * f + m
                act.wait_ge(s_proj_done, 6 * f + m + 1)
                if not (isinstance(f, int) and f == 0 and m < 2):
                    act.wait_ge(s_conv_kv, 3 * (n - 1))
                if m == 0:
                    act.wait_ge(s_t1_done, 4 * f)
                    act.wait_ge(s_ksq_ready, f)
                act.activation(RAW[m % 2][:, KS - 1:KS - 1 + L], PS[m % 2][:, :], ACT.Copy)
                act.activation(QKV[:, m, :], PS[m % 2][:, :], ACT.Copy, scale=prm_("taps", m * KS + KS - 1, 1)
                               ).then_inc(s_proj_read_kv, 1)

            def project_q(f, m):
                act.wait_ge(s_proj_done, 6 * f + 4 + m + 1)
                if not (isinstance(f, int) and f == 0):
                    act.wait_ge(s_conv_q, 14 * (f - 1) + 7 * (m + 1))
                act.activation(RAW[2 + m][:, KS - 1:KS - 1 + L], PS[m % 2][:, :], ACT.Copy
                               ).then_inc(s_proj_read_q, 1)

            def silu_kv(f):
                act.wait_ge(s_conv_kv, 12 * f + 12)
                act.activation(QKV[:, 0:4, :], QKV[:, 0:4, :], ACT.Silu).then_inc(s_silu_kv, 1)

            def silu_q(f):
                act.wait_ge(s_conv_q, 14 * f + 14)
                act.activation(QKV[:, 4:6, :], QKV[:, 4:6, :], ACT.Silu).then_inc(s_silu_q, 1)

            def squares_k(f):
                act.wait_ge(s_silu_kv, f + 1)
                act.wait_ge(s_yn_done, 2 * f)
                act.activation(SQ[:, :, :], QKV[:, 0:2, :], ACT.Square).then_inc(s_ksq_ready, 1)

            def back(b, more):
                f = b + 1
                first = isinstance(b, int) and b == 0
                act.preload_act_table_set(log_exp)
                act.wait_ge(s_ssk_done, b + 1)
                act.wait_ge(s_k_rn, b)
                act.activation(RK[:, :, :], PS[5][:, 0:TB * NH].rearrange("p (t h) -> p t h", t=TB), ACT.Ln
                               ).then_inc(s_k_ln, 1)
                act.wait_ge(s_k_ln, b + 1)
                act.wait_ge(s_t1_read, 4 * b)
                act.activation(CF[:, :, 0, :], RK[:, :, :], ACT.Exp, scale=-0.5).then_inc(s_k_rn, 1)
                act.wait_ge(s_silu_q, b + 1)
                act.activation(SQ[:, :, :], QKV[:, 4:6, :], ACT.Square).then_inc(s_qsq_ready, 1)
                act.wait_ge(s_kwu_ready, 4 * b)
                for t in range(TB):
                    act.wait_ge(s_t2_done, 4 * b + t + 1)
                    act.activation(KTT[:, :, t * P:(t + 1) * P],
                                   PS[2 + t % 2][:, :].rearrange("p (c t) -> p c t", c=4), ACT.Copy
                                   ).then_inc(s_t2_read, 1)
                q8p = PS[6][:, 0:128].rearrange("p (h n c) -> p h n c", h=2, n=NC)
                act.wait_ge(s_q8_ss, b + 1)
                act.wait_ge(s_q8_n, b)
                act.wait_ge(s_u8_a, b)
                act.activation(Q8[0][:, :, :, :], q8p, ACT.Ln).then_inc(s_q8_ln, 1)
                act.wait_ge(s_q8_ln, b + 1)
                act.activation(Q8[2][:, :, :, :], Q8[0][:, :, :, :], ACT.Exp, scale=-0.5).then_inc(s_q8_r, 1)
                act.activation(Q8[3][:, :, :, :], Q8[0][:, :, :, :], ACT.Exp, scale=0.5).then_inc(s_q8_n, 1)
                for l, s in enumerate(LEVELS):
                    act.wait_ge(s_lv2_done, NL * b + l + 1)
                    nb = L // (2 * s)
                    if l < NL - 1:
                        out_ = bass.AP(XY, 0, [[2 * L, P], [L + s, 2], [2 * s, nb], [1, s]])
                        act.activation(out_, PS[5][:, :].rearrange("p (x n c) -> p x n c", x=2, c=s), ACT.Copy
                                       ).then_inc(s_lv2_read, 1)
                    else:
                        act.activation(XY[:, 1, :].rearrange("p (n c) -> p n c", c=2 * s)[:, :, s:2 * s],
                                       PS[5][:, L // 2:L].rearrange("p (n c) -> p n c", c=s), ACT.Copy
                                       ).then_inc(s_lv2_read, 1)
                    if more and l < 4:
                        project_kv(f, l)
                if more:
                    silu_kv(f)
                act.wait_ge(s_y_fixed, b + 1)
                act.wait_ge(s_o_ready, 2 * b)
                act.activation(YS[:, :, :], Y2[:, :, :], ACT.Square).then_inc(s_ysq_ready, 1)
                act.preload_act_table_set(log_exp)
                for h in range(2):
                    if h == 0:
                        act.wait_ge(s_yn_done, 2 * b + 2)
                    act.activation(YS[:, h, :], PS[6 + h][:, :], ACT.Ln).then_inc(s_yn_ln, 1)
                    act.wait_ge(s_yn_ln, 2 * b + h + 1)
                    act.activation(YS[:, h, :], YS[:, h, :], ACT.Exp, scale=-0.5).then_inc(s_yn_r, 1)
                if more:
                    project_q(f, 0)
                    project_q(f, 1)
                    squares_k(f)
                    silu_q(f)

            act.wait_ge(s_ld_prm, 16)
            for m in range(4):
                project_kv(0, m)
            project_q(0, 0)
            project_q(0, 1)
            silu_kv(0)
            squares_k(0)
            silu_q(0)
            back(0, True)
            with act.Fori(1, B - 1) as b:
                back(b, True)
            back(B - 1, False)

            def hidden(j):
                act.wait_ge(s_h_ps, 2 * j + 1)
                act.wait_ge(s_ht_ps, 2 * j)
                act.activation(H[:, 0, :], PS[1][:, :], ACT.Copy).then_inc(s_h_act, 1)

            def relu(j):
                e = act.value_load(EBLK[0:1, bass.ds(j, 1)], min_val=0, max_val=E - 1)
                act.wait_ge(s_ht_ps, 2 * j + 1)
                act.wait_ge(s_y_ps, j)
                for c in range(4):
                    ins = act.activation(HT[:, c, :], PS[3][:, c * P:(c + 1) * P], ACT.Relu,
                                         bias=PR[:, bass.ds(e * FC + (PRM["b1"][0] + c), 1)])
                ins.then_inc(s_ht_act, 1)

            act.wait_ge(s_attention_done, 1)
            hidden(0)
            relu(0)
            hidden(1)
            with act.Fori(1, NBLK - 1) as j:
                relu(j)
                hidden(j + 1)
            relu(NBLK - 1)

        @block.tensor
        def _(pe):
            pe.wait_ge(s_ld_con, 16)
            pe.wait_ge(s_ld_prm, 16)

            def norm(i):
                first = isinstance(i, int)
                for h in range(2):
                    g = 2 * i + h
                    pe.wait_ge(s_xn_ready, g + 1)
                    if not first:
                        pe.wait_ge(s_xnt_ready, g - 1)
                    for k in range(2):
                        for t in range(TB):
                            ins = pe.transpose(PS[2 * h + k][:, t * P:(t + 1) * P],
                                               XN[h][:, t, k * P:(k + 1) * P], ident)
                    ins.then_inc(s_xn_t, 1)
                for h in range(2):
                    g = 2 * i + h
                    pe.wait_ge(s_xnt_ready, g + 1)
                    if not first:
                        pe.wait_ge(s_aff_sb, g - 1)
                    for k in range(2):
                        ins = pe.matmul(PS[4 + h][0:E + NH, :], CW[:, k, :], XNT[:, k, bass.ds(g * L, L)],
                                        start=(k == 0), stop=(k == 1))
                    ins.then_inc(s_aff_t, 1)
                for h in range(2):
                    g = 2 * i + h
                    pe.wait_ge(s_aff_sb, g + 1)
                    pe.sem_inc(s_wait_carrier, 1)
                    if not first:
                        pe.wait_ge(s_ab_ready, g - 1)
                        pe.sem_inc(s_wait_carrier, 1)
                    for t in range(TB):
                        n = E + NH
                        ins = pe.transpose(PS[6 + h][:, t * n:(t + 1) * n], AF[h][:, t * P:(t + 1) * P],
                                           ident[0:n, 0:n])
                    ins.then_inc(s_aff_back, 1)

            norm(0)
            with pe.Fori(1, B // 2) as i:
                norm(i)

            def project(f, m, k):
                n = 6 * f + m
                if k == 0:
                    if m >= 2:
                        pe.wait_ge(s_proj_read_kv, 4 * f + m - 1)
                    elif not (isinstance(f, int) and f == 0):
                        pe.wait_ge(s_proj_read_q, 2 * f + m - 1)
                ins = pe.matmul(PS[m % 2][:, :], WQKV[:, k, m * P:(m + 1) * P], XNT[:, k, bass.ds(f * L, L)],
                                start=(k == 0), stop=(k == 1))
                if k:
                    ins.then_inc(s_proj_done, 1)

            def back(b, more):
                f = b + 1
                first = isinstance(b, int) and b == 0
                fill = [(m, k) for m in range(6) for k in range(2)] if more else []

                def filler(n=1):
                    for _ in range(n):
                        if fill:
                            project(f, *fill.pop(0))

                pe.wait_ge(s_ksq_ready, b + 1)
                pe.wait_ge(s_lv2_read, NL * b)
                for t in range(TB):
                    for h in range(2):
                        ins = pe.matmul(PS[5][:, t * NH + 2 * h:t * NH + 2 * h + 2], SQ[:, h, t * P:(t + 1) * P],
                                        con_("head_cols"), start=True, stop=True)
                ins.then_inc(s_ssk_done, 1)
                pe.wait_ge(s_silu_kv, b + 1)
                for p in range(2):
                    for t in (2 * p, 2 * p + 1):
                        if p == 0 and not first:
                            pe.wait_ge(s_ll_half, 2 * b + t - 1)
                        elif p:
                            pe.wait_ge(s_t2_read, 4 * b + t - 1)
                        for c in range(4):
                            ins = pe.transpose(PS[2 + t % 2][:, c * P:(c + 1) * P],
                                               QKV[:, c, t * P:(t + 1) * P], ident)
                        ins.then_inc(s_t1_done, 1)
                    for t in (2 * p, 2 * p + 1):
                        pe.wait_ge(s_t1_read, 4 * b + t + 1)
                        for c in range(4):
                            ins = pe.transpose(PS[2 + t % 2][:, c * P:(c + 1) * P],
                                               KK[:, t, c * P:(c + 1) * P], ident)
                        ins.then_inc(s_t2_done, 1)
                pe.wait_ge(s_t2_read, 4 * b + 4)
                for u in range(2):
                    for t in (2 * u, 2 * u + 1):
                        for x in range(2):
                            for h in range(2):
                                sl = slice(t * P, (t + 1) * P)
                                at = (t % 2) * 2 * P + x * P
                                ins = pe.matmul(PS[2 + u][:, at:at + P], KTT[:, (2 - 2 * x) + h, sl],
                                                KTT[:, 2 * x + h, sl], start=(h == 0), stop=(h == 1))
                    ins.then_inc(s_a_done, 1)
                pe.wait_ge(s_q8_sq, b + 1)
                pe.wait_ge(s_base_ready, 2 * b)
                pe.matmul(PS[6][:, 0:128], con_("head_ones"), Q8[0][:, :, :, :].rearrange("p h n c -> p (h n c)"),
                          start=True, stop=True).then_inc(s_q8_ss, 1)
                for l, s in enumerate(LEVELS):
                    if l == 0:
                        pe.wait_ge(s_xy_init, b + 1)
                    else:
                        pe.wait_ge(s_lv2_read, NL * b + l)
                    pe.wait_ge(s_lv1_read, NL * b + l)
                    nb = P // (2 * s)
                    for x in range(2):
                        for t in range(TB):
                            o = PS[4][:, (x * TB + t) * 64:(x * TB + t + 1) * 64]
                            ins = pe.matmul(o.rearrange("p (n c) -> p n c", n=nb),
                                            LL[:, 1 - x, t * P:(t + 1) * P], cols(x, s, t), start=True, stop=True)
                    ins.then_inc(s_lv1_done, 1)
                    filler()
                    if l == 0:
                        pe.wait_ge(s_q8_kr, b + 1)
                        for h in range(2):
                            ins = pe.matmul(PS[6][:, 128:192], ones, Q8[1][:, h].rearrange("p n c -> p (n c)"),
                                            start=(h == 0), stop=(h == 1))
                        ins.then_inc(s_a8_done, 1)
                    pe.wait_ge(s_lv1_read, NL * b + l + 1)
                    for x in range(2) if l < NL - 1 else (1,):
                        for t in range(TB):
                            ins = pe.matmul(PS[5][:, (x * TB + t) * 64:(x * TB + t + 1) * 64],
                                            XY[:, 1 - x, t * P:(t + 1) * P], WV[:, x, t * 64:(t + 1) * 64],
                                            start=True, stop=True)
                    ins.then_inc(s_lv2_done, 1)
                    if l < 4:
                        filler()
                pe.wait_ge(s_tt_ready, b + 1)
                for t in range(TB):
                    if t == 0:
                        pe.wait_ge(s_a8_masked, b + 1)
                    elif t > 1:
                        pe.wait_ge(s_wu_read, 4 * b + t - 1)
                    for c in range(4):
                        ins = pe.matmul(PS[6 + t % 2][:, c * P:(c + 1) * P],
                                        KK[:, t, (2 + c) * P:(3 + c) * P], TT[:, t * P:(t + 1) * P],
                                        start=True, stop=True)
                    ins.then_inc(s_wu_done, 1)
                filler(4)
                pe.wait_ge(s_ysq_ready, b + 1)
                pe.wait_ge(s_qsq_ready, b + 1)
                pe.wait_ge(s_wu_read, 4 * b + 4)
                for h in range(2):
                    pe.matmul(PS[6 + h][:, :], con_("head_eps"), SQ[:, h, :], start=True, stop=False)
                    pe.matmul(PS[6 + h][:, :], con_("head_mean"), YS[:, h, :], start=False, stop=True
                              ).then_inc(s_yn_done, 1)
                pe.wait_ge(s_o_ready, 2 * b + 2)
                for u in range(2):
                    for t in (2 * u, 2 * u + 1):
                        for h in range(2):
                            ins = pe.matmul(PS[6 + u][:, (t % 2) * D:(t % 2 + 1) * D],
                                            Y2[:, h, t * P:(t + 1) * P], WOG[:, h, :],
                                            start=(h == 0), stop=(h == 1))
                    ins.then_inc(s_wo_done, 1)

            pe.wait_ge(s_ld_wqkv, 16)
            pe.wait_ge(s_xnt_ready, B)
            for m in range(6):
                for k in range(2):
                    if m == 2 and k == 0:
                        pe.wait_ge(s_route_a, 2)
                        pe.wait_ge(s_ab_ready, B)
                        pe.matmul(PS[6][:, 0:256], con_("earlier"), RT[2], start=True, stop=True)
                        pe.matmul(PS[7][:, 0:256], ones, RT[2], start=True, stop=True).then_inc(s_counts, 1)
                    project(0, m, k)
            pe.wait_ge(s_wog_ready, 2)
            back(0, True)
            with pe.Fori(1, B - 1) as b:
                back(b, True)
            back(B - 1, False)

            def rows_t(j):
                pe.wait_ge(s_rows_in, 16 * j + 16)
                pe.wait_ge(s_xgt_ready, j)
                for k in range(2):
                    ins = pe.transpose(PS[0][:, k * P:(k + 1) * P], XG[:, k * P:(k + 1) * P], ident)
                ins.then_inc(s_xgt_ps, 1)

            def up(j):
                e = pe.value_load(EBLK[0:1, bass.ds(j, 1)], min_val=0, max_val=E - 1)
                pe.wait_ge(s_xgt_ready, j + 1)
                pe.wait_ge(s_w_ready, e + 1)
                pe.wait_ge(s_h_act, j)
                pe.wait_ge(s_h_dve, j)
                for h in range(2):
                    for k in range(2):
                        ins = pe.matmul(PS[1 + h][:, :], XGT[:, k, :], w1_of(e, k, h), start=(k == 0), stop=(k == 1))
                    ins.then_inc(s_h_ps, 1)

            def turn(j):
                for u, s_in, s_used in ((0, s_h_act, s_ht_act), (1, s_h_dve, s_ht_dve)):
                    pe.wait_ge(s_in, j + 1)
                    pe.wait_ge(s_used, j)
                    for c in range(4):
                        ins = pe.transpose(PS[3 + u][:, c * P:(c + 1) * P], H[:, u, c * P:(c + 1) * P], ident)
                    ins.then_inc(s_ht_ps, 1)

            def down(j):
                e = pe.value_load(EBLK[0:1, bass.ds(j, 1)], min_val=0, max_val=E - 1)
                pe.wait_ge(s_ht_act, j + 1)
                pe.wait_ge(s_y_bias, j)
                for c in range(FC):
                    if c == 4:
                        pe.wait_ge(s_ht_dve, j + 1)
                    ins = pe.matmul(PS[5][:, 0:D], HT[:, c, :], w2_of(e, c), start=(c == 0), stop=(c == FC - 1))
                ins.then_inc(s_y_ps, 1)

            pe.wait_ge(s_attention_done, 1)
            rows_t(0)
            up(0)
            rows_t(1)
            turn(0)
            up(1)
            with pe.Fori(1, NBLK - 1) as j:
                rows_t(j + 1)
                down(j - 1)
                turn(j)
                up(j + 1)
            down(NBLK - 2)
            turn(NBLK - 1)
            down(NBLK - 1)


def constants():
    import numpy as np
    p = np.arange(P)[:, None]
    q = np.arange(P)[None, :]
    same_head = (p // HD == q // HD).astype(np.float32)
    lower = ((p // C == q // C) & (p > q)).astype(np.float32)
    parts = {
        "ident": np.eye(P), "ones": np.ones((P, P)), "head_ones": same_head, "head_mean": same_head / HD,
        "head_eps": same_head * EPS, "head_cols": (p // HD == np.arange(2)[None, :]),
        "neg_strict": np.concatenate([-lower, -lower.T], 1),
        "minus_2i": -2.0 * np.eye(P),
        "tril_rows": np.tile((np.arange(CORR)[None, :] <= np.arange(B)[:, None]).reshape(1, -1), (P, 1)),
        "earlier": (p < q),
        "rank8": np.tile(E - np.arange(E), (P, 1)),
        "thresholds": np.tile(P * np.arange(NT), (P, E)),
        "block_ids": np.tile(np.repeat(np.arange(NBLK), E), (P, 1)),
        "not_first": np.tile((np.arange(NT) > 0), (P, E)),
        "eps": np.full((P, 1), EPS),
    }
    x1 = np.eye(P) + ((p == q + 1) & (p % 2 == 1))
    parts["first_merge"] = np.concatenate([x1, x1.T], 1)
    merge = []
    for s in LEVELS:
        n = np.arange(P // 2)[None, :]
        blk, c = n // s, n % s
        col, tcol = blk * 2 * s + c, blk * 2 * s + s + c
        merge.append((p == col) | ((p // (2 * s) == blk) & (p % (2 * s) >= s)))
        merge.append((p == tcol) | ((p // (2 * s) == blk) & (p % (2 * s) < s)))
    parts["merge"] = np.concatenate(merge, 1)
    out = np.zeros((P, CON_W), np.float32)
    for name, (at, w) in CON.items():
        out[:, at:at + w] = parts[name]
    ids = np.concatenate([P * np.arange(NT)[None, :] + p, np.full((P, NBLK), T)], 1).astype(np.int32)
    return out, ids


def kernel(L0_attn_x, L0_attn_Wq, L0_attn_Wk, L0_attn_Wv, L0_attn_Wb, L0_attn_conv_q, L0_attn_conv_k,
           L0_attn_conv_v, L0_attn_g, L0_attn_Wo, L0_ffn_centroids, L0_ffn_ln_g, L0_ffn_ln_b, L0_ffn_w1,
           L0_ffn_b1, L0_ffn_w2, L0_ffn_b2):
    import numpy as np
    import concourse.bacc as bacc
    from concourse.bass_utils import run_bass_kernel_spmd

    a = np.ascontiguousarray
    con, ids = constants()
    by_part = lambda v, n: np.asarray(v).reshape(-1, n, P).transpose(2, 0, 1).reshape(P, -1)
    taps = np.concatenate([np.asarray(w).reshape(2, P, KS).transpose(1, 0, 2).reshape(P, 2 * KS)
                           for w in (L0_attn_conv_k, L0_attn_conv_v, L0_attn_conv_q)], 1)
    cw = np.concatenate([np.asarray(L0_ffn_centroids).T, np.asarray(L0_attn_Wb)], 1)
    prm = np.concatenate([taps, by_part(L0_ffn_ln_g, 2), by_part(L0_ffn_ln_b, 2), by_part(L0_ffn_b1, FC),
                          np.tile(np.asarray(L0_attn_g), 2).reshape(P, 1),
                          cw.reshape(2, P, E + NH).transpose(1, 0, 2).reshape(P, -1)], 1)
    arrays = {
        "x": a(np.asarray(L0_attn_x).reshape(T, D)), "con": con, "ids": ids, "prm": a(prm),
        "wqkv": a(np.concatenate([L0_attn_Wk, L0_attn_Wv, L0_attn_Wq], 1)), "wo": a(L0_attn_Wo),
        "w1": a(L0_ffn_w1), "w2": a(L0_ffn_w2), "b2": a(np.asarray(L0_ffn_b2).reshape(E * D)),
    }
    nc = bacc.Bacc("TRN2", target_bir_lowering=False, num_devices=1)
    aps = {n: nc.dram_tensor(n, v.shape, mybir.dt.from_np(v.dtype), kind="ExternalInput").ap()
           for n, v in arrays.items()}
    out = nc.dram_tensor("out", (T, D), mybir.dt.float32, kind="ExternalOutput").ap()
    block_kernel(nc, **aps, out=out)
    r = run_bass_kernel_spmd(nc, [arrays], core_ids=[0])
    return r.results[0]["out"].reshape(B, L, D)
```

```python
import concourse.bass as bass
from concourse import mybir
from contextlib import ExitStack

P = 128
D = 256
B, L = 8, 512
T = B * L
NT = T // P
TB = L // P
NH, HD = 4, 64
C = 64
NC = L // C
KS = 4
E, F = 8, 1024
FC = F // P
NBLK = NT + E - 1
EPS = 1e-5
LEVELS = [2, 4, 8, 16, 32]
NL = len(LEVELS)
CORR = B
RING = 3
SETS = 7

CON = {}
_at = 0
for _n, _w in (("ident", P), ("ones", P), ("head_ones", P),
               ("head_cols", 2), ("neg_strict", 2 * P), ("first_merge", 2 * P),
               ("merge", NL * P), ("minus_2i", P), ("tril_rows", B * CORR), ("earlier", P),
               ("rank8", E), ("thresholds", E * NT), ("block_ids", NBLK * E), ("not_first", E * NT),
               ("eps", 1)):
    CON[_n] = (_at, _w)
    _at += _w
CON_W = _at
PRM = {}
_at = 0
for _n, _w in (("taps", 6 * KS), ("ln_g", E * 2), ("ln_b", E * 2), ("b1", E * FC), ("g", 1), ("cw", 2 * (E + NH))):
    PRM[_n] = (_at, _w)
    _at += _w
PRM_W = _at


def block_kernel(nc, x, con, ids, prm, wqkv, wo, w1, w2, b2, out):
    fp32, i32 = mybir.dt.float32, mybir.dt.int32
    ALU, ACT, AX = mybir.AluOpType, mybir.ActivationFunctionType, mybir.AxisListType.X
    ctx = ExitStack()
    with ctx:
        def sb(name, shape, dt=fp32):
            return ctx.enter_context(nc.sbuf_tensor(name, shape, dt))

        def sem(name):
            return ctx.enter_context(nc.semaphore(name))

        ffn_rows = nc.dram_tensor("ffn_rows", (T, D), fp32, kind="Internal").ap()
        xn_cols = nc.dram_tensor("xn_cols", (2, P, T), fp32, kind="Internal").ap()
        expert_rows = nc.dram_tensor("expert_rows", (T, D), fp32, kind="Internal").ap()
        slot_token = nc.dram_tensor("slot_token", (NBLK * P, 1), i32, kind="Internal").ap()

        WE = 2 * F + FC * D
        W = sb("W", [P, RING * WE])

        def w1_of(slot, k, h):
            return W[:, bass.ds(slot * WE + (k * F + h * 512), 512)]

        def w2_of(slot, c):
            return W[:, bass.ds(slot * WE + (2 * F + c * D), D)]

        XX = sb("XX", [P, NT, D])
        CO = sb("CO", [P, CON_W])
        PR = sb("PR", [P, PRM_W])
        IDS = sb("IDS", [P, NT + NBLK], i32)
        WQKV = sb("WQKV", [P, 2, 3 * D])
        WOG = sb("WOG", [P, 2, D])
        B2 = sb("B2", [P, E, D])

        def con_(name, lo=0, n=None):
            a, w = CON[name]
            return CO[:, a + lo:a + lo + (w if n is None else n)]

        def prm_(name, lo=0, n=None):
            a, w = PRM[name]
            return PR[:, a + lo:a + lo + (w if n is None else n)]

        ident, ones, eps = con_("ident"), con_("ones"), con_("eps")
        CW = prm_("cw").rearrange("p (k n) -> p k n", k=2)

        ST = [sb(f"ST{h}", [P, TB, 6]) for h in range(2)]
        MV = [sb(f"MV{h}", [P, TB, 2]) for h in range(2)]
        MW = [sb(f"MW{h}", [P, TB, 2]) for h in range(2)]
        RS = [sb(f"RS{h}", [P, 4, TB]) for h in range(2)]
        AF = [sb(f"AF{h}", [E + NH, L]) for h in range(2)]
        AB = sb("AB", [P, NT, E + NH])
        MX = sb("MX", [P, NT])
        ALPHA = sb("ALPHA", [P, NT])
        BETA = sb("BETA", [P, NT, NH])
        SLOT = sb("SLOT", [P, NT], i32)
        EB = sb("EB", [P, 2, NBLK], i32)
        CUMB = sb("CUMB", [P, E], i32)
        IDX = sb("IDX", [P, NBLK], i32)
        XT = sb("XT", [P, 2, L])
        QKV = sb("QKV", [P, 6, L])
        KK = sb("KK", [P, TB, 3 * D])
        KTT = sb("KTT", [P, 4, L])
        RAW = [sb(f"RAW{i}", [P, KS - 1 + L]) for i in range(2)]
        SQ = sb("SQ", [P, 2, L])
        YS = sb("YS", [P, 2, L])
        RK = sb("RK", [P, TB, NH])
        CF = sb("CF", [P, TB, 2, NH])
        LL = sb("LL", [P, 2, L])
        XY = sb("XY", [P, 2, L])
        WV = sb("WV", [P, 2, L // 2])
        WU8 = sb("WU8", [P, 4, NC, CORR])
        KWU = sb("KWU", [P, 4, NC])
        KEEP = sb("KEEP", [P, 2, NC])
        SD = sb("SD", [P, 2, NC + 1])
        Y2 = sb("Y2", [P, 2, L])
        Q8 = [sb(f"Q8_{i}", [P, 2, NC, CORR]) for i in range(6)]
        A8 = sb("A8", [P, NC, CORR])
        PP = LL[:, :, :].rearrange("p a (c t) -> p a c t", t=P)
        TT = WV[:, :, :].rearrange("p a b -> p (a b)")
        KKf = KK[:, :, :].rearrange("p t c -> p (t c)")
        XN = [KKf[:, h * TB * D:(h + 1) * TB * D].rearrange("p (t d) -> p t d", d=D) for h in range(2)]
        XN2 = [KKf[:, 2 * TB * D:3 * TB * D].rearrange("p (t d) -> p t d", d=D),
               KTT[:, 0:2, :].rearrange("p c t -> p (c t)").rearrange("p (t d) -> p t d", d=D)]
        XTA = [KTT[:, 2:4, :], LL[:, :, :]]
        XG = sb("XG", [P, D])
        XGT = sb("XGT", [P, 2, P])
        H = sb("H", [P, 2, 512])
        HT = sb("HT", [P, FC, P])
        YO = sb("YO", [P, D])
        CUR = [sb(f"CUR{i}", [P, 1], i32) for i in range(2)]
        YT = [H[:, :, :].rearrange("p a b -> p (a b)").rearrange("p (t d) -> p t d", d=D),
              HT[:, :, :].rearrange("p a b -> p (a b)").rearrange("p (t d) -> p t d", d=D)]
        RT = [v[:, a, o:o + 256] for v in (Y2, YS) for a in range(2) for o in (0, 256)]
        RB = SQ[:, :, :].rearrange("p a b -> p (a b)")
        RSM = sb("RSM", [P, 3, E])
        SCR = sb("SCR", [P, 2, NT])

        PS = [ctx.enter_context(nc.psum_tensor(f"PS{i}", [P, 512], fp32)) for i in range(8)]

        s_ld_con = sem("ld_con")
        s_ld_x = [sem(f"ld_x{i}") for i in range(B)]
        s_ld_prm = sem("ld_prm")
        s_ld_ids = sem("ld_ids")
        s_x_ready = sem("x_ready")
        s_slot_filled = sem("slot_filled")
        s_ld_wqkv = sem("ld_wqkv")
        s_ld_wo = sem("ld_wo")
        s_xn2_ready = sem("xn2_ready")
        s_wait_carrier = sem("wait_carrier")
        s_xn2_stored = [sem(f"xn2_stored{i}") for i in range(2)]
        s_xt_ready = sem("xt_ready")
        s_xt_stored = [sem(f"xt_stored{i}") for i in range(2)]
        s_ld_w = [sem(f"ld_w{i}") for i in range(E)]
        s_ld_b2 = sem("ld_b2")
        s_slot_scattered = sem("slot_scattered")
        s_idx_loaded = sem("idx_loaded")
        s_w_ready = sem("w_ready")
        s_eblk_ready = sem("eblk_ready")
        s_finished = sem("finished")
        s_y_out = sem("y_out")
        s_out_stored = [sem(f"out_stored{i}") for i in range(2)]
        s_yt_in = [sem(f"yt_in{i}") for i in range(2)]
        s_summed = sem("summed")
        s_pads_zeroed = sem("pads_zeroed")
        s_sd_zero = sem("sd_zero")
        s_xg_zero = sem("xg_zero")
        s_xn_ready = sem("xn_ready")
        s_xx_ready = sem("xx_ready")
        s_slots_ready = sem("slots_ready")
        s_rows_in = sem("rows_in")
        s_idx_cur = [sem(f"idx_cur{i}") for i in range(2)]
        s_xgt_ps = sem("xgt_ps")
        s_route_chain = sem("route_chain")
        s_shift1 = sem("shift1")
        s_stats2 = sem("stats2")
        s_stats1 = sem("stats1")
        s_rstd1 = sem("rstd1")
        s_xn_t = sem("xn_t")
        s_rstd2 = sem("rstd2")
        s_shift2 = sem("shift2")
        s_ab_ready = sem("ab_ready")
        s_route_a = sem("route_a")
        s_gate_exp = sem("gate_exp")
        s_gates_ready = sem("gates_ready")
        s_counts = sem("counts")
        s_wog_ready = sem("wog_ready")
        s_h_ps = sem("h_ps")
        s_xgt_ready = sem("xgt_ready")
        s_ht_ps = sem("ht_ps")
        s_y_ps = sem("y_ps")
        s_ht_dve = sem("ht_dve")
        s_proj_read = sem("proj_read")
        s_conv = sem("conv")
        s_silu_q = sem("silu_q")
        s_y_fixed = sem("y_fixed")
        s_q8_sq = sem("q8_sq")
        s_k_rn = sem("k_rn")
        s_coef = sem("coef")
        s_wu_done = sem("wu_done")
        s_t1_done = sem("t1_done")
        s_t1_read = sem("t1_read")
        s_kwu_ready = sem("kwu_ready")
        s_a_done = sem("a_done")
        s_ll_half = sem("ll_half")
        s_ll_ready = sem("ll_ready")
        s_xy_init = sem("xy_init")
        s_q8_k = sem("q8_k")
        s_q8_r = sem("q8_r")
        s_q8_kr = sem("q8_kr")
        s_lv1_done = sem("lv1_done")
        s_lv1_read = sem("lv1_read")
        s_a8_done = sem("a8_done")
        s_a8_masked = sem("a8_masked")
        s_q8_n = sem("q8_n")
        s_u8_a = sem("u8_a")
        s_lv2_read = sem("lv2_read")
        s_tt_ready = sem("tt_ready")
        s_pp_ready = sem("pp_ready")
        s_wu_read = sem("wu_read")
        s_keep_ready = sem("keep_ready")
        s_scan_ready = sem("scan_ready")
        s_wo_done = sem("wo_done")
        s_y_ready = sem("y_ready")
        s_u8_b = sem("u8_b")
        s_ysq_ready = sem("ysq_ready")
        s_qsq_ready = sem("qsq_ready")
        s_ys_ready = sem("ys_ready")
        s_yn_r = sem("yn_r")
        s_o_ready = sem("o_ready")
        s_base_ready = sem("base_ready")
        s_rstd1_ln = sem("rstd1_ln")
        s_rstd2_ln = sem("rstd2_ln")
        s_aff_t = sem("aff_t")
        s_aff_back = sem("aff_back")
        s_aff_sb = sem("aff_sb")
        s_h_act = sem("h_act")
        s_ht_act = sem("ht_act")
        s_proj_done = sem("proj_done")
        s_xt_in = sem("xt_in")
        s_ksq_ready = sem("ksq_ready")
        s_silu_kv = sem("silu_kv")
        s_ssk_done = sem("ssk_done")
        s_k_ln = sem("k_ln")
        s_q8_ss = sem("q8_ss")
        s_q8_ln = sem("q8_ln")
        s_t2_done = sem("t2_done")
        s_t2_read = sem("t2_read")
        s_lv2_done = sem("lv2_done")
        s_yn_done = sem("yn_done")
        s_yn_ln = sem("yn_ln")
        block = ctx.enter_context(nc.Block())
        rows = "(t p) d -> p t d"

        def chunks(ap, k=NC):
            return ap.rearrange("p h (n c) -> p h n c", n=k)

        def cols(half, s, tile):
            v = XY[:, half, tile * P:(tile + 1) * P].rearrange("p (n c) -> p n c", c=2 * s)
            return v[:, :, half * s:half * s + s]

        def is_block(j):
            return not isinstance(j, int) or 0 <= j < NBLK

        def parts_of(b):
            if isinstance(b, int):
                js = {0: [-1, 0], B - 2: range(1 + SETS * (B - 3), NBLK + 1), B - 1: []}[b]
            else:
                js = [(b - 1) * SETS + (1 + r) for r in range(SETS)]
            return iter([(j, part) for j in js for part in range(6)])

        @block.sync
        def _(sp):
            sp.dma_start(CO[:, :], con).then_inc(s_ld_con, 16)
            for g in range(B):
                sp.dma_start(XX[:, g * TB:(g + 1) * TB, :],
                             x[g * L:(g + 1) * L, :].rearrange(rows, p=P)).then_inc(s_ld_x[g], 16)
                if g == 1:
                    sp.dma_start(PR[:, :], prm).then_inc(s_ld_prm, 16)
            sp.dma_start(IDS[:, :], ids).then_inc(s_ld_ids, 16)
            for g in range(B):
                sp.wait_ge(s_ld_x[g], 16)
                sp.sem_inc(s_x_ready, 1)
            sp.wait_ge(s_ld_ids, 16)
            sp.dma_start(slot_token.rearrange("(p j) a -> p (j a)", p=P), IDS[:, NT:NT + NBLK]
                         ).then_inc(s_slot_filled, 16)
            sp.dma_start(WQKV[:, :, :], wqkv.rearrange("(k p) n -> p k n", p=P)).then_inc(s_ld_wqkv, 16)
            sp.dma_start(WOG[:, :, :], wo.rearrange("(k p) n -> p k n", p=P)).then_inc(s_ld_wo, 16)

            def store_norms(i, h):
                sp.wait_ge(s_xn2_ready, 2 * i + h + 1)
                sp.sem_inc(s_wait_carrier, 1)
                sp.dma_start(ffn_rows[bass.ds((2 * i + h) * L, L), :].rearrange(rows, p=P),
                             XN2[h]).then_inc(s_xn2_stored[h], 16)
                sp.wait_ge(s_xt_ready, 2 * i + h + 1)
                sp.sem_inc(s_wait_carrier, 1)
                for k in range(2):
                    sp.dma_start(xn_cols[k, :, bass.ds((2 * i + h) * L, L)], XTA[h][:, k, :]
                                 ).then_inc(s_xt_stored[h], 16)

            with sp.Fori(0, B // 2) as i:
                for h in range(2):
                    store_norms(i, h)

            def load_w(e):
                at = (e % RING) * WE
                sp.dma_start(W[:, at:at + 2 * F].rearrange("p (k f) -> p k f", k=2),
                             w1[e].rearrange("(k p) f -> p k f", p=P)).then_inc(s_ld_w[e], 16)
                sp.dma_start(W[:, at + 2 * F:at + WE].rearrange("p (c d) -> p c d", d=D),
                             w2[e].rearrange("(c p) d -> p c d", p=P)).then_inc(s_ld_w[e], 16)

            for e in range(RING):
                load_w(e)
            sp.dma_start(B2[:, :, :].rearrange("p e d -> p (e d)"), b2.partition_broadcast(P)
                         ).then_inc(s_ld_b2, 16)
            sp.wait_ge(s_slot_scattered, 16 * NT)
            sp.dma_start(IDX[:, :], slot_token.rearrange("(j p) a -> p (j a)", p=P),
                         allow_slow_non_contiguous=True).then_inc(s_idx_loaded, 16)
            for e in range(RING):
                sp.wait_ge(s_ld_w[e], 32)
                sp.sem_inc(s_w_ready, 1)
            sp.wait_ge(s_eblk_ready, 1)
            for e in range(RING, E):
                done = sp.value_load(CUMB[0:1, e - RING:e - RING + 1], min_val=0, max_val=NBLK)
                sp.wait_ge(s_finished, done + 1)
                sp.sem_inc(s_wait_carrier, 1)
                load_w(e)
                sp.wait_ge(s_ld_w[e], 32)
                sp.sem_inc(s_w_ready, 1)
            sp.wait_ge(s_y_out, 16 * NBLK)

            def fetch(g):
                if g >= 2:
                    sp.wait_ge(s_out_stored[g % 2], 16 * (g // 2))
                sp.dma_start(YT[g % 2], expert_rows[g * L:(g + 1) * L, :].rearrange(rows, p=P)
                             ).then_inc(s_yt_in[g % 2], 16)

            fetch(0)
            fetch(1)
            for g in range(B):
                sp.wait_ge(s_summed, g + 1)
                sp.dma_start(out[g * L:(g + 1) * L, :].rearrange(rows, p=P), YT[g % 2]
                             ).then_inc(s_out_stored[g % 2], 16)
                if g + 2 < B:
                    fetch(g + 2)
            for h in range(2):
                sp.wait_ge(s_out_stored[h], 16 * (B // 2))

        @block.gpsimd
        def _(pool):
            for i in range(2):
                last = pool.memset(RAW[i][:, 0:KS - 1], 0.0)
            last.then_inc(s_pads_zeroed, 1)
            pool.memset(SD[:, :, 0:1], 0.0).then_inc(s_sd_zero, 1)
            pool.memset(XG[:, :], 0.0).then_inc(s_xg_zero, 1)

            def residual(i, h):
                pool.wait_ge(s_xn_ready, 2 * i + h + 1)
                pool.sem_inc(s_wait_carrier, 1)
                v = XX[:, bass.ds((2 * i + h) * TB, TB), :]
                pool.tensor_tensor(v, v, XN[h], ALU.add).then_inc(s_xx_ready, 1)

            with pool.Fori(0, B // 2) as i:
                for h in range(2):
                    residual(i, h)
            pool.wait_ge(s_slots_ready, 1)
            pool.wait_ge(s_slot_filled, 16)
            for t in range(NT):
                pool.indirect_dma_start(out=slot_token,
                                        out_offset=bass.IndirectOffsetOnAxis(ap=SLOT[:, t:t + 1], axis=0),
                                        in_=IDS[:, t:t + 1], in_offset=None).then_inc(s_slot_scattered, 16)

            def rows_of(j):
                pool.wait_ge(s_rows_in, 16 * j)
                pool.sem_inc(s_wait_carrier, 1)
                pool.tensor_copy(CUR[0][:, :], IDX[:, bass.ds(j, 1)]).then_inc(s_idx_cur[0], 1)
                pool.wait_ge(s_idx_cur[0], j + 1)
                pool.sem_inc(s_wait_carrier, 1)
                pool.wait_ge(s_xgt_ps, j)
                pool.sem_inc(s_wait_carrier, 1)
                pool.indirect_dma_start(out=XG[:, :], out_offset=None, in_=ffn_rows,
                                        in_offset=bass.IndirectOffsetOnAxis(ap=CUR[0][:, 0:1], axis=0),
                                        bounds_check=T - 1, oob_is_err=False).then_inc(s_rows_in, 16)

            def put(j):
                pool.wait_ge(s_y_out, 16 * j)
                pool.sem_inc(s_wait_carrier, 1)
                pool.tensor_copy(CUR[1][:, :], IDX[:, bass.ds(j, 1)]).then_inc(s_idx_cur[1], 1)
                pool.wait_ge(s_idx_cur[1], j + 1)
                pool.sem_inc(s_wait_carrier, 1)
                pool.wait_ge(s_finished, j + 2)
                pool.sem_inc(s_wait_carrier, 1)
                pool.indirect_dma_start(out=expert_rows,
                                        out_offset=bass.IndirectOffsetOnAxis(ap=CUR[1][:, 0:1], axis=0),
                                        in_=YO[:, :], in_offset=None,
                                        bounds_check=T - 1, oob_is_err=False).then_inc(s_y_out, 16)

            pool.wait_ge(s_idx_loaded, 16)
            pool.wait_ge(s_xg_zero, 1)
            for h in range(2):
                pool.wait_ge(s_xn2_stored[h], 16 * (B // 2))
            rows_of(0)
            rows_of(1)
            rows_of(2)
            rows_of(3)
            put(0)
            with pool.Fori(2, NBLK - 2) as j:
                rows_of(j + 2)
                put(j - 1)
            for j in range(NBLK - 2, NBLK + 1):
                put(j - 1)
            pool.wait_ge(s_y_out, 16 * NBLK)

        @block.vector
        def _(dve):
            n_chain = [0]

            def chain(ins):
                n_chain[0] += 1
                ins.then_inc(s_route_chain, 1)
                dve.wait_ge(s_route_chain, n_chain[0])

            def tile_of(g, t):
                return XX[:, bass.ds(g * TB + t, 1), :].rearrange("p a d -> p (a d)")

            def statistics(i):
                for h in range(2):
                    g = 2 * i + h
                    dve.wait_ge(s_x_ready, g + 1)
                    if not isinstance(i, int):
                        dve.wait_ge(s_shift1, g - 1)
                        dve.wait_ge(s_stats2, 2 * g - 2)
                    for t in range(TB):
                        ins = dve.bn_stats(ST[h][:, t, :], tile_of(g, t))
                    ins.then_inc(s_stats1, 1)
                    dve.wait_ge(s_stats1, 2 * g + 1)
                    dve.sem_inc(s_wait_carrier, 1)
                    for t in range(TB):
                        ins = dve.bn_aggr(MV[h][:, t, :], ST[h][:, t, :])
                    ins.then_inc(s_stats1, 1)

            def normalise(i):
                for h in range(2):
                    g = 2 * i + h
                    dve.wait_ge(s_rstd1, g + 1)
                    dve.wait_ge(s_stats1, 2 * g + 2)
                    dve.scalar_tensor_tensor(RS[h][:, 1, :], MV[h][:, :, 0], -1.0, RS[h][:, 0, :],
                                             ALU.mult, ALU.mult).then_inc(s_shift1, 1)
                    dve.wait_ge(s_shift1, g + 1)
                    if not (isinstance(i, int) and i == 0):
                        dve.wait_ge(s_xn_t, g - 1)
                        dve.wait_ge(s_xn2_ready, g - 1)
                        dve.wait_ge(s_xx_ready, g - 1)
                    for t in range(TB):
                        ins = dve.tensor_scalar(XN[h][:, t, :], tile_of(g, t), RS[h][:, 0, t:t + 1],
                                                RS[h][:, 1, t:t + 1], ALU.mult, ALU.add)
                    ins.then_inc(s_xn_ready, 1)
                    dve.wait_ge(s_xn_ready, g + 1)
                    for t in range(TB):
                        ins = dve.bn_stats(ST[h][:, t, :], XN[h][:, t, :])
                    ins.then_inc(s_stats2, 1)
                    dve.wait_ge(s_stats2, 2 * g + 1)
                    dve.sem_inc(s_wait_carrier, 1)
                    for t in range(TB):
                        ins = dve.bn_aggr(MW[h][:, t, :], ST[h][:, t, :])
                    ins.then_inc(s_stats2, 1)

            def second_shift(i):
                for h in range(2):
                    g = 2 * i + h
                    dve.wait_ge(s_rstd2, g + 1)
                    dve.wait_ge(s_stats2, 2 * g + 2)
                    dve.scalar_tensor_tensor(RS[h][:, 3, :], MW[h][:, :, 0], -1.0, RS[h][:, 2, :],
                                             ALU.mult, ALU.mult).then_inc(s_shift2, 1)

            statistics(0)
            normalise(0)
            with dve.Fori(1, B // 2) as i:
                statistics(i)
                second_shift(i - 1)
                normalise(i)
            second_shift(B // 2 - 1)

            dve.wait_ge(s_ab_ready, B)
            dve.wait_ge(s_ld_con, 16)
            aff = AB[:, :, 0:E]
            te = [r.rearrange("p (t e) -> p t e", e=E) for r in RT]
            et = [r.rearrange("p (e t) -> p e t", e=E) for r in RT]
            dve.tensor_reduce(MX[:, :], aff, AX, ALU.max).then_inc(s_route_a, 1)
            dve.wait_ge(s_route_a, 1)
            chain(dve.tensor_tensor(te[0], aff, MX[:, :].unsqueeze(2).to_broadcast([P, NT, E]), ALU.is_ge))
            rank8 = con_("rank8").unsqueeze(1).to_broadcast([P, NT, E])
            chain(dve.tensor_tensor(te[1], te[0], rank8, ALU.mult))
            chain(dve.tensor_reduce(SCR[:, 0, :], te[1], AX, ALU.max))
            dve.tensor_tensor(te[2], rank8, SCR[:, 0, :].unsqueeze(2).to_broadcast([P, NT, E]), ALU.is_equal
                              ).then_inc(s_route_a, 1)
            dve.wait_ge(s_gate_exp, 2)
            chain(dve.tensor_scalar(ALPHA[:, :], ALPHA[:, :], 1.0, None, ALU.add))
            dve.reciprocal(ALPHA[:, :], ALPHA[:, :]).then_inc(s_gates_ready, 1)
            chain(dve.tensor_scalar(BETA[:, :, :], BETA[:, :, :], 1.0, None, ALU.add))
            dve.reciprocal(BETA[:, :, :], BETA[:, :, :]).then_inc(s_gates_ready, 1)
            dve.wait_ge(s_counts, 1)
            chain(dve.tensor_copy(et[3], PS[7][:, 0:256].rearrange("p (t e) -> p e t", e=E)))
            chain(dve.tensor_tensor_scan(RT[4], con_("not_first"), RT[3], 0.0, ALU.mult, ALU.add))
            total = et[4][:, :, NT - 1:NT]
            chain(dve.tensor_tensor(et[5], total.to_broadcast([P, E, NT]),
                                    con_("thresholds").rearrange("p (e k) -> p e k", e=E), ALU.is_gt))
            chain(dve.tensor_reduce(RSM[:, 0, :], et[5], AX, ALU.add))
            chain(dve.tensor_tensor_scan(RSM[:, 1, :], ones[:, 0:E], RSM[:, 0, :], 0.0, ALU.mult, ALU.add))
            chain(dve.tensor_tensor(RSM[:, 2, :], RSM[:, 1, :], RSM[:, 0, :], ALU.subtract))
            chain(dve.tensor_scalar(RSM[:, 2, :], RSM[:, 2, :], float(P), None, ALU.mult))
            chain(dve.tensor_tensor(et[5], et[4], et[3], ALU.subtract))
            chain(dve.tensor_tensor(et[5], et[5], RSM[:, 2, :].unsqueeze(2).to_broadcast([P, E, NT]), ALU.add))
            chain(dve.tensor_tensor(te[6], PS[6][:, 0:256].rearrange("p (t e) -> p t e", e=E),
                                    RT[5].rearrange("p (e t) -> p t e", e=E), ALU.add))
            chain(dve.tensor_tensor(te[7], te[6], te[2], ALU.mult))
            chain(dve.tensor_reduce(SCR[:, 1, :], te[7], AX, ALU.add))
            dve.tensor_copy(SLOT[:, :], SCR[:, 1, :]).then_inc(s_slots_ready, 1)
            jb = RB[:, 0:NBLK * E].rearrange("p (j e) -> p j e", e=E)
            eb, e3, e6 = (RB[:, 512 + i * 64:512 + i * 64 + NBLK] for i in range(3))
            dve.tensor_copy(CUMB[:, :], RSM[:, 1, :]).then_inc(s_eblk_ready, 1)
            chain(dve.tensor_tensor(jb, con_("block_ids").rearrange("p (j e) -> p j e", e=E),
                                    RSM[:, 1, :].unsqueeze(1).to_broadcast([P, NBLK, E]), ALU.is_ge))
            chain(dve.tensor_reduce(eb, jb, AX, ALU.add))
            chain(dve.tensor_scalar(eb, eb, float(E - 1), None, ALU.min))
            dve.tensor_copy(EB[:, 0, :], eb).then_inc(s_eblk_ready, 1)
            chain(dve.tensor_scalar(e3, eb, float(RING), float(-RING), ALU.is_ge, ALU.mult))
            chain(dve.tensor_scalar(e6, eb, float(2 * RING), float(-RING), ALU.is_ge, ALU.mult))
            chain(dve.tensor_tensor(e3, e3, e6, ALU.add))
            dve.tensor_tensor(EB[:, 1, :], eb, e3, ALU.add).then_inc(s_eblk_ready, 1)
            dve.wait_ge(s_ld_prm, 16)
            dve.wait_ge(s_ld_wo, 16)
            for k in range(2):
                dve.tensor_scalar(WOG[:, k, :], WOG[:, k, :], prm_("g"), None, ALU.mult).then_inc(s_wog_ready, 1)
            dve.sem_inc(s_finished, 1)

            def expert(j):
                return dve.value_load(EB[0:1, 0, bass.ds(j, 1)], min_val=0, max_val=E - 1)

            def rows_in(j):
                e = expert(j)
                dve.wait_ge(s_xgt_ps, j + 1)
                dve.wait_ge(s_h_ps, 2 * j)
                for k in range(2):
                    ins = dve.tensor_scalar(XGT[:, k, :], PS[6][:, k * P:(k + 1) * P],
                                            PR[:, bass.ds(e * 2 + (PRM["ln_g"][0] + k), 1)],
                                            PR[:, bass.ds(e * 2 + (PRM["ln_b"][0] + k), 1)], ALU.mult, ALU.add)
                ins.then_inc(s_xgt_ready, 1)

            def relu(j):
                e = expert(j)
                dve.wait_ge(s_ht_ps, 2 * j + 2)
                dve.wait_ge(s_y_ps, j)
                for c in range(4, FC):
                    ins = dve.tensor_scalar(HT[:, c, :], PS[6][:, (c - 4) * P:(c - 3) * P],
                                            PR[:, bass.ds(e * FC + (PRM["b1"][0] + c), 1)], 0.0, ALU.add, ALU.max)
                ins.then_inc(s_ht_dve, 1)

            def finish(j):
                e = expert(j)
                dve.wait_ge(s_y_ps, j + 1)
                dve.wait_ge(s_y_out, 16 * j)
                dve.tensor_tensor(YO[:, :], PS[7][:, 0:D], B2[:, bass.ds(e, 1), :].rearrange("p a d -> p (a d)"),
                                  ALU.add).then_inc(s_finished, 1)

            def part(todo):
                j, n = next(todo, (None, None))
                if n == 0 and is_block(j + 1):
                    rows_in(j + 1)
                elif n == 1 and is_block(j - 1):
                    finish(j - 1)
                elif n == 4 and is_block(j):
                    relu(j)
                return n is not None

            def tap(f, m, j):
                if j == 0:
                    dve.wait_ge(s_proj_read, 6 * f + m + 1)
                else:
                    dve.wait_ge(s_conv, (6 * f + m) * (KS - 1) + j)
                v = QKV[:, m, :]
                dve.scalar_tensor_tensor(v, RAW[m % 2][:, j:j + L], prm_("taps", m * KS + j, 1), v,
                                         ALU.mult, ALU.add).then_inc(s_conv, 1)

            def back(b, more):
                f = b + 1
                first = isinstance(b, int) and b == 0
                todo = parts_of(b)
                dve.wait_ge(s_silu_q, b + 1)
                dve.wait_ge(s_y_fixed, b)
                q8 = [chunks(QKV[:, 4:6, :])[:, h, :, 0:CORR] for h in range(2)]
                k8 = [chunks(KTT[:, 0:2, :])[:, h, :, 0:CORR] for h in range(2)]
                for h in range(2):
                    ins = dve.tensor_tensor(Q8[0][:, h], q8[h], q8[h], ALU.mult)
                ins.then_inc(s_q8_sq, 1)
                dve.wait_ge(s_k_rn, b + 1)
                if first:
                    dve.wait_ge(s_gates_ready, 2)
                beta = BETA[:, bass.ds(b * TB, TB), :]
                dve.tensor_tensor(CF[:, :, 1, :], CF[:, :, 0, :], beta, ALU.mult).then_inc(s_coef, 1)
                part(todo)
                dve.wait_ge(s_coef, b + 1)
                dve.wait_ge(s_wu_done, 4 * b)
                for p in range(2):
                    for t in (2 * p, 2 * p + 1):
                        dve.wait_ge(s_t1_done, 4 * b + t + 1)
                        ps = PS[(1, 3)[t % 2]]
                        kk = KK[:, t, 0:2 * D].rearrange("p (a h d) -> p a h d", a=2, h=NH)
                        for a in range(2):
                            dve.tensor_tensor(kk[:, a], ps[:, 0:D].rearrange("p (h d) -> p h d", h=NH),
                                              CF[:, t, a, :].unsqueeze(2).to_broadcast([P, NH, HD]), ALU.mult)
                        dve.tensor_tensor(KK[:, t, 2 * D:3 * D].rearrange("p (h d) -> p h d", h=NH),
                                          ps[:, D:2 * D].rearrange("p (h d) -> p h d", h=NH),
                                          BETA[:, bass.ds(b * TB + t, 1), :].rearrange("p a h -> p (a h)")
                                          .unsqueeze(2).to_broadcast([P, NH, HD]), ALU.mult
                                          ).then_inc(s_t1_read, 1)
                    for _ in range(4):
                        part(todo)
                dve.wait_ge(s_kwu_ready, 4 * b)
                for u in range(2):
                    dve.wait_ge(s_a_done, 2 * b + u + 1)
                    dve.tensor_tensor(
                        LL[:, :, u * 2 * P:(u + 1) * 2 * P].rearrange("p x (t c) -> p t x c", t=2),
                        PS[(1, 3)[u]][:, :].rearrange("p (t x c) -> p t x c", t=2, x=2),
                        con_("neg_strict").rearrange("p (x c) -> p x c", x=2).unsqueeze(1)
                        .to_broadcast([P, 2, 2, P]), ALU.mult).then_inc(s_ll_half, 1)
                dve.wait_ge(s_ll_half, 2 * b + 2)
                l8 = LL[:, :, :].rearrange("p x (t c) -> p (x t) c", c=P)
                dve.tensor_tensor(l8, l8, ident.unsqueeze(1).to_broadcast([P, 8, P]), ALU.add
                                  ).then_inc(s_ll_ready, 1)
                dve.wait_ge(s_ll_ready, b + 1)
                dve.tensor_tensor(XY[:, :, :].rearrange("p x (t c) -> p x t c", c=P),
                                  LL[:, :, :].rearrange("p x (t c) -> p x t c", c=P),
                                  con_("first_merge").rearrange("p (x c) -> p x c", x=2).unsqueeze(2)
                                  .to_broadcast([P, 2, TB, P]), ALU.mult).then_inc(s_xy_init, 1)
                for h in range(2):
                    ins = dve.tensor_tensor(Q8[1][:, h], q8[h], k8[h], ALU.mult)
                ins.then_inc(s_q8_k, 1)
                dve.wait_ge(s_q8_r, b + 1)
                dve.wait_ge(s_q8_k, b + 1)
                dve.tensor_tensor(Q8[1][:, :, :, :], Q8[1][:, :, :, :], Q8[2][:, :, :, :], ALU.mult
                                  ).then_inc(s_q8_kr, 1)
                for _ in range(3):
                    part(todo)
                for l, s in enumerate(LEVELS):
                    dve.wait_ge(s_lv1_done, NL * b + l + 1)
                    dve.tensor_tensor(WV[:, :, :].rearrange("p x (t c) -> p x t c", t=TB),
                                      PS[2][:, :].rearrange("p (x t c) -> p x t c", x=2, t=TB),
                                      con_("merge", l * P, P).rearrange("p (x c) -> p x c", x=2).unsqueeze(2)
                                      .to_broadcast([P, 2, TB, P // 2]), ALU.mult).then_inc(s_lv1_read, 1)
                    part(todo)
                    if l == 1:
                        dve.wait_ge(s_a8_done, b + 1)
                        dve.tensor_tensor(A8[:, :, :], PS[3][:, 0:64].rearrange("p (n c) -> p n c", c=CORR),
                                          con_("tril_rows").rearrange("p (b c) -> p b c", b=B)
                                          [:, bass.ds(b, 1), :].to_broadcast([P, NC, CORR]), ALU.mult
                                          ).then_inc(s_a8_masked, 1)
                        dve.wait_ge(s_a8_masked, b + 1)
                        dve.wait_ge(s_q8_n, b + 1)
                        for h in range(2):
                            ins = dve.tensor_tensor(Q8[4][:, h], Q8[3][:, h], A8[:, :, :], ALU.mult)
                        ins.then_inc(s_u8_a, 1)
                    if more and l:
                        for j in range(KS - 1):
                            tap(f, l - 1, j)
                    part(todo)
                dve.wait_ge(s_lv2_read, NL * b + NL)
                dve.scalar_tensor_tensor(TT.rearrange("p (t c) -> p t c", c=P),
                                         XY[:, 1, :].rearrange("p (t c) -> p t c", c=P), 3.0,
                                         con_("minus_2i").unsqueeze(1).to_broadcast([P, TB, P]),
                                         ALU.mult, ALU.add).then_inc(s_tt_ready, 1)
                part(todo)
                for t in range(TB):
                    dve.wait_ge(s_wu_done, 4 * b + t + 1)
                    ps = PS[(3, 1)[t % 2]][:, :]
                    if t or not first:
                        dve.wait_ge(s_kwu_ready, 4 * b + t - 1)
                    pp = PP[:, t % 2]
                    for a in range(2):
                        ins = dve.tensor_tensor(pp[:, 2 * a:2 * a + 2, :],
                                                ps[:, a * D:(a + 1) * D].rearrange("p (h c) -> p h c", h=2),
                                                KTT[:, 0:2, t * P:(t + 1) * P], ALU.mult)
                    ins.then_inc(s_pp_ready, 1)
                    dve.tensor_copy(WU8[:, :, 2 * t:2 * t + 2, :],
                                    ps.rearrange("p (c n k) -> p c n k", c=4, n=2)[:, :, :, 0:CORR]
                                    ).then_inc(s_wu_read, 1)
                    dve.wait_ge(s_pp_ready, 4 * b + t + 1)
                    dve.tensor_reduce(KWU[:, :, 2 * t:2 * t + 2], pp.rearrange("p c (n k) -> p c n k", n=2),
                                      AX, ALU.add).then_inc(s_kwu_ready, 1)
                    part(todo)
                dve.wait_ge(s_kwu_ready, 4 * b + 4)
                dve.tensor_scalar(KEEP[:, :, :], KWU[:, 0:2, :], -1.0, 1.0, ALU.mult, ALU.add
                                  ).then_inc(s_keep_ready, 1)
                dve.wait_ge(s_keep_ready, b + 1)
                if first:
                    dve.wait_ge(s_sd_zero, 1)
                for h in range(2):
                    ins = dve.tensor_tensor_scan(SD[:, h, 1:NC + 1], KEEP[:, h, :], KWU[:, 2 + h, :], 0.0,
                                                 ALU.mult, ALU.add)
                ins.then_inc(s_scan_ready, 1)
                dve.wait_ge(s_scan_ready, b + 1)
                dve.wait_ge(s_wo_done, 2 * b)
                for h in range(2):
                    ins = dve.tensor_tensor(chunks(Y2[:, :, :])[:, h], chunks(QKV[:, 4:6, :])[:, h],
                                            SD[:, h, 0:NC].unsqueeze(2).to_broadcast([P, NC, C]), ALU.mult)
                ins.then_inc(s_y_ready, 1)
                sd8 = SD[:, :, 0:NC].unsqueeze(3).to_broadcast([P, 2, NC, CORR])
                dve.wait_ge(s_wu_read, 4 * b + 4)
                dve.tensor_tensor(Q8[5][:, :, :, :], WU8[:, 0:2], sd8, ALU.mult).then_inc(s_u8_b, 1)
                dve.wait_ge(s_u8_b, 3 * b + 1)
                dve.tensor_tensor(Q8[5][:, :, :, :], WU8[:, 2:4], Q8[5][:, :, :, :], ALU.subtract
                                  ).then_inc(s_u8_b, 1)
                dve.wait_ge(s_u8_b, 3 * b + 2)
                dve.wait_ge(s_u8_a, b + 1)
                dve.tensor_tensor(Q8[5][:, :, :, :], Q8[5][:, :, :, :], Q8[4][:, :, :, :], ALU.mult
                                  ).then_inc(s_u8_b, 1)
                dve.wait_ge(s_u8_b, 3 * b + 3)
                dve.wait_ge(s_y_ready, b + 1)
                y8 = chunks(Y2[:, :, :])
                for h in range(2):
                    ins = dve.tensor_tensor(y8[:, h, :, 0:CORR], y8[:, h, :, 0:CORR], Q8[5][:, h], ALU.add)
                ins.then_inc(s_y_fixed, 1)
                part(todo)
                part(todo)
                dve.wait_ge(s_ysq_ready, b + 1)
                dve.wait_ge(s_qsq_ready, b + 1)
                dve.tensor_tensor(YS[:, :, :], YS[:, :, :], SQ[:, :, :], ALU.add).then_inc(s_ys_ready, 1)
                if more:
                    for j in range(KS - 1):
                        tap(f, 4, j)
                part(todo)
                part(todo)
                for h in range(2):
                    dve.wait_ge(s_yn_r, 2 * b + h + 1)
                    dve.tensor_tensor(Y2[:, h, :], Y2[:, h, :], YS[:, h, :], ALU.mult).then_inc(s_o_ready, 1)
                if more:
                    for j in range(KS - 1):
                        tap(f, 5, j)
                part(todo)
                part(todo)
                if first:
                    dve.wait_ge(s_xx_ready, B)
                for u in range(2):
                    dve.wait_ge(s_wo_done, 2 * b + u + 1)
                    v = XX[:, bass.ds(b * TB + 2 * u, 2), :]
                    dve.tensor_tensor(v, PS[(1, 3)[u]][:, :].rearrange("p (t d) -> p t d", t=2), v, ALU.add
                                      ).then_inc(s_base_ready, 1)
                while part(todo):
                    pass

            def combine(g):
                dve.wait_ge(s_yt_in[g % 2], 16 * (g // 2) + 16)
                dve.wait_ge(s_base_ready, 2 * g + 2)
                for t in range(TB):
                    n = g * TB + t
                    ins = dve.scalar_tensor_tensor(YT[g % 2][:, t, :], YT[g % 2][:, t, :], ALPHA[:, n:n + 1],
                                                   XX[:, n, :], ALU.mult, ALU.add)
                ins.then_inc(s_summed, 1)

            dve.wait_ge(s_pads_zeroed, 1)
            for m in range(6):
                for j in range(KS - 1):
                    tap(0, m, j)
            dve.wait_ge(s_eblk_ready, 3)
            dve.wait_ge(s_ld_b2, 16)
            back(0, True)
            with dve.Fori(1, B - 2) as b:
                back(b, True)
            back(B - 2, True)
            back(B - 1, False)
            for g in range(B):
                combine(g)

        @block.scalar
        def _(act):
            log_exp = "natural_log_exp_and_others"
            act.preload_act_table_set(log_exp)
            act.wait_ge(s_ld_con, 16)

            def rsqrt(out, in_, s_ln, ln_n, s_done):
                act.activation(out, in_, ACT.Ln, bias=eps).then_inc(s_ln, 1)
                act.wait_ge(s_ln, ln_n)
                act.activation(out, out, ACT.Exp, scale=-0.5).then_inc(s_done, 1)

            def first_rstd(i):
                for h in range(2):
                    g = 2 * i + h
                    act.wait_ge(s_stats1, 2 * g + 2)
                    if not (isinstance(i, int) and i == 0):
                        act.wait_ge(s_xn_ready, g - 1)
                    rsqrt(RS[h][:, 0, :], MV[h][:, :, 1], s_rstd1_ln, g + 1, s_rstd1)

            def second_rstd(i):
                for h in range(2):
                    g = 2 * i + h
                    act.wait_ge(s_stats2, 2 * g + 2)
                    rsqrt(RS[h][:, 2, :], MW[h][:, :, 1], s_rstd2_ln, g + 1, s_rstd2)

            def rest(i):
                late = not (isinstance(i, int) and i == 0)
                for h in range(2):
                    g = 2 * i + h
                    act.wait_ge(s_shift2, g + 1)
                    act.wait_ge(s_rstd2, g + 1)
                    if late:
                        act.wait_ge(s_xn2_stored[h], 16 * i)
                    for t in range(TB):
                        ins = act.activation(XN2[h][:, t, :], XN[h][:, t, :], ACT.Identity,
                                             scale=RS[h][:, 2, t:t + 1], bias=RS[h][:, 3, t:t + 1])
                    ins.then_inc(s_xn2_ready, 1)
                for h in range(2):
                    g = 2 * i + h
                    act.wait_ge(s_xn_t, g + 1)
                    if late:
                        act.wait_ge(s_aff_t, g - 1)
                        act.wait_ge(s_xt_stored[h], 32 * i)
                    for k in range(2):
                        ins = act.activation(XTA[h][:, k, :], PS[2 * h + k][:, :], ACT.Copy)
                    ins.then_inc(s_xt_ready, 1)
                for h in range(2):
                    g = 2 * i + h
                    act.wait_ge(s_aff_t, g + 1)
                    if late:
                        act.wait_ge(s_aff_back, g - 1)
                    act.activation(AF[h][:, :], PS[4 + h][0:E + NH, :], ACT.Copy).then_inc(s_aff_sb, 1)
                for h in range(2):
                    g = 2 * i + h
                    act.wait_ge(s_aff_back, g + 1)
                    act.activation(AB[:, bass.ds(g * TB, TB), :],
                                   PS[6 + h][:, 0:TB * (E + NH)].rearrange("p (t n) -> p t n", t=TB), ACT.Copy
                                   ).then_inc(s_ab_ready, 1)

            first_rstd(0)
            second_rstd(0)
            first_rstd(1)
            rest(0)
            second_rstd(1)
            with act.Fori(2, B // 2) as i:
                first_rstd(i)
                rest(i - 1)
                second_rstd(i)
            rest(B // 2 - 1)
            act.wait_ge(s_route_a, 1)
            act.wait_ge(s_ab_ready, B)
            act.activation(ALPHA[:, :], MX[:, :], ACT.Exp, scale=-1.0).then_inc(s_gate_exp, 1)
            act.activation(BETA[:, :, :], AB[:, :, E:E + NH], ACT.Exp, scale=-1.0).then_inc(s_gate_exp, 1)

            def hidden(j, h):
                act.wait_ge(s_h_ps, 2 * j + h + 1)
                if not (isinstance(j, int) and j == 0):
                    act.wait_ge(s_ht_ps, 2 * j + h - 1)
                act.activation(H[:, h, :], PS[4 + h][:, :], ACT.Copy).then_inc(s_h_act, 1)

            def relu(j):
                e = act.value_load(EB[0:1, 0, bass.ds(j, 1)], min_val=0, max_val=E - 1)
                act.wait_ge(s_ht_ps, 2 * j + 1)
                act.wait_ge(s_y_ps, j)
                for c in range(4):
                    ins = act.activation(HT[:, c, :], PS[6][:, c * P:(c + 1) * P], ACT.Relu,
                                         bias=PR[:, bass.ds(e * FC + (PRM["b1"][0] + c), 1)])
                ins.then_inc(s_ht_act, 1)

            def part(todo):
                j, n = next(todo, (None, None))
                if n == 2 and is_block(j):
                    relu(j)
                elif n == 3 and is_block(j + 1):
                    hidden(j + 1, 0)
                elif n == 5 and is_block(j + 1):
                    hidden(j + 1, 1)
                return n is not None

            def load_xt(f):
                act.wait_ge(s_proj_done, 6 * f)
                for k in range(2):
                    act.dma_start(XT[:, k, :], xn_cols[k, :, bass.ds(f * L, L)]).then_inc(s_xt_in, 16)

            def project(f, m):
                n = 6 * f + m
                act.wait_ge(s_proj_done, n + 1)
                if not (isinstance(f, int) and f == 0 and m < 2):
                    act.wait_ge(s_conv, (KS - 1) * (n - 1))
                if m == 0:
                    act.wait_ge(s_t1_done, 4 * f)
                    act.wait_ge(s_ksq_ready, f)
                if m == 4:
                    act.wait_ge(s_y_fixed, f)
                    act.wait_ge(s_qsq_ready, f)
                act.activation(RAW[m % 2][:, KS - 1:KS - 1 + L], PS[0][:, :], ACT.Copy)
                act.activation(QKV[:, m, :], PS[0][:, :], ACT.Copy, scale=prm_("taps", m * KS + KS - 1, 1)
                               ).then_inc(s_proj_read, 1)

            def silu_kv(f):
                act.wait_ge(s_conv, (KS - 1) * (6 * f + 4))
                act.activation(QKV[:, 0:4, :], QKV[:, 0:4, :], ACT.Silu).then_inc(s_silu_kv, 1)

            def silu_q(f):
                act.wait_ge(s_conv, (KS - 1) * (6 * f + 6))
                act.activation(QKV[:, 4:6, :], QKV[:, 4:6, :], ACT.Silu).then_inc(s_silu_q, 1)

            def squares_k(f):
                act.wait_ge(s_silu_kv, f + 1)
                act.wait_ge(s_ys_ready, f)
                act.activation(SQ[:, :, :], QKV[:, 0:2, :], ACT.Square).then_inc(s_ksq_ready, 1)

            def back(b, more):
                f = b + 1
                todo = parts_of(b)
                act.preload_act_table_set(log_exp)
                act.wait_ge(s_ssk_done, b + 1)
                act.wait_ge(s_k_rn, b)
                act.activation(RK[:, :, :], PS[2][:, 0:TB * NH].rearrange("p (t h) -> p t h", t=TB), ACT.Ln
                               ).then_inc(s_k_ln, 1)
                act.wait_ge(s_k_ln, b + 1)
                act.wait_ge(s_t1_read, 4 * b)
                act.activation(CF[:, :, 0, :], RK[:, :, :], ACT.Exp, scale=-0.5).then_inc(s_k_rn, 1)
                act.wait_ge(s_q8_ss, b + 1)
                act.wait_ge(s_q8_n, b)
                act.wait_ge(s_u8_a, b)
                act.activation(Q8[0][:, :, :, :], PS[3][:, 0:128].rearrange("p (h n c) -> p h n c", h=2, n=NC),
                               ACT.Ln).then_inc(s_q8_ln, 1)
                act.wait_ge(s_q8_ln, b + 1)
                act.activation(Q8[2][:, :, :, :], Q8[0][:, :, :, :], ACT.Exp, scale=-0.5).then_inc(s_q8_r, 1)
                act.activation(Q8[3][:, :, :, :], Q8[0][:, :, :, :], ACT.Exp, scale=0.5).then_inc(s_q8_n, 1)
                act.wait_ge(s_silu_q, b + 1)
                act.activation(SQ[:, :, :], QKV[:, 4:6, :], ACT.Square, scale=EPS ** 0.5).then_inc(s_qsq_ready, 1)
                part(todo)
                act.wait_ge(s_kwu_ready, 4 * b)
                for p in range(2):
                    part(todo)
                    part(todo)
                    for t in (2 * p, 2 * p + 1):
                        act.wait_ge(s_t2_done, 4 * b + t + 1)
                        act.activation(KTT[:, :, t * P:(t + 1) * P],
                                       PS[(1, 3)[t % 2]][:, :].rearrange("p (c t) -> p c t", c=4), ACT.Copy
                                       ).then_inc(s_t2_read, 1)
                    part(todo)
                    part(todo)
                for _ in range(3):
                    part(todo)
                for l, s in enumerate(LEVELS):
                    part(todo)
                    act.wait_ge(s_lv2_done, NL * b + l + 1)
                    nb = L // (2 * s)
                    if l < NL - 1:
                        out_ = bass.AP(XY, 0, [[2 * L, P], [L + s, 2], [2 * s, nb], [1, s]])
                        act.activation(out_, PS[2][:, :].rearrange("p (x n c) -> p x n c", x=2, c=s), ACT.Copy
                                       ).then_inc(s_lv2_read, 1)
                    else:
                        act.activation(XY[:, 1, :].rearrange("p (n c) -> p n c", c=2 * s)[:, :, s:2 * s],
                                       PS[2][:, L // 2:L].rearrange("p (n c) -> p n c", c=s), ACT.Copy
                                       ).then_inc(s_lv2_read, 1)
                    if more and l < 4:
                        project(f, l)
                    part(todo)
                part(todo)
                part(todo)
                if more:
                    silu_kv(f)
                for _ in range(TB - 1):
                    part(todo)
                act.wait_ge(s_y_fixed, b + 1)
                act.wait_ge(s_o_ready, 2 * b)
                act.activation(YS[:, :, :], Y2[:, :, :], ACT.Square, scale=HD ** -0.5).then_inc(s_ysq_ready, 1)
                if more:
                    project(f, 4)
                part(todo)
                part(todo)
                act.preload_act_table_set(log_exp)
                for h in range(2):
                    act.wait_ge(s_yn_done, 2 * b + h + 1)
                    act.activation(YS[:, h, :], PS[2 + h][:, :], ACT.Ln).then_inc(s_yn_ln, 1)
                    act.wait_ge(s_yn_ln, 2 * b + h + 1)
                    act.activation(YS[:, h, :], YS[:, h, :], ACT.Exp, scale=-0.5).then_inc(s_yn_r, 1)
                if more:
                    project(f, 5)
                    if not (isinstance(b, int) and b == B - 2):
                        load_xt(f + 1)
                part(todo)
                part(todo)
                if more:
                    squares_k(f)
                part(todo)
                part(todo)
                while part(todo):
                    pass
                if more:
                    silu_q(f)

            act.wait_ge(s_ld_prm, 16)
            for h in range(2):
                act.wait_ge(s_xt_stored[h], 32 * (B // 2))
            load_xt(0)
            for m in range(6):
                project(0, m)
            load_xt(1)
            silu_kv(0)
            squares_k(0)
            silu_q(0)
            act.wait_ge(s_eblk_ready, 3)
            back(0, True)
            with act.Fori(1, B - 2) as b:
                back(b, True)
            back(B - 2, True)
            back(B - 1, False)

        @block.tensor
        def _(pe):
            pe.wait_ge(s_ld_con, 16)
            pe.wait_ge(s_ld_prm, 16)

            def norm(i):
                late = not (isinstance(i, int) and i == 0)
                for h in range(2):
                    g = 2 * i + h
                    pe.wait_ge(s_xn_ready, g + 1)
                    if late:
                        pe.wait_ge(s_xt_ready, g - 1)
                    for k in range(2):
                        for t in range(TB):
                            ins = pe.transpose(PS[2 * h + k][:, t * P:(t + 1) * P],
                                               XN[h][:, t, k * P:(k + 1) * P], ident)
                    ins.then_inc(s_xn_t, 1)
                for h in range(2):
                    g = 2 * i + h
                    pe.wait_ge(s_xt_ready, g + 1)
                    if late:
                        pe.wait_ge(s_aff_sb, g - 1)
                    for k in range(2):
                        ins = pe.matmul(PS[4 + h][0:E + NH, :], CW[:, k, :], XTA[h][:, k, :],
                                        start=(k == 0), stop=(k == 1))
                    ins.then_inc(s_aff_t, 1)
                for h in range(2):
                    g = 2 * i + h
                    n = E + NH
                    pe.wait_ge(s_aff_sb, g + 1)
                    if late:
                        pe.wait_ge(s_ab_ready, g - 1)
                    pe.sem_inc(s_wait_carrier, 1)
                    for t in range(TB):
                        ins = pe.transpose(PS[6 + h][:, t * n:(t + 1) * n], AF[h][:, t * P:(t + 1) * P],
                                           ident[0:n, 0:n])
                    ins.then_inc(s_aff_back, 1)

            norm(0)
            with pe.Fori(1, B // 2) as i:
                norm(i)

            def rows_t(j):
                pe.wait_ge(s_rows_in, 16 * j + 16)
                if not (isinstance(j, int) and j == 0):
                    pe.wait_ge(s_ht_dve, j - 1)
                for k in range(2):
                    ins = pe.transpose(PS[6][:, k * P:(k + 1) * P], XG[:, k * P:(k + 1) * P], ident)
                ins.then_inc(s_xgt_ps, 1)

            def slot_of(j):
                return pe.value_load(EB[0:1, 1, bass.ds(j, 1)], min_val=0, max_val=RING - 1)

            def up(j, h):
                slot = slot_of(j)
                if h == 0:
                    e = pe.value_load(EB[0:1, 0, bass.ds(j, 1)], min_val=0, max_val=E - 1)
                    pe.wait_ge(s_w_ready, e + 1)
                    pe.wait_ge(s_xgt_ready, j + 1)
                if not (isinstance(j, int) and j == 0):
                    pe.wait_ge(s_h_act, 2 * j + h - 1)
                for k in range(2):
                    ins = pe.matmul(PS[4 + h][:, :], XGT[:, k, :], w1_of(slot, k, h), start=(k == 0), stop=(k == 1))
                ins.then_inc(s_h_ps, 1)

            def turn(j, u):
                pe.wait_ge(s_h_act, 2 * j + u + 1)
                if u == 0:
                    pe.wait_ge(s_xgt_ready, j + 2 if is_block(j + 1) else j + 1)
                else:
                    pe.wait_ge(s_ht_act, j + 1)
                for c in range(4):
                    ins = pe.transpose(PS[6][:, c * P:(c + 1) * P], H[:, u, c * P:(c + 1) * P], ident)
                ins.then_inc(s_ht_ps, 1)

            def down(j, u):
                slot = slot_of(j)
                if u == 0:
                    pe.wait_ge(s_ht_act, j + 1)
                    pe.wait_ge(s_finished, j + 1)
                else:
                    pe.wait_ge(s_ht_dve, j + 1)
                for c in range(4 * u, 4 * u + 4):
                    ins = pe.matmul(PS[7][:, 0:D], HT[:, c, :], w2_of(slot, c), start=(c == 0), stop=(c == FC - 1))
                if u:
                    ins.then_inc(s_y_ps, 1)

            def part(todo):
                j, n = next(todo, (None, None))
                if n == 0:
                    if is_block(j + 1):
                        rows_t(j + 1)
                    if is_block(j - 1):
                        down(j - 1, 0)
                elif n == 1 and is_block(j - 1):
                    down(j - 1, 1)
                elif n in (2, 4) and is_block(j):
                    turn(j, (n - 2) // 2)
                elif n in (3, 5) and is_block(j + 1):
                    up(j + 1, (n - 3) // 2)
                return n is not None

            def project(f, m, k):
                if k == 0:
                    pe.wait_ge(s_proj_read, 6 * f + m)
                    if m == 0:
                        pe.wait_ge(s_xt_in, 32 * f + 32)
                ins = pe.matmul(PS[0][:, :], WQKV[:, k, m * P:(m + 1) * P], XT[:, k, :],
                                start=(k == 0), stop=(k == 1))
                if k:
                    ins.then_inc(s_proj_done, 1)

            def back(b, more):
                f = b + 1
                first = isinstance(b, int) and b == 0
                todo = parts_of(b)
                pe.wait_ge(s_ksq_ready, b + 1)
                pe.wait_ge(s_lv2_read, NL * b)
                pe.wait_ge(s_yn_ln, 2 * b)
                for t in range(TB):
                    for h in range(2):
                        ins = pe.matmul(PS[2][:, t * NH + 2 * h:t * NH + 2 * h + 2], SQ[:, h, t * P:(t + 1) * P],
                                        con_("head_cols"), start=True, stop=True)
                ins.then_inc(s_ssk_done, 1)
                pe.wait_ge(s_q8_sq, b + 1)
                pe.wait_ge(s_base_ready, 2 * b)
                pe.matmul(PS[3][:, 0:128], con_("head_ones"), Q8[0][:, :, :, :].rearrange("p h n c -> p (h n c)"),
                          start=True, stop=True).then_inc(s_q8_ss, 1)
                part(todo)
                pe.wait_ge(s_silu_kv, b + 1)
                pe.wait_ge(s_q8_ln, b + 1)
                for p in range(2):
                    for t in (2 * p, 2 * p + 1):
                        if p:
                            pe.wait_ge(s_t2_read, 4 * b + t - 1)
                        for c in range(4):
                            ins = pe.transpose(PS[(1, 3)[t % 2]][:, c * P:(c + 1) * P],
                                               QKV[:, c, t * P:(t + 1) * P], ident)
                        ins.then_inc(s_t1_done, 1)
                    part(todo)
                    part(todo)
                    for t in (2 * p, 2 * p + 1):
                        pe.wait_ge(s_t1_read, 4 * b + t + 1)
                        for c in range(4):
                            ins = pe.transpose(PS[(1, 3)[t % 2]][:, c * P:(c + 1) * P],
                                               KK[:, t, c * P:(c + 1) * P], ident)
                        ins.then_inc(s_t2_done, 1)
                    part(todo)
                    part(todo)
                pe.wait_ge(s_t2_read, 4 * b + 4)
                for u in range(2):
                    for t in (2 * u, 2 * u + 1):
                        for x in range(2):
                            for h in range(2):
                                sl = slice(t * P, (t + 1) * P)
                                at = (t % 2) * 2 * P + x * P
                                ins = pe.matmul(PS[(1, 3)[u]][:, at:at + P], KTT[:, (2 - 2 * x) + h, sl],
                                                KTT[:, 2 * x + h, sl], start=(h == 0), stop=(h == 1))
                    ins.then_inc(s_a_done, 1)
                for _ in range(3):
                    part(todo)
                for l, s in enumerate(LEVELS):
                    if l == 0:
                        pe.wait_ge(s_xy_init, b + 1)
                        pe.wait_ge(s_k_ln, b + 1)
                    else:
                        pe.wait_ge(s_lv2_read, NL * b + l)
                    nb = P // (2 * s)
                    for x in range(2):
                        for t in range(TB):
                            o = PS[2][:, (x * TB + t) * 64:(x * TB + t + 1) * 64]
                            ins = pe.matmul(o.rearrange("p (n c) -> p n c", n=nb),
                                            LL[:, 1 - x, t * P:(t + 1) * P], cols(x, s, t), start=True, stop=True)
                    ins.then_inc(s_lv1_done, 1)
                    if l == 0:
                        pe.wait_ge(s_q8_kr, b + 1)
                        for h in range(2):
                            ins = pe.matmul(PS[3][:, 0:64], ones, Q8[1][:, h].rearrange("p n c -> p (n c)"),
                                            start=(h == 0), stop=(h == 1))
                        ins.then_inc(s_a8_done, 1)
                    if more and l < 4:
                        project(f, l, 0)
                    part(todo)
                    pe.wait_ge(s_lv1_read, NL * b + l + 1)
                    for x in range(2) if l < NL - 1 else (1,):
                        for t in range(TB):
                            ins = pe.matmul(PS[2][:, (x * TB + t) * 64:(x * TB + t + 1) * 64],
                                            XY[:, 1 - x, t * P:(t + 1) * P], WV[:, x, t * 64:(t + 1) * 64],
                                            start=True, stop=True)
                    ins.then_inc(s_lv2_done, 1)
                    if more and l < 4:
                        project(f, l, 1)
                    part(todo)
                part(todo)
                pe.wait_ge(s_tt_ready, b + 1)
                for t in range(TB):
                    if t == 0:
                        pe.wait_ge(s_a8_masked, b + 1)
                    elif t > 1:
                        pe.wait_ge(s_wu_read, 4 * b + t - 1)
                    for c in range(4):
                        ins = pe.matmul(PS[(3, 1)[t % 2]][:, c * P:(c + 1) * P],
                                        KK[:, t, (2 + c) * P:(3 + c) * P], TT[:, t * P:(t + 1) * P],
                                        start=True, stop=True)
                    ins.then_inc(s_wu_done, 1)
                    part(todo)
                if more:
                    project(f, 4, 0)
                    project(f, 4, 1)
                part(todo)
                part(todo)
                pe.wait_ge(s_ys_ready, b + 1)
                pe.wait_ge(s_wu_read, 4 * b + 4)
                for h in range(2):
                    pe.matmul(PS[2 + h][:, :], con_("head_ones"), YS[:, h, :], start=True, stop=True
                              ).then_inc(s_yn_done, 1)
                if more:
                    project(f, 5, 0)
                    project(f, 5, 1)
                part(todo)
                part(todo)
                pe.wait_ge(s_o_ready, 2 * b + 2)
                for u in range(2):
                    for t in (2 * u, 2 * u + 1):
                        for h in range(2):
                            ins = pe.matmul(PS[(1, 3)[u]][:, (t % 2) * D:(t % 2 + 1) * D],
                                            Y2[:, h, t * P:(t + 1) * P], WOG[:, h, :],
                                            start=(h == 0), stop=(h == 1))
                    ins.then_inc(s_wo_done, 1)
                part(todo)
                part(todo)
                while part(todo):
                    pass

            pe.wait_ge(s_route_a, 2)
            pe.wait_ge(s_ab_ready, B)
            pe.matmul(PS[6][:, 0:256], con_("earlier"), RT[2], start=True, stop=True)
            pe.matmul(PS[7][:, 0:256], ones, RT[2], start=True, stop=True).then_inc(s_counts, 1)
            pe.wait_ge(s_ld_wqkv, 16)
            for m in range(6):
                for k in range(2):
                    project(0, m, k)
            pe.wait_ge(s_wog_ready, 2)
            pe.wait_ge(s_eblk_ready, 3)
            back(0, True)
            with pe.Fori(1, B - 2) as b:
                back(b, True)
            back(B - 2, True)
            back(B - 1, False)


def constants():
    import numpy as np
    p = np.arange(P)[:, None]
    q = np.arange(P)[None, :]
    same_head = (p // HD == q // HD).astype(np.float32)
    lower = ((p // C == q // C) & (p > q)).astype(np.float32)
    parts = {
        "ident": np.eye(P), "ones": np.ones((P, P)), "head_ones": same_head,
        "head_cols": (p // HD == np.arange(2)[None, :]),
        "neg_strict": np.concatenate([-lower, -lower.T], 1),
        "minus_2i": -2.0 * np.eye(P),
        "tril_rows": np.tile((np.arange(CORR)[None, :] <= np.arange(B)[:, None]).reshape(1, -1), (P, 1)),
        "earlier": (p < q),
        "rank8": np.tile(E - np.arange(E), (P, 1)),
        "thresholds": np.tile(P * np.arange(NT), (P, E)),
        "block_ids": np.tile(np.repeat(np.arange(NBLK), E), (P, 1)),
        "not_first": np.tile((np.arange(NT) > 0), (P, E)),
        "eps": np.full((P, 1), EPS),
    }
    x1 = np.eye(P) + ((p == q + 1) & (p % 2 == 1))
    parts["first_merge"] = np.concatenate([x1, x1.T], 1)
    merge = []
    for s in LEVELS:
        n = np.arange(P // 2)[None, :]
        blk, c = n // s, n % s
        col, tcol = blk * 2 * s + c, blk * 2 * s + s + c
        merge.append((p == col) | ((p // (2 * s) == blk) & (p % (2 * s) >= s)))
        merge.append((p == tcol) | ((p // (2 * s) == blk) & (p % (2 * s) < s)))
    parts["merge"] = np.concatenate(merge, 1)
    out = np.zeros((P, CON_W), np.float32)
    for name, (at, w) in CON.items():
        out[:, at:at + w] = parts[name]
    ids = np.concatenate([P * np.arange(NT)[None, :] + p, np.full((P, NBLK), T)], 1).astype(np.int32)
    return out, ids


def kernel(L0_attn_x, L0_attn_Wq, L0_attn_Wk, L0_attn_Wv, L0_attn_Wb, L0_attn_conv_q, L0_attn_conv_k,
           L0_attn_conv_v, L0_attn_g, L0_attn_Wo, L0_ffn_centroids, L0_ffn_ln_g, L0_ffn_ln_b, L0_ffn_w1,
           L0_ffn_b1, L0_ffn_w2, L0_ffn_b2):
    import numpy as np
    import concourse.bacc as bacc
    from concourse.bass_utils import run_bass_kernel_spmd

    a = np.ascontiguousarray
    con, ids = constants()
    by_part = lambda v, n: np.asarray(v).reshape(-1, n, P).transpose(2, 0, 1).reshape(P, -1)
    taps = np.concatenate([np.asarray(w).reshape(2, P, KS).transpose(1, 0, 2).reshape(P, 2 * KS)
                           for w in (L0_attn_conv_k, L0_attn_conv_v, L0_attn_conv_q)], 1)
    cw = np.concatenate([np.asarray(L0_ffn_centroids).T, np.asarray(L0_attn_Wb)], 1)
    prm = np.concatenate([taps, by_part(L0_ffn_ln_g, 2), by_part(L0_ffn_ln_b, 2), by_part(L0_ffn_b1, FC),
                          np.tile(np.asarray(L0_attn_g), 2).reshape(P, 1),
                          cw.reshape(2, P, E + NH).transpose(1, 0, 2).reshape(P, -1)], 1)
    arrays = {
        "x": a(np.asarray(L0_attn_x).reshape(T, D)), "con": con, "ids": ids, "prm": a(prm),
        "wqkv": a(np.concatenate([L0_attn_Wk, L0_attn_Wv, L0_attn_Wq], 1)), "wo": a(L0_attn_Wo),
        "w1": a(L0_ffn_w1), "w2": a(L0_ffn_w2), "b2": a(np.asarray(L0_ffn_b2).reshape(E * D)),
    }
    nc = bacc.Bacc("TRN2", target_bir_lowering=False, num_devices=1)
    aps = {n: nc.dram_tensor(n, v.shape, mybir.dt.from_np(v.dtype), kind="ExternalInput").ap()
           for n, v in arrays.items()}
    out = nc.dram_tensor("out", (T, D), mybir.dt.float32, kind="ExternalOutput").ap()
    block_kernel(nc, **aps, out=out)
    r = run_bass_kernel_spmd(nc, [arrays], core_ids=[0])
    return r.results[0]["out"].reshape(B, L, D)
```

```python
import concourse.bass as bass
from concourse import mybir
from contextlib import ExitStack

P = 128
D = 256
B, L = 8, 512
T = B * L
NT = T // P
TB = L // P
NH, HD = 4, 64
C = 64
NC = L // C
KS = 4
E, F = 8, 1024
FC = F // P
NBLK = NT + E - 1
EPS = 1e-5
LEVELS = [2, 4, 8, 16, 32]
NL = len(LEVELS)
CORR = B
RING = 2
SLOTS = 33
FIRST_PARTS = (0, 0, 0, 0, 0, 0, 0, 0, 0, 0, 0, 0, 0, 0, 0, 0, 0, 0, 0, 1, 1, 1, 1, 3, 2, 0, 3, 3, 1, 2, 0, 0, 0)
LOOP_PARTS = (2, 2, 0, 0, 2, 0, 1, 0, 1, 3, 0, 1, 0, 1, 0, 2, 0, 1, 0, 2, 0, 0, 1, 2, 2, 0, 2, 1, 2, 0, 2, 0, 0)
LATE_PARTS = (2, 1, 2, 1, 0, 1, 0, 0, 1, 0, 3, 1, 0, 1, 0, 1, 1, 1, 0, 2, 0, 0, 1, 1, 1, 2, 2, 0, 3, 2, 0, 0, 0)
LAST_PARTS = (3, 1, 1, 2, 4, 0, 6, 2, 0, 2, 2, 1, 3, 2, 1, 2, 2, 2, 4, 3, 1, 0, 0, 0, 0, 0, 0, 0, 0, 0, 0, 0, 0)
SUMS = (0, 0, 0, 0, 0, 0, 0, 0, 0, 2, 1, 1)
SETS = sum(LOOP_PARTS) // 6
assert sum(FIRST_PARTS) + (B - 3) * sum(LOOP_PARTS) + sum(LATE_PARTS) + sum(LAST_PARTS) == 6 * (NBLK + 1) + 2

CON = {}
_at = 0
for _n, _w in (("ident", P), ("ones", P), ("head_ones", P),
               ("head_cols", 2), ("neg_upper", P), ("first_merge", P),
               ("merge", NL * P), ("minus_2i", P), ("tril_rows", B * CORR), ("earlier", P),
               ("rank8", E), ("thresholds", E * NT), ("block_ids", NBLK * E), ("not_first", E * NT)):
    CON[_n] = (_at, _w)
    _at += _w
CON_W = _at
PRM = {}
_at = 0
for _n, _w in (("taps", 6 * KS), ("ln_g", E * 2), ("ln_b", E * 2), ("b1", E * FC), ("g", 1), ("cw", 2 * (E + NH))):
    PRM[_n] = (_at, _w)
    _at += _w
PRM_W = _at


def block_kernel(nc, x, con, ids, prm, wqkv, wo, w1, w2, b2, out):
    fp32, fp32r, i32 = mybir.dt.float32, mybir.dt.float32r, mybir.dt.int32
    ALU, ACT, AX = mybir.AluOpType, mybir.ActivationFunctionType, mybir.AxisListType.X
    ctx = ExitStack()
    with ctx:
        def sb(name, shape, dt=fp32):
            return ctx.enter_context(nc.sbuf_tensor(name, shape, dt))

        def sem(name):
            return ctx.enter_context(nc.semaphore(name))

        ffn_rows = nc.dram_tensor("ffn_rows", (T, D), fp32, kind="Internal").ap()
        xn_cols = nc.dram_tensor("xn_cols", (2, P, T), fp32, kind="Internal").ap()
        expert_rows = nc.dram_tensor("expert_rows", (T, D), fp32, kind="Internal").ap()
        slot_token = nc.dram_tensor("slot_token", (NBLK * P, 1), i32, kind="Internal").ap()

        WE = 2 * F + FC * D
        W = sb("W", [P, RING * WE])

        def w1_of(slot, k, h):
            return W[:, bass.ds(slot * WE + (k * F + h * 512), 512)]

        def w2_of(slot, c):
            return W[:, bass.ds(slot * WE + (2 * F + c * D), D)]

        XX = sb("XX", [P, NT, D])
        CO = sb("CO", [P, CON_W])
        PR = sb("PR", [P, PRM_W])
        IDS = sb("IDS", [P, NT + NBLK], i32)
        WQ_HI, WQ_LO = (sb(f"WQ_{n}", [P, 2, 3 * D], fp32r) for n in ("HI", "LO"))
        XT_HI, XT_LO = (sb(f"XT_{n}", [P, 2, L], fp32r) for n in ("HI", "LO"))
        WQKV = W[:, 0:6 * D].rearrange("p (k n) -> p k n", k=2)
        WOG = sb("WOG", [P, 2, D])
        B2 = sb("B2", [P, E, D])

        def con_(name, lo=0, n=None):
            a, w = CON[name]
            return CO[:, a + lo:a + lo + (w if n is None else n)]

        def prm_(name, lo=0, n=None):
            a, w = PRM[name]
            return PR[:, a + lo:a + lo + (w if n is None else n)]

        ident, ones = con_("ident"), con_("ones")
        EPSC = sb("EPSC", [P, 2])
        eps, eps_sq = EPSC[:, 0:1], EPSC[:, 1:2]

        def conv_of(m):
            return QKV[:, m, :] if m < 4 else QC[:, m - 4, :]

        CW = prm_("cw").rearrange("p (k n) -> p k n", k=2)

        ST = [sb(f"ST{h}", [P, TB, 6]) for h in range(2)]
        MV = [sb(f"MV{g}", [P, TB, 2]) for g in range(B)]
        RS = [sb(f"RS{g}", [P, 4, TB]) for g in range(B)]
        AB = sb("AB", [P, NT, E + NH])
        MX = sb("MX", [P, NT])
        ALPHA = sb("ALPHA", [P, NT])
        BETA = sb("BETA", [P, NT, NH])
        SLOT = sb("SLOT", [P, NT], i32)
        EB = sb("EB", [P, 2, NBLK], i32)
        CUMB = sb("CUMB", [P, E], i32)
        IDX = sb("IDX", [P, NBLK], i32)
        XT = sb("XT", [P, 2, L])
        QKV = sb("QKV", [P, 6, L])
        KK = sb("KK", [P, TB, 3 * D])
        KTT = sb("KTT", [P, 4, L])
        RAW = [sb(f"RAW{i}", [P, KS - 1 + L]) for i in range(2)]
        SQ = sb("SQ", [P, 2, L])
        YS = sb("YS", [P, 2, L])
        RK = sb("RK", [P, TB, NH])
        CF = sb("CF", [P, TB, 2, NH])
        LT = sb("LT", [P, L])
        QC = sb("QC", [P, 2, L])
        XY = sb("XY", [P, 2, L])
        WV = sb("WV", [P, L])
        WU8 = sb("WU8", [P, 4, NC, CORR])
        KWU = sb("KWU", [P, 4, NC])
        KEEP = sb("KEEP", [P, 2, NC])
        SD = sb("SD", [P, 2, NC + 1])
        Y2 = sb("Y2", [P, 2, L])
        Q8 = [sb(f"Q8_{i}", [P, 2, NC, CORR]) for i in range(6)]
        A8 = sb("A8", [P, NC, CORR])
        PP = XY[:, :, :].rearrange("p a (c t) -> p a c t", t=P)
        KKf = KK[:, :, :].rearrange("p t c -> p (t c)")
        XN = [KKf[:, h * TB * D:(h + 1) * TB * D].rearrange("p (t d) -> p t d", d=D) for h in range(2)]
        XN2 = [KKf[:, 2 * TB * D:3 * TB * D].rearrange("p (t d) -> p t d", d=D),
               KTT[:, 0:2, :].rearrange("p c t -> p (c t)").rearrange("p (t d) -> p t d", d=D)]
        XTA = [KTT[:, 2:4, :], XY[:, :, :]]

        def columns_of(g):
            return XTA[g % 2] if g else XT[:, :, :]

        XG = sb("XG", [P, D])
        XGT = sb("XGT", [P, 2, P])
        H = sb("H", [P, 2, 512])
        HT = sb("HT", [P, FC, P])
        YO = sb("YO", [P, D])
        CUR = [sb(f"CUR{i}", [P, 1], i32) for i in range(2)]
        YT = [W[:, g * TB * D:(g + 1) * TB * D].rearrange("p (t d) -> p t d", d=D) for g in range(B)]
        RT = [v[:, a, o:o + 256] for v in (Y2, YS) for a in range(2) for o in (0, 256)]
        RB = XY[:, :, :].rearrange("p a b -> p (a b)")
        RSM = sb("RSM", [P, 3, E])
        SCR = sb("SCR", [P, 2, NT])

        PS = [ctx.enter_context(nc.psum_tensor(f"PS{i}", [P, 512], fp32)) for i in range(8)]

        s_ld_x = [sem(f"ld_x{i}") for i in range(B)]
        s_ld_ident = sem("ld_ident")
        s_ld_prm = sem("ld_prm")
        s_ld_wqkv = sem("ld_wqkv")
        s_ld_con = sem("ld_con")
        s_ld_ids = sem("ld_ids")
        s_xn2_ready = sem("xn2_ready")
        s_xn2_stored = [sem(f"xn2_stored{i}") for i in range(2)]
        s_xt_ready = sem("xt_ready")
        s_xt_stored = [sem(f"xt_stored{i}") for i in range(2)]
        s_slot_filled = sem("slot_filled")
        s_ld_wo = sem("ld_wo")
        s_ld_w = [sem(f"ld_w{i}") for i in range(E)]
        s_wq_lo = sem("wq_lo")
        s_ld_b2 = sem("ld_b2")
        s_slot_scattered = sem("slot_scattered")
        s_idx_loaded = sem("idx_loaded")
        s_w_ready = sem("w_ready")
        s_eblk_ready = sem("eblk_ready")
        s_finished = sem("finished")
        s_wait_carrier = sem("wait_carrier")
        s_y_out = sem("y_out")
        s_yt_in = [sem(f"yt_in{i}") for i in range(B)]
        s_summed = sem("summed")
        s_out_stored = [sem(f"out_stored{i}") for i in range(B)]
        s_base_ready = sem("base_ready")
        s_eps_set = sem("eps_set")
        s_pads_zeroed = sem("pads_zeroed")
        s_sd_zero = sem("sd_zero")
        s_xg_zero = sem("xg_zero")
        s_shift = sem("shift")
        s_rstd = sem("rstd")
        s_xn_ready = sem("xn_ready")
        s_xx_ready = sem("xx_ready")
        s_slots_ready = sem("slots_ready")
        s_rows_in = sem("rows_in")
        s_idx_cur = [sem(f"idx_cur{i}") for i in range(2)]
        s_xgt_ps = sem("xgt_ps")
        s_gates_ready = sem("gates_ready")
        s_gated = sem("gated")
        s_route_chain = sem("route_chain")
        s_proj_read = sem("proj_read")
        s_conv = sem("conv")
        s_silu_q = sem("silu_q")
        s_q8_n = sem("q8_n")
        s_q8_sq = sem("q8_sq")
        s_stats = sem("stats")
        s_xn_t = sem("xn_t")
        s_xt_hi = sem("xt_hi")
        s_xt_lo = sem("xt_lo")
        s_wq_hi = sem("wq_hi")
        s_ab_ready = sem("ab_ready")
        s_route_a = sem("route_a")
        s_counts = sem("counts")
        s_gate_exp = sem("gate_exp")
        s_wog_ready = sem("wog_ready")
        s_summed_dve = sem("summed_dve")
        s_h_ps = sem("h_ps")
        s_xgt_ready = sem("xgt_ready")
        s_ht_ps = sem("ht_ps")
        s_y_ps = sem("y_ps")
        s_ht_dve = sem("ht_dve")
        s_k_rn = sem("k_rn")
        s_coef = sem("coef")
        s_wu_done = sem("wu_done")
        s_t1_done = sem("t1_done")
        s_t1_read = sem("t1_read")
        s_kwu_ready = sem("kwu_ready")
        s_a_done = sem("a_done")
        s_a_masked = sem("a_masked")
        s_lt_ready = sem("lt_ready")
        s_xt_init = sem("xt_init")
        s_q8_k = sem("q8_k")
        s_q8_r = sem("q8_r")
        s_q8_kr = sem("q8_kr")
        s_lv1_done = sem("lv1_done")
        s_lv1_read = sem("lv1_read")
        s_a8_done = sem("a8_done")
        s_a8_masked = sem("a8_masked")
        s_u8_a = sem("u8_a")
        s_lv2_read = sem("lv2_read")
        s_tt_ready = sem("tt_ready")
        s_pp_ready = sem("pp_ready")
        s_wu_read = sem("wu_read")
        s_keep_ready = sem("keep_ready")
        s_scan_ready = sem("scan_ready")
        s_wo_done = sem("wo_done")
        s_y_ready = sem("y_ready")
        s_u8_b = sem("u8_b")
        s_y_fixed = sem("y_fixed")
        s_ysq_ready = sem("ysq_ready")
        s_qsq_ready = sem("qsq_ready")
        s_ys_ready = sem("ys_ready")
        s_yn_r = sem("yn_r")
        s_o_ready = sem("o_ready")
        s_xt_in = sem("xt_in")
        s_proj_done = sem("proj_done")
        s_ksq_ready = sem("ksq_ready")
        s_silu_kv = sem("silu_kv")
        s_rstd_ln = sem("rstd_ln")
        s_aff_done = sem("aff_done")
        s_h_act = sem("h_act")
        s_ht_act = sem("ht_act")
        s_head_ss = sem("head_ss")
        s_k_ln = sem("k_ln")
        s_q8_ln = sem("q8_ln")
        s_t2_done = sem("t2_done")
        s_t2_read = sem("t2_read")
        s_x_init = sem("x_init")
        s_xy_ready = sem("xy_ready")
        s_lv2_done = sem("lv2_done")
        s_yn_done = sem("yn_done")
        s_yn_ln = sem("yn_ln")
        block = ctx.enter_context(nc.Block())
        rows = "(t p) d -> p t d"

        def chunks(ap, k=NC):
            return ap.rearrange("p h (n c) -> p h n c", n=k)

        def cols(v, half, s):
            return v.rearrange("p (n c) -> p n c", c=2 * s)[:, :, half * s:half * s + s]

        POOL_SUMS = list(range(B - 1 - sum(SUMS)))
        POOL_SUMS.insert(len(POOL_SUMS) - 1, B - 1)

        def is_block(j):
            return not isinstance(j, int) or 0 <= j < NBLK

        def parts_of(b):
            last = isinstance(b, int) and b == B - 1
            counts, start = LOOP_PARTS, 0
            if isinstance(b, int):
                counts = {0: FIRST_PARTS, B - 2: LATE_PARTS, B - 1: LAST_PARTS}[b]
                start = -6 if b == 0 else 6 * NBLK + 2 - sum(LAST_PARTS) - (0 if last else sum(LATE_PARTS))
            places, n = [], 0
            for at, count in enumerate(counts):
                here = []
                for m in range(n, n + count):
                    if isinstance(b, int):
                        here.append(((start + m) // 6, m % 6))
                    else:
                        here.append((SETS * b + (sum(FIRST_PARTS) // 6 - 1 - SETS + m // 6), m % 6))
                n += count
                if last and at >= SLOTS - len(SUMS):
                    done = B - 1 - sum(SUMS[at - SLOTS + len(SUMS):])
                    here += [(done + g, 6) for g in range(SUMS[at - SLOTS + len(SUMS)])]
                places.append(here)
            return iter(places)

        @block.sync
        def _(sp):
            for g in range(B):
                sp.dma_start(XX[:, g * TB:(g + 1) * TB, :],
                             x[g * L:(g + 1) * L, :].rearrange(rows, p=P)).then_inc(s_ld_x[g], 16)
                if g == 0:
                    sp.dma_start(CO[:, 0:P], con[:, 0:P]).then_inc(s_ld_ident, 16)
                if g == 1:
                    sp.dma_start(PR[:, :], prm).then_inc(s_ld_prm, 16)
                    sp.dma_start(WQKV, wqkv.rearrange("(k p) n -> p k n", p=P)).then_inc(s_ld_wqkv, 16)
            sp.dma_start(CO[:, P:CON_W], con[:, P:CON_W]).then_inc(s_ld_con, 16)
            sp.dma_start(IDS[:, :], ids).then_inc(s_ld_ids, 16)
            for g in range(B):
                h = g % 2
                sp.wait_ge(s_xn2_ready, g + 1)
                sp.dma_start(ffn_rows[g * L:(g + 1) * L, :].rearrange(rows, p=P), XN2[h]
                             ).then_inc(s_xn2_stored[h], 16)
                if g:
                    sp.wait_ge(s_xt_ready, g + 1)
                    for k in range(2):
                        sp.dma_start(xn_cols[k, :, g * L:(g + 1) * L], XTA[h][:, k, :]
                                     ).then_inc(s_xt_stored[h], 16)
            sp.wait_ge(s_ld_ids, 16)
            sp.dma_start(slot_token.rearrange("(p j) a -> p (j a)", p=P), IDS[:, NT:NT + NBLK]
                         ).then_inc(s_slot_filled, 16)
            sp.dma_start(WOG[:, :, :], wo.rearrange("(k p) n -> p k n", p=P)).then_inc(s_ld_wo, 16)

            def load_w(e):
                at = (e % RING) * WE
                sp.dma_start(W[:, at:at + 2 * F].rearrange("p (k f) -> p k f", k=2),
                             w1[e].rearrange("(k p) f -> p k f", p=P)).then_inc(s_ld_w[e], 16)
                sp.dma_start(W[:, at + 2 * F:at + WE].rearrange("p (c d) -> p c d", d=D),
                             w2[e].rearrange("(c p) d -> p c d", p=P)).then_inc(s_ld_w[e], 16)

            sp.wait_ge(s_wq_lo, 1)
            for e in range(RING):
                load_w(e)
            sp.dma_start(B2[:, :, :].rearrange("p e d -> p (e d)"), b2.partition_broadcast(P)
                         ).then_inc(s_ld_b2, 16)
            sp.wait_ge(s_slot_scattered, 16 * NT)
            sp.dma_start(IDX[:, :], slot_token.rearrange("(j p) a -> p (j a)", p=P),
                         allow_slow_non_contiguous=True).then_inc(s_idx_loaded, 16)
            for e in range(RING):
                sp.wait_ge(s_ld_w[e], 32)
                sp.sem_inc(s_w_ready, 1)
            sp.wait_ge(s_eblk_ready, 1)
            for e in range(RING, E):
                done = sp.value_load(CUMB[0:1, e - RING:e - RING + 1], min_val=0, max_val=NBLK)
                sp.wait_ge(s_finished, done + 1)
                sp.sem_inc(s_wait_carrier, 1)
                load_w(e)
                sp.wait_ge(s_ld_w[e], 32)
                sp.sem_inc(s_w_ready, 1)
            sp.wait_ge(s_y_out, 16 * NBLK)
            for g in range(B):
                sp.dma_start(YT[g], expert_rows[g * L:(g + 1) * L, :].rearrange(rows, p=P)).then_inc(s_yt_in[g], 16)
            for n, g in enumerate(POOL_SUMS):
                if g == B - 1:
                    continue
                sp.wait_ge(s_summed, n + 1)
                sp.dma_start(out[g * L:(g + 1) * L, :].rearrange(rows, p=P), YT[g]).then_inc(s_out_stored[g], 16)
            for u in range(2):
                lo = (B - 1) * L + u * 2 * P
                sp.wait_ge(s_base_ready, 2 * B - 1 + u)
                sp.dma_start(out[lo:lo + 2 * P, :].rearrange(rows, p=P), XX[:, lo // P:lo // P + 2, :]
                             ).then_inc(s_out_stored[B - 1], 16)
            for g in range(B):
                sp.wait_ge(s_out_stored[g], 16 if g < B - 1 else 32)

        @block.gpsimd
        def _(pool):
            pool.memset(eps, EPS)
            pool.memset(eps_sq, EPS * EPS).then_inc(s_eps_set, 1)
            for i in range(2):
                last = pool.memset(RAW[i][:, 0:KS - 1], 0.0)
            last.then_inc(s_pads_zeroed, 1)
            pool.memset(SD[:, :, 0:1], 0.0).then_inc(s_sd_zero, 1)
            pool.memset(XG[:, :], 0.0).then_inc(s_xg_zero, 1)

            for g in range(B):
                h = g % 2
                pool.wait_ge(s_shift, g + 1)
                pool.wait_ge(s_rstd, g + 1)
                if g >= 2:
                    pool.wait_ge(s_xn2_stored[h], 16 * (g // 2))
                for t in range(TB):
                    ins = pool.tensor_scalar(XN2[h][:, t, :], XX[:, g * TB + t, :], RS[g][:, 1, t:t + 1],
                                             RS[g][:, 3, t:t + 1], ALU.mult, ALU.add)
                ins.then_inc(s_xn2_ready, 1)
                pool.wait_ge(s_xn_ready, g + 1)
                pool.wait_ge(s_xn2_ready, g + 1)
                v = XX[:, g * TB:(g + 1) * TB, :]
                pool.tensor_tensor(v, v, XN[h], ALU.add).then_inc(s_xx_ready, 1)
            pool.wait_ge(s_slots_ready, 1)
            pool.wait_ge(s_slot_filled, 16)
            for t in range(NT):
                pool.indirect_dma_start(out=slot_token,
                                        out_offset=bass.IndirectOffsetOnAxis(ap=SLOT[:, t:t + 1], axis=0),
                                        in_=IDS[:, t:t + 1], in_offset=None).then_inc(s_slot_scattered, 16)

            def rows_of(j):
                pool.wait_ge(s_rows_in, 16 * j)
                pool.sem_inc(s_wait_carrier, 1)
                pool.tensor_copy(CUR[0][:, :], IDX[:, bass.ds(j, 1)]).then_inc(s_idx_cur[0], 1)
                pool.wait_ge(s_idx_cur[0], j + 1)
                pool.sem_inc(s_wait_carrier, 1)
                pool.wait_ge(s_xgt_ps, j)
                pool.sem_inc(s_wait_carrier, 1)
                pool.indirect_dma_start(out=XG[:, :], out_offset=None, in_=ffn_rows,
                                        in_offset=bass.IndirectOffsetOnAxis(ap=CUR[0][:, 0:1], axis=0),
                                        bounds_check=T - 1, oob_is_err=False).then_inc(s_rows_in, 16)

            def put(j):
                pool.wait_ge(s_y_out, 16 * j)
                pool.sem_inc(s_wait_carrier, 1)
                pool.tensor_copy(CUR[1][:, :], IDX[:, bass.ds(j, 1)]).then_inc(s_idx_cur[1], 1)
                pool.wait_ge(s_idx_cur[1], j + 1)
                pool.sem_inc(s_wait_carrier, 1)
                pool.wait_ge(s_finished, j + 2)
                pool.sem_inc(s_wait_carrier, 1)
                pool.indirect_dma_start(out=expert_rows,
                                        out_offset=bass.IndirectOffsetOnAxis(ap=CUR[1][:, 0:1], axis=0),
                                        in_=YO[:, :], in_offset=None,
                                        bounds_check=T - 1, oob_is_err=False).then_inc(s_y_out, 16)

            pool.wait_ge(s_idx_loaded, 16)
            pool.wait_ge(s_xg_zero, 1)
            for h in range(2):
                pool.wait_ge(s_xn2_stored[h], 16 * (B // 2))
            rows_of(0)
            rows_of(1)
            rows_of(2)
            rows_of(3)
            put(0)
            with pool.Fori(2, NBLK - 2) as j:
                rows_of(j + 2)
                put(j - 1)
            for j in range(NBLK - 2, NBLK + 1):
                put(j - 1)
            pool.wait_ge(s_gates_ready, 1)
            n_gated = 0
            for g in POOL_SUMS:
                pool.wait_ge(s_yt_in[g], 16)
                if g < B - 1:
                    pool.wait_ge(s_base_ready, 2 * g + 2)
                for t in range(TB):
                    ins = pool.tensor_scalar(YT[g][:, t, :], YT[g][:, t, :], ALPHA[:, g * TB + t:g * TB + t + 1],
                                             0.0, ALU.mult, ALU.add)
                ins.then_inc(s_gated, 1)
                n_gated += 1
                pool.wait_ge(s_gated, n_gated)
                v = XX[:, g * TB:(g + 1) * TB, :]
                pool.tensor_tensor(v if g == B - 1 else YT[g], YT[g], v, ALU.add).then_inc(s_summed, 1)

        @block.vector
        def _(dve):
            n_chain = [0]

            def chain(ins):
                n_chain[0] += 1
                ins.then_inc(s_route_chain, 1)
                dve.wait_ge(s_route_chain, n_chain[0])

            def tap(f, m, j):
                if j == 0:
                    dve.wait_ge(s_proj_read, 6 * f + m + 1)
                else:
                    dve.wait_ge(s_conv, (6 * f + m) * (KS - 1) + j)
                v = conv_of(m)
                dve.scalar_tensor_tensor(v, RAW[m % 2][:, j:j + L], prm_("taps", m * KS + j, 1), v,
                                         ALU.mult, ALU.add).then_inc(s_conv, 1)

            def q8_squares(f):
                dve.wait_ge(s_silu_q, f + 1)
                dve.wait_ge(s_q8_n, f)
                for h in range(2):
                    q8 = chunks(QKV[:, 4:6, :])[:, h, :, 0:CORR]
                    ins = dve.tensor_tensor(Q8[0][:, h], q8, q8, ALU.mult)
                ins.then_inc(s_q8_sq, 1)

            def statistics(g):
                h = g % 2
                dve.wait_ge(s_ld_x[g], 16)
                for t in range(TB):
                    ins = dve.bn_stats(ST[h][:, t, :], XX[:, g * TB + t, :])
                ins.then_inc(s_stats, 1)
                dve.wait_ge(s_stats, 2 * g + 1)
                for t in range(TB):
                    ins = dve.bn_aggr(MV[g][:, t, :], ST[h][:, t, :])
                ins.then_inc(s_stats, 1)

            def normalise(g):
                h = g % 2
                dve.wait_ge(s_rstd, g + 1)
                dve.wait_ge(s_stats, 2 * g + 2)
                if g >= 2:
                    dve.wait_ge(s_xn_t, g - 1)
                    dve.wait_ge(s_xx_ready, g - 1)
                for n in range(2):
                    ins = dve.scalar_tensor_tensor(RS[g][:, 2 + n, :], MV[g][:, :, 0], -1.0, RS[g][:, n, :],
                                                   ALU.mult, ALU.mult)
                ins.then_inc(s_shift, 1)
                dve.wait_ge(s_shift, g + 1)
                for t in range(TB):
                    ins = dve.tensor_scalar(XN[h][:, t, :], XX[:, g * TB + t, :], RS[g][:, 0, t:t + 1],
                                            RS[g][:, 2, t:t + 1], ALU.mult, ALU.add)
                ins.then_inc(s_xn_ready, 1)

            def split_xt(f):
                dve.wait_ge(s_xt_hi, f + 1)
                if isinstance(f, int) and f == 0:
                    dve.wait_ge(s_xt_ready, 1)
                dve.tensor_tensor(XT_LO[:, :, :], XT[:, :, :], XT_HI[:, :, :].bitcast(fp32), ALU.subtract
                                  ).then_inc(s_xt_lo, 1)

            dve.wait_ge(s_pads_zeroed, 1)
            statistics(0)
            statistics(1)
            for g in range(B):
                normalise(g)
                if g + 2 < B:
                    statistics(g + 2)
                if g == 1:
                    split_xt(0)
                    dve.wait_ge(s_wq_hi, 1)
                    dve.tensor_tensor(WQ_LO[:, :, :], WQKV, WQ_HI[:, :, :].bitcast(fp32), ALU.subtract
                                      ).then_inc(s_wq_lo, 1)
                if g >= 3:
                    for j in range(KS - 1):
                        tap(0, g - 3, j)
            for j in range(KS - 1):
                tap(0, 5, j)

            dve.wait_ge(s_ab_ready, B)
            dve.wait_ge(s_ld_con, 16)
            aff = AB[:, :, 0:E]
            te = [r.rearrange("p (t e) -> p t e", e=E) for r in RT]
            et = [r.rearrange("p (e t) -> p e t", e=E) for r in RT]
            dve.tensor_reduce(MX[:, :], aff, AX, ALU.max).then_inc(s_route_a, 1)
            dve.wait_ge(s_route_a, 1)
            chain(dve.tensor_tensor(te[0], aff, MX[:, :].unsqueeze(2).to_broadcast([P, NT, E]), ALU.is_ge))
            rank8 = con_("rank8").unsqueeze(1).to_broadcast([P, NT, E])
            chain(dve.tensor_tensor(te[1], te[0], rank8, ALU.mult))
            chain(dve.tensor_reduce(SCR[:, 0, :], te[1], AX, ALU.max))
            dve.tensor_tensor(te[2], rank8, SCR[:, 0, :].unsqueeze(2).to_broadcast([P, NT, E]), ALU.is_equal
                              ).then_inc(s_route_a, 1)
            dve.wait_ge(s_counts, 1)
            chain(dve.tensor_copy(et[3], PS[7][:, 0:256].rearrange("p (t e) -> p e t", e=E)))
            chain(dve.tensor_tensor_scan(RT[4], con_("not_first"), RT[3], 0.0, ALU.mult, ALU.add))
            total = et[4][:, :, NT - 1:NT]
            chain(dve.tensor_tensor(et[5], total.to_broadcast([P, E, NT]),
                                    con_("thresholds").rearrange("p (e k) -> p e k", e=E), ALU.is_gt))
            chain(dve.tensor_reduce(RSM[:, 0, :], et[5], AX, ALU.add))
            chain(dve.tensor_tensor_scan(RSM[:, 1, :], ones[:, 0:E], RSM[:, 0, :], 0.0, ALU.mult, ALU.add))
            chain(dve.tensor_tensor(RSM[:, 2, :], RSM[:, 1, :], RSM[:, 0, :], ALU.subtract))
            chain(dve.tensor_scalar(RSM[:, 2, :], RSM[:, 2, :], float(P), None, ALU.mult))
            chain(dve.tensor_tensor(et[5], et[4], et[3], ALU.subtract))
            chain(dve.tensor_tensor(et[5], et[5], RSM[:, 2, :].unsqueeze(2).to_broadcast([P, E, NT]), ALU.add))
            chain(dve.tensor_tensor(te[6], PS[6][:, 0:256].rearrange("p (t e) -> p t e", e=E),
                                    RT[5].rearrange("p (e t) -> p t e", e=E), ALU.add))
            chain(dve.tensor_tensor(te[7], te[6], te[2], ALU.mult))
            chain(dve.tensor_reduce(SCR[:, 1, :], te[7], AX, ALU.add))
            dve.tensor_copy(SLOT[:, :], SCR[:, 1, :]).then_inc(s_slots_ready, 1)
            dve.wait_ge(s_gate_exp, 2)
            chain(dve.tensor_scalar(ALPHA[:, :], ALPHA[:, :], 1.0, None, ALU.add))
            dve.reciprocal(ALPHA[:, :], ALPHA[:, :]).then_inc(s_gates_ready, 1)
            chain(dve.tensor_scalar(BETA[:, :, :], BETA[:, :, :], 1.0, None, ALU.add))
            dve.reciprocal(BETA[:, :, :], BETA[:, :, :]).then_inc(s_gates_ready, 1)
            q8_squares(0)

            def block_table():
                dve.wait_ge(s_xt_stored[1], 32 * (B // 2))
                jb = RB[:, 0:NBLK * E].rearrange("p (j e) -> p j e", e=E)
                eb, slot, turns = (RB[:, 512 + i * 64:512 + i * 64 + NBLK] for i in range(3))
                dve.tensor_copy(CUMB[:, :], RSM[:, 1, :]).then_inc(s_eblk_ready, 1)
                chain(dve.tensor_tensor(jb, con_("block_ids").rearrange("p (j e) -> p j e", e=E),
                                        RSM[:, 1, :].unsqueeze(1).to_broadcast([P, NBLK, E]), ALU.is_ge))
                chain(dve.tensor_reduce(eb, jb, AX, ALU.add))
                chain(dve.tensor_scalar(eb, eb, float(E - 1), None, ALU.min))
                dve.tensor_copy(EB[:, 0, :], eb).then_inc(s_eblk_ready, 1)
                chain(dve.tensor_copy(slot, eb))
                for n in range(RING, E, RING):
                    chain(dve.tensor_scalar(turns, eb, float(n), float(-RING), ALU.is_ge, ALU.mult))
                    chain(dve.tensor_tensor(slot, slot, turns, ALU.add))
                dve.tensor_copy(EB[:, 1, :], slot).then_inc(s_eblk_ready, 1)
                dve.wait_ge(s_ld_prm, 16)
                dve.wait_ge(s_ld_wo, 16)
                for k in range(2):
                    dve.tensor_scalar(WOG[:, k, :], WOG[:, k, :], prm_("g"), None, ALU.mult).then_inc(s_wog_ready, 1)
                dve.sem_inc(s_finished, 1)

            def combine(g):
                dve.wait_ge(s_yt_in[g], 16)
                dve.wait_ge(s_base_ready, 2 * g + 2)
                for t in range(TB):
                    n = g * TB + t
                    ins = dve.scalar_tensor_tensor(YT[g][:, t, :], YT[g][:, t, :], ALPHA[:, n:n + 1],
                                                   XX[:, n, :], ALU.mult, ALU.add)
                ins.then_inc(s_summed_dve, 1)

            def expert(j):
                return dve.value_load(EB[0:1, 0, bass.ds(j, 1)], min_val=0, max_val=E - 1)

            def rows_in(j):
                e = expert(j)
                dve.wait_ge(s_xgt_ps, j + 1)
                dve.wait_ge(s_h_ps, 2 * j)
                for k in range(2):
                    ins = dve.tensor_scalar(XGT[:, k, :], PS[6][:, k * P:(k + 1) * P],
                                            PR[:, bass.ds(e * 2 + (PRM["ln_g"][0] + k), 1)],
                                            PR[:, bass.ds(e * 2 + (PRM["ln_b"][0] + k), 1)], ALU.mult, ALU.add)
                ins.then_inc(s_xgt_ready, 1)

            def relu(j):
                e = expert(j)
                dve.wait_ge(s_ht_ps, 2 * j + 2)
                dve.wait_ge(s_y_ps, j)
                for c in range(4, FC):
                    ins = dve.tensor_scalar(HT[:, c, :], PS[6][:, (c - 4) * P:(c - 3) * P],
                                            PR[:, bass.ds(e * FC + (PRM["b1"][0] + c), 1)], 0.0, ALU.add, ALU.max)
                ins.then_inc(s_ht_dve, 1)

            def finish(j):
                e = expert(j)
                dve.wait_ge(s_y_ps, j + 1)
                dve.wait_ge(s_y_out, 16 * j)
                dve.tensor_tensor(YO[:, :], PS[7][:, 0:D], B2[:, bass.ds(e, 1), :].rearrange("p a d -> p (a d)"),
                                  ALU.add).then_inc(s_finished, 1)

            def part(todo):
                for j, n in next(todo):
                    if n == 0 and is_block(j + 1):
                        rows_in(j + 1)
                    elif n == 1 and is_block(j - 1):
                        finish(j - 1)
                    elif n == 4 and is_block(j):
                        relu(j)
                    elif n == 6:
                        combine(j)

            def coefficients(f):
                dve.wait_ge(s_k_rn, f + 1)
                dve.tensor_tensor(CF[:, :, 1, :], CF[:, :, 0, :], BETA[:, bass.ds(f * TB, TB), :], ALU.mult
                                  ).then_inc(s_coef, 1)

            def back(b, more):
                f = b + 1
                first = isinstance(b, int) and b == 0
                todo = parts_of(b)
                q8 = [chunks(QKV[:, 4:6, :])[:, h, :, 0:CORR] for h in range(2)]
                k8 = [chunks(KTT[:, 0:2, :])[:, h, :, 0:CORR] for h in range(2)]
                part(todo)
                dve.wait_ge(s_coef, b + 1)
                dve.wait_ge(s_wu_done, 4 * b)
                if first:
                    dve.wait_ge(s_xx_ready, B)
                    for h in range(2):
                        dve.wait_ge(s_xn2_stored[h], 16 * (B // 2))
                for p in range(2):
                    for t in (2 * p, 2 * p + 1):
                        dve.wait_ge(s_t1_done, 4 * b + t + 1)
                        ps = PS[(1, 3)[t % 2]]
                        kk = KK[:, t, 0:2 * D].rearrange("p (a h d) -> p a h d", a=2, h=NH)
                        for a in range(2):
                            dve.tensor_tensor(kk[:, a], ps[:, 0:D].rearrange("p (h d) -> p h d", h=NH),
                                              CF[:, t, a, :].unsqueeze(2).to_broadcast([P, NH, HD]), ALU.mult)
                        dve.tensor_tensor(KK[:, t, 2 * D:3 * D].rearrange("p (h d) -> p h d", h=NH),
                                          ps[:, D:2 * D].rearrange("p (h d) -> p h d", h=NH),
                                          BETA[:, bass.ds(b * TB + t, 1), :].rearrange("p a h -> p (a h)")
                                          .unsqueeze(2).to_broadcast([P, NH, HD]), ALU.mult
                                          ).then_inc(s_t1_read, 1)
                    for _ in range(4):
                        part(todo)
                if first:
                    block_table()
                    dve.wait_ge(s_eblk_ready, 3)
                if more:
                    split_xt(f)
                dve.wait_ge(s_kwu_ready, 4 * b)
                dve.wait_ge(s_a_done, b + 1)
                lt = LT[:, :].rearrange("p (t c) -> p t c", c=P)
                dve.tensor_tensor(lt, PS[1][:, :].rearrange("p (t c) -> p t c", c=P),
                                  con_("neg_upper").unsqueeze(1).to_broadcast([P, TB, P]), ALU.mult
                                  ).then_inc(s_a_masked, 1)
                dve.wait_ge(s_a_masked, b + 1)
                dve.tensor_tensor(lt, lt, ident.unsqueeze(1).to_broadcast([P, TB, P]), ALU.add
                                  ).then_inc(s_lt_ready, 1)
                dve.wait_ge(s_lt_ready, b + 1)
                dve.tensor_tensor(XY[:, 1, :].rearrange("p (t c) -> p t c", c=P), lt,
                                  con_("first_merge").unsqueeze(1).to_broadcast([P, TB, P]), ALU.mult
                                  ).then_inc(s_xt_init, 1)
                for h in range(2):
                    ins = dve.tensor_tensor(Q8[1][:, h], q8[h], k8[h], ALU.mult)
                ins.then_inc(s_q8_k, 1)
                dve.wait_ge(s_q8_r, b + 1)
                dve.wait_ge(s_q8_k, b + 1)
                dve.tensor_tensor(Q8[1][:, :, :, :], Q8[1][:, :, :, :], Q8[2][:, :, :, :], ALU.mult
                                  ).then_inc(s_q8_kr, 1)
                for _ in range(3):
                    part(todo)
                for l, s in enumerate(LEVELS):
                    dve.wait_ge(s_lv1_done, NL * b + l + 1)
                    dve.tensor_tensor(WV[:, :].rearrange("p (t c) -> p t c", c=P),
                                      PS[2][:, :].rearrange("p (t c) -> p t c", c=P),
                                      con_("merge", l * P, P).unsqueeze(1).to_broadcast([P, TB, P]), ALU.mult
                                      ).then_inc(s_lv1_read, 1)
                    part(todo)
                    if l == 1:
                        dve.wait_ge(s_a8_done, b + 1)
                        dve.tensor_tensor(A8[:, :, :], PS[3][:, 0:64].rearrange("p (n c) -> p n c", c=CORR),
                                          con_("tril_rows").rearrange("p (b c) -> p b c", b=B)
                                          [:, bass.ds(b, 1), :].to_broadcast([P, NC, CORR]), ALU.mult
                                          ).then_inc(s_a8_masked, 1)
                        dve.wait_ge(s_a8_masked, b + 1)
                        dve.wait_ge(s_q8_n, b + 1)
                        for h in range(2):
                            ins = dve.tensor_tensor(Q8[4][:, h], Q8[3][:, h], A8[:, :, :], ALU.mult)
                        ins.then_inc(s_u8_a, 1)
                    if more:
                        for j in range(KS - 1):
                            tap(f, l, j)
                    part(todo)
                dve.wait_ge(s_lv2_read, NL * b + NL)
                dve.scalar_tensor_tensor(WV[:, :].rearrange("p (t c) -> p t c", c=P),
                                         XY[:, 1, :].rearrange("p (t c) -> p t c", c=P), 3.0,
                                         con_("minus_2i").unsqueeze(1).to_broadcast([P, TB, P]),
                                         ALU.mult, ALU.add).then_inc(s_tt_ready, 1)
                part(todo)
                if more:
                    for j in range(KS - 1):
                        tap(f, 5, j)
                for t in range(TB):
                    dve.wait_ge(s_wu_done, 4 * b + t + 1)
                    ps = PS[(3, 1)[t % 2]][:, :]
                    if t or not first:
                        dve.wait_ge(s_kwu_ready, 4 * b + t - 1)
                    pp = PP[:, t % 2]
                    for a in range(2):
                        ins = dve.tensor_tensor(pp[:, 2 * a:2 * a + 2, :],
                                                ps[:, a * D:(a + 1) * D].rearrange("p (h c) -> p h c", h=2),
                                                KTT[:, 0:2, t * P:(t + 1) * P], ALU.mult)
                    ins.then_inc(s_pp_ready, 1)
                    dve.tensor_copy(WU8[:, :, 2 * t:2 * t + 2, :],
                                    ps.rearrange("p (c n k) -> p c n k", c=4, n=2)[:, :, :, 0:CORR]
                                    ).then_inc(s_wu_read, 1)
                    dve.wait_ge(s_pp_ready, 4 * b + t + 1)
                    dve.tensor_reduce(KWU[:, :, 2 * t:2 * t + 2], pp.rearrange("p c (n k) -> p c n k", n=2),
                                      AX, ALU.add).then_inc(s_kwu_ready, 1)
                    part(todo)
                dve.wait_ge(s_kwu_ready, 4 * b + 4)
                dve.tensor_scalar(KEEP[:, :, :], KWU[:, 0:2, :], -1.0, 1.0, ALU.mult, ALU.add
                                  ).then_inc(s_keep_ready, 1)
                dve.wait_ge(s_keep_ready, b + 1)
                if first:
                    dve.wait_ge(s_sd_zero, 1)
                for h in range(2):
                    ins = dve.tensor_tensor_scan(SD[:, h, 1:NC + 1], KEEP[:, h, :], KWU[:, 2 + h, :], 0.0,
                                                 ALU.mult, ALU.add)
                ins.then_inc(s_scan_ready, 1)
                dve.wait_ge(s_scan_ready, b + 1)
                dve.wait_ge(s_wo_done, 2 * b)
                for h in range(2):
                    ins = dve.tensor_tensor(chunks(Y2[:, :, :])[:, h], chunks(QKV[:, 4:6, :])[:, h],
                                            SD[:, h, 0:NC].unsqueeze(2).to_broadcast([P, NC, C]), ALU.mult)
                ins.then_inc(s_y_ready, 1)
                sd8 = SD[:, :, 0:NC].unsqueeze(3).to_broadcast([P, 2, NC, CORR])
                dve.wait_ge(s_wu_read, 4 * b + 4)
                dve.tensor_tensor(Q8[5][:, :, :, :], WU8[:, 0:2], sd8, ALU.mult).then_inc(s_u8_b, 1)
                dve.wait_ge(s_u8_b, 3 * b + 1)
                dve.tensor_tensor(Q8[5][:, :, :, :], WU8[:, 2:4], Q8[5][:, :, :, :], ALU.subtract
                                  ).then_inc(s_u8_b, 1)
                dve.wait_ge(s_u8_b, 3 * b + 2)
                dve.wait_ge(s_u8_a, b + 1)
                dve.tensor_tensor(Q8[5][:, :, :, :], Q8[5][:, :, :, :], Q8[4][:, :, :, :], ALU.mult
                                  ).then_inc(s_u8_b, 1)
                dve.wait_ge(s_u8_b, 3 * b + 3)
                dve.wait_ge(s_y_ready, b + 1)
                y8 = chunks(Y2[:, :, :])
                for h in range(2):
                    ins = dve.tensor_tensor(y8[:, h, :, 0:CORR], y8[:, h, :, 0:CORR], Q8[5][:, h], ALU.add)
                ins.then_inc(s_y_fixed, 1)
                part(todo)
                part(todo)
                dve.wait_ge(s_ysq_ready, b + 1)
                dve.wait_ge(s_qsq_ready, b + 1)
                dve.tensor_tensor(YS[:, :, :], YS[:, :, :], SQ[:, :, :], ALU.add).then_inc(s_ys_ready, 1)
                if more:
                    q8_squares(f)
                part(todo)
                part(todo)
                for h in range(2):
                    dve.wait_ge(s_yn_r, 2 * b + h + 1)
                    dve.tensor_tensor(Y2[:, h, :], Y2[:, h, :], YS[:, h, :], ALU.mult).then_inc(s_o_ready, 1)
                if more:
                    coefficients(f)
                part(todo)
                part(todo)
                if not more:
                    dve.wait_ge(s_summed, POOL_SUMS.index(B - 1) + 1)
                for u in range(2):
                    dve.wait_ge(s_wo_done, 2 * b + u + 1)
                    v = XX[:, bass.ds(b * TB + 2 * u, 2), :]
                    dve.tensor_tensor(v, PS[(1, 3)[u]][:, :].rearrange("p (t d) -> p t d", t=2), v, ALU.add
                                      ).then_inc(s_base_ready, 1)

            dve.wait_ge(s_gates_ready, 2)
            coefficients(0)
            dve.wait_ge(s_ld_b2, 16)
            back(0, True)
            with dve.Fori(1, B - 2) as b:
                back(b, True)
            back(B - 2, True)
            back(B - 1, False)

        @block.scalar
        def _(act):
            log_exp = "natural_log_exp_and_others"
            act.preload_act_table_set(log_exp)
            act.wait_ge(s_eps_set, 1)

            def load_xt(f):
                act.wait_ge(s_xt_lo, f)
                for k in range(2):
                    act.dma_start(XT[:, k, :], xn_cols[k, :, bass.ds(f * L, L)]).then_inc(s_xt_in, 16)

            def split_xt(f):
                act.wait_ge(s_xt_in, 32 * f)
                act.wait_ge(s_proj_done, 6 * f)
                act.activation(XT_HI[:, :, :], XT[:, :, :], ACT.Copy).then_inc(s_xt_hi, 1)

            def project(f, m):
                n = 6 * f + m
                act.wait_ge(s_proj_done, n + 1)
                if not (isinstance(f, int) and f == 0 and m < 2):
                    act.wait_ge(s_conv, (KS - 1) * (n - 1))
                if m == 0 and not (isinstance(f, int) and f == 0):
                    act.wait_ge(s_t1_done, 4 * f)
                    act.wait_ge(s_ksq_ready, f)
                ps = PS[7 if isinstance(f, int) and f == 0 else 0][:, :]
                act.activation(RAW[m % 2][:, KS - 1:KS - 1 + L], ps, ACT.Copy)
                act.activation(conv_of(m), ps, ACT.Copy, scale=prm_("taps", m * KS + KS - 1, 1)
                               ).then_inc(s_proj_read, 1)

            def silu_kv(f):
                act.wait_ge(s_conv, (KS - 1) * (6 * f + 4))
                act.activation(QKV[:, 0:4, :], QKV[:, 0:4, :], ACT.Silu).then_inc(s_silu_kv, 1)

            def silu_q(f):
                act.wait_ge(s_conv, (KS - 1) * (6 * f + 6))
                act.wait_ge(s_y_fixed, f)
                act.activation(QKV[:, 4:6, :], QC[:, :, :], ACT.Silu).then_inc(s_silu_q, 1)

            def squares_k(f):
                act.wait_ge(s_silu_kv, f + 1)
                act.wait_ge(s_ys_ready, f)
                act.activation(SQ[:, :, :], QKV[:, 0:2, :], ACT.Square).then_inc(s_ksq_ready, 1)

            def scales(g):
                act.wait_ge(s_stats, 2 * g + 2)
                act.activation(RS[g][:, 0, :], MV[g][:, :, 1], ACT.Ln, bias=eps)
                act.activation(RS[g][:, 1, :], MV[g][:, :, 1], ACT.Ln, scale=1.0 + EPS, bias=eps_sq
                               ).then_inc(s_rstd_ln, 1)
                act.wait_ge(s_rstd_ln, g + 1)
                act.activation(RS[g][:, 0:2, :], RS[g][:, 0:2, :], ACT.Exp, scale=-0.5).then_inc(s_rstd, 1)

            def affinities(g):
                act.wait_ge(s_aff_done, g + 1)
                act.activation(AB[:, g * TB:(g + 1) * TB, :],
                               PS[4 + g % 2][:, 0:TB * (E + NH)].rearrange("p (t n) -> p t n", t=TB), ACT.Copy
                               ).then_inc(s_ab_ready, 1)

            scales(0)
            scales(1)
            for g in range(B):
                h = g % 2
                if g + 1 < B and g:
                    scales(g + 1)
                act.wait_ge(s_xn_t, g + 1)
                if g >= 3:
                    act.wait_ge(s_aff_done, g - 1)
                    act.wait_ge(s_xt_stored[h], 32 * ((g - 1) // 2))
                if g == 0:
                    for k in range(2):
                        ins = act.activation(XT_HI[:, k, :], PS[k][:, :], ACT.Copy)
                    ins.then_inc(s_xt_hi, 1)
                for k in range(2):
                    ins = act.activation(columns_of(g)[:, k, :], PS[2 * h + k][:, :], ACT.Copy)
                ins.then_inc(s_xt_ready, 1)
                if g:
                    affinities(g - 1)
                if g == 0:
                    act.wait_ge(s_ld_wqkv, 16)
                    act.activation(WQ_HI[:, :, :], WQKV, ACT.Copy).then_inc(s_wq_hi, 1)
                if g == 1:
                    act.wait_ge(s_ld_prm, 16)
                if 1 <= g <= 6:
                    project(0, g - 1)
            affinities(B - 1)
            silu_kv(0)
            silu_q(0)
            act.preload_act_table_set(log_exp)
            squares_k(0)
            act.wait_ge(s_route_a, 1)
            act.wait_ge(s_ab_ready, B)
            act.activation(ALPHA[:, :], MX[:, :], ACT.Exp, scale=-1.0).then_inc(s_gate_exp, 1)
            act.activation(BETA[:, :, :], AB[:, :, E:E + NH], ACT.Exp, scale=-1.0).then_inc(s_gate_exp, 1)

            def hidden(j, h):
                act.wait_ge(s_h_ps, 2 * j + h + 1)
                if not (isinstance(j, int) and j == 0):
                    act.wait_ge(s_ht_ps, 2 * j + h - 1)
                act.activation(H[:, h, :], PS[4 + h][:, :], ACT.Copy).then_inc(s_h_act, 1)

            def relu(j):
                e = act.value_load(EB[0:1, 0, bass.ds(j, 1)], min_val=0, max_val=E - 1)
                act.wait_ge(s_ht_ps, 2 * j + 1)
                act.wait_ge(s_y_ps, j)
                for c in range(4):
                    ins = act.activation(HT[:, c, :], PS[6][:, c * P:(c + 1) * P], ACT.Relu,
                                         bias=PR[:, bass.ds(e * FC + (PRM["b1"][0] + c), 1)])
                ins.then_inc(s_ht_act, 1)

            def part(todo):
                for j, n in next(todo):
                    if n == 2 and is_block(j):
                        relu(j)
                    elif n == 3 and is_block(j + 1):
                        hidden(j + 1, 0)
                    elif n == 5 and is_block(j + 1):
                        hidden(j + 1, 1)

            def head(f):
                act.wait_ge(s_head_ss, f + 1)
                act.wait_ge(s_k_rn, f)
                act.activation(RK[:, :, :], PS[0][:, 0:TB * NH].rearrange("p (t h) -> p t h", t=TB), ACT.Ln
                               ).then_inc(s_k_ln, 1)
                act.wait_ge(s_u8_a, f)
                act.activation(Q8[0][:, :, :, :], PS[0][:, P:2 * P].rearrange("p (h n c) -> p h n c", h=2, n=NC),
                               ACT.Ln).then_inc(s_q8_ln, 1)
                act.wait_ge(s_k_ln, f + 1)
                act.wait_ge(s_t1_read, 4 * f)
                act.activation(CF[:, :, 0, :], RK[:, :, :], ACT.Exp, scale=-0.5).then_inc(s_k_rn, 1)
                act.wait_ge(s_q8_ln, f + 1)
                act.activation(Q8[2][:, :, :, :], Q8[0][:, :, :, :], ACT.Exp, scale=-0.5).then_inc(s_q8_r, 1)
                act.activation(Q8[3][:, :, :, :], Q8[0][:, :, :, :], ACT.Exp, scale=0.5).then_inc(s_q8_n, 1)
                act.wait_ge(s_silu_q, f + 1)
                act.activation(SQ[:, :, :], QKV[:, 4:6, :], ACT.Square, scale=EPS ** 0.5).then_inc(s_qsq_ready, 1)

            def back(b, more):
                f = b + 1
                todo = parts_of(b)
                part(todo)
                if more:
                    split_xt(f)
                act.wait_ge(s_kwu_ready, 4 * b)
                for p in range(2):
                    part(todo)
                    part(todo)
                    for t in (2 * p, 2 * p + 1):
                        act.wait_ge(s_t2_done, 4 * b + t + 1)
                        act.activation(KTT[:, :, t * P:(t + 1) * P],
                                       PS[(1, 3)[t % 2]][:, :].rearrange("p (c t) -> p c t", c=4), ACT.Copy
                                       ).then_inc(s_t2_read, 1)
                    part(todo)
                    part(todo)
                if isinstance(b, int) and b == 0:
                    act.wait_ge(s_eblk_ready, 3)
                part(todo)
                part(todo)
                act.wait_ge(s_x_init, b + 1)
                act.activation(XY[:, 0, :], PS[3][:, :], ACT.Copy).then_inc(s_xy_ready, 1)
                if more:
                    project(f, 0)
                part(todo)
                for l, s in enumerate(LEVELS):
                    part(todo)
                    act.wait_ge(s_lv2_done, NL * b + l + 1)
                    nb = L // (2 * s)
                    if l < NL - 1:
                        out_ = bass.AP(XY, 0, [[2 * L, P], [L + s, 2], [2 * s, nb], [1, s]])
                        act.activation(out_, PS[2][:, :].rearrange("p (x n c) -> p x n c", x=2, c=s), ACT.Copy
                                       ).then_inc(s_lv2_read, 1)
                    else:
                        act.activation(XY[:, 1, :].rearrange("p (n c) -> p n c", c=2 * s)[:, :, s:2 * s],
                                       PS[2][:, L // 2:L].rearrange("p (n c) -> p n c", c=s), ACT.Copy
                                       ).then_inc(s_lv2_read, 1)
                    if more:
                        project(f, l + 1)
                    part(todo)
                part(todo)
                part(todo)
                if more:
                    silu_kv(f)
                for _ in range(TB - 1):
                    part(todo)
                act.wait_ge(s_y_fixed, b + 1)
                act.wait_ge(s_o_ready, 2 * b)
                act.activation(YS[:, :, :], Y2[:, :, :], ACT.Square, scale=HD ** -0.5).then_inc(s_ysq_ready, 1)
                if more:
                    silu_q(f)
                    squares_k(f)
                part(todo)
                part(todo)
                act.preload_act_table_set(log_exp)
                for h in range(2):
                    act.wait_ge(s_yn_done, 2 * b + h + 1)
                    act.activation(YS[:, h, :], PS[2 + h][:, :], ACT.Ln).then_inc(s_yn_ln, 1)
                    act.wait_ge(s_yn_ln, 2 * b + h + 1)
                    act.activation(YS[:, h, :], YS[:, h, :], ACT.Exp, scale=-0.5).then_inc(s_yn_r, 1)
                if more:
                    head(f)
                    if not (isinstance(b, int) and b == B - 2):
                        load_xt(f + 1)
                part(todo)
                part(todo)
                part(todo)
                part(todo)

            for h in range(2):
                act.wait_ge(s_xt_stored[h], 32 * (B // 2 - 1 + h))
            load_xt(1)
            head(0)
            back(0, True)
            with act.Fori(1, B - 2) as b:
                back(b, True)
            back(B - 2, True)
            back(B - 1, False)
            for g in range(B - 1 - sum(SUMS), B - 1):
                act.wait_ge(s_summed_dve, g - (B - 1 - sum(SUMS)) + 1)
                act.dma_start(out[g * L:(g + 1) * L, :].rearrange(rows, p=P), YT[g]).then_inc(s_out_stored[g], 16)

        @block.tensor
        def _(pe):
            pe.wait_ge(s_ld_ident, 16)

            def project(f, m, k):
                first = isinstance(f, int) and f == 0
                if k == 0:
                    if not (first and m == 0):
                        pe.wait_ge(s_proj_read, 6 * f + m)
                    if m == 0 and not first:
                        pe.wait_ge(s_k_ln, f)
                        pe.wait_ge(s_q8_ln, f)
                    if m == 0:
                        pe.wait_ge(s_xt_lo, f + 1)
                for n, (w, v) in enumerate(((WQ_LO, XT_HI), (WQ_HI, XT_LO), (WQ_HI, XT_HI))):
                    ins = pe.matmul(PS[7 if first else 0][:, :], w[:, k, m * P:(m + 1) * P], v[:, k, :],
                                    start=(k == 0 and n == 0), stop=(k == 1 and n == 2))
                if k:
                    ins.then_inc(s_proj_done, 1)

            def columns(g):
                h = g % 2
                pe.wait_ge(s_xn_ready, g + 1)
                if g >= 2:
                    pe.wait_ge(s_xt_ready, g - 1)
                for k in range(2):
                    for t in range(TB):
                        ins = pe.transpose(PS[2 * h + k][:, t * P:(t + 1) * P],
                                           XN[h][:, t, k * P:(k + 1) * P], ident)
                ins.then_inc(s_xn_t, 1)

            def affinities(g):
                n = E + NH
                pe.wait_ge(s_xt_ready, g + 1)
                if g >= 2:
                    pe.wait_ge(s_ab_ready, g - 1)
                for t in range(TB):
                    for k in range(2):
                        ins = pe.matmul(PS[4 + g % 2][:, t * n:(t + 1) * n], columns_of(g)[:, k, t * P:(t + 1) * P],
                                        CW[:, k, :], start=(k == 0), stop=(k == 1))
                ins.then_inc(s_aff_done, 1)

            columns(0)
            pe.wait_ge(s_ld_prm, 16)
            for g in range(B):
                if g + 1 < B:
                    columns(g + 1)
                affinities(g)
                if g == 0:
                    pe.wait_ge(s_wq_lo, 1)
                if g < 6:
                    project(0, g, 0)
                    project(0, g, 1)

            def rows_t(j):
                pe.wait_ge(s_rows_in, 16 * j + 16)
                if not (isinstance(j, int) and j == 0):
                    pe.wait_ge(s_ht_dve, j - 1)
                for k in range(2):
                    ins = pe.transpose(PS[6][:, k * P:(k + 1) * P], XG[:, k * P:(k + 1) * P], ident)
                ins.then_inc(s_xgt_ps, 1)

            def slot_of(j):
                return pe.value_load(EB[0:1, 1, bass.ds(j, 1)], min_val=0, max_val=RING - 1)

            def up(j, h):
                slot = slot_of(j)
                if h == 0:
                    e = pe.value_load(EB[0:1, 0, bass.ds(j, 1)], min_val=0, max_val=E - 1)
                    pe.wait_ge(s_w_ready, e + 1)
                    pe.wait_ge(s_xgt_ready, j + 1)
                if not (isinstance(j, int) and j == 0):
                    pe.wait_ge(s_h_act, 2 * j + h - 1)
                for k in range(2):
                    ins = pe.matmul(PS[4 + h][:, :], XGT[:, k, :], w1_of(slot, k, h), start=(k == 0), stop=(k == 1))
                ins.then_inc(s_h_ps, 1)

            def turn(j, u):
                pe.wait_ge(s_h_act, 2 * j + u + 1)
                if u == 0:
                    pe.wait_ge(s_xgt_ready, j + 2 if is_block(j + 1) else j + 1)
                else:
                    pe.wait_ge(s_ht_act, j + 1)
                for c in range(4):
                    ins = pe.transpose(PS[6][:, c * P:(c + 1) * P], H[:, u, c * P:(c + 1) * P], ident)
                ins.then_inc(s_ht_ps, 1)

            def down(j, u):
                slot = slot_of(j)
                if u == 0:
                    pe.wait_ge(s_ht_act, j + 1)
                    pe.wait_ge(s_finished, j + 1)
                else:
                    pe.wait_ge(s_ht_dve, j + 1)
                for c in range(4 * u, 4 * u + 4):
                    ins = pe.matmul(PS[7][:, 0:D], HT[:, c, :], w2_of(slot, c), start=(c == 0), stop=(c == FC - 1))
                if u:
                    ins.then_inc(s_y_ps, 1)

            def part(todo):
                for j, n in next(todo):
                    if n == 0:
                        if is_block(j + 1):
                            rows_t(j + 1)
                        if is_block(j - 1):
                            down(j - 1, 0)
                    elif n == 1 and is_block(j - 1):
                        down(j - 1, 1)
                    elif n in (2, 4) and is_block(j):
                        turn(j, (n - 2) // 2)
                    elif n in (3, 5) and is_block(j + 1):
                        up(j + 1, (n - 3) // 2)

            def head(f):
                pe.wait_ge(s_ksq_ready, f + 1)
                pe.wait_ge(s_q8_sq, f + 1)
                pe.wait_ge(s_proj_read, 6 * f + 6)
                for t in range(TB):
                    for h in range(2):
                        pe.matmul(PS[0][:, t * NH + 2 * h:t * NH + 2 * h + 2], SQ[:, h, t * P:(t + 1) * P],
                                  con_("head_cols"), start=True, stop=True)
                pe.matmul(PS[0][:, P:2 * P], con_("head_ones"), Q8[0][:, :, :, :].rearrange("p h n c -> p (h n c)"),
                          start=True, stop=True).then_inc(s_head_ss, 1)

            def back(b, more):
                f = b + 1
                todo = parts_of(b)
                part(todo)
                pe.wait_ge(s_silu_kv, b + 1)
                pe.wait_ge(s_base_ready, 2 * b)
                for p in range(2):
                    for t in (2 * p, 2 * p + 1):
                        if p:
                            pe.wait_ge(s_t2_read, 4 * b + t - 1)
                        for c in range(4):
                            ins = pe.transpose(PS[(1, 3)[t % 2]][:, c * P:(c + 1) * P],
                                               QKV[:, c, t * P:(t + 1) * P], ident)
                        ins.then_inc(s_t1_done, 1)
                    part(todo)
                    part(todo)
                    for t in (2 * p, 2 * p + 1):
                        pe.wait_ge(s_t1_read, 4 * b + t + 1)
                        for c in range(4):
                            ins = pe.transpose(PS[(1, 3)[t % 2]][:, c * P:(c + 1) * P],
                                               KK[:, t, c * P:(c + 1) * P], ident)
                        ins.then_inc(s_t2_done, 1)
                    part(todo)
                    part(todo)
                if isinstance(b, int) and b == 0:
                    pe.wait_ge(s_eblk_ready, 3)
                    pe.wait_ge(s_wog_ready, 2)
                pe.wait_ge(s_t2_read, 4 * b + 4)
                for t in range(TB):
                    sl = slice(t * P, (t + 1) * P)
                    for h in range(2):
                        ins = pe.matmul(PS[1][:, sl], KTT[:, h, sl], KTT[:, 2 + h, sl], start=(h == 0), stop=(h == 1))
                ins.then_inc(s_a_done, 1)
                part(todo)
                part(todo)
                pe.wait_ge(s_xt_init, b + 1)
                for t in range(TB):
                    sl = slice(t * P, (t + 1) * P)
                    ins = pe.transpose(PS[3][:, sl], XY[:, 1, sl], ident)
                ins.then_inc(s_x_init, 1)
                if more:
                    project(f, 0, 0)
                    project(f, 0, 1)
                part(todo)
                for l, s in enumerate(LEVELS):
                    if l == 0:
                        pe.wait_ge(s_xy_ready, b + 1)
                        pe.wait_ge(s_yn_ln, 2 * b)
                    else:
                        pe.wait_ge(s_lv2_read, NL * b + l)
                    for t in range(TB):
                        sl = slice(t * P, (t + 1) * P)
                        ins = pe.matmul(PS[2][:, sl], LT[:, sl], XY[:, 0, sl], start=True, stop=True)
                    ins.then_inc(s_lv1_done, 1)
                    if l == 0:
                        pe.wait_ge(s_q8_kr, b + 1)
                        for h in range(2):
                            ins = pe.matmul(PS[3][:, 0:64], ones, Q8[1][:, h].rearrange("p n c -> p (n c)"),
                                            start=(h == 0), stop=(h == 1))
                        ins.then_inc(s_a8_done, 1)
                    if more:
                        project(f, l + 1, 0)
                        project(f, l + 1, 1)
                    part(todo)
                    pe.wait_ge(s_lv1_read, NL * b + l + 1)
                    nb = P // (2 * s)
                    for x in range(2) if l < NL - 1 else (1,):
                        for t in range(TB):
                            o = PS[2][:, (x * TB + t) * 64:(x * TB + t + 1) * 64]
                            wv = WV[:, t * P:(t + 1) * P]
                            if x == 0:
                                ins = pe.matmul(o.rearrange("p (n c) -> p n c", n=nb), XY[:, 1, t * P:(t + 1) * P],
                                                cols(wv, 0, s), start=True, stop=True)
                            else:
                                ins = pe.matmul(o.rearrange("p (n c) -> p n c", n=nb), wv,
                                                cols(XY[:, 1, t * P:(t + 1) * P], 1, s), start=True, stop=True)
                    ins.then_inc(s_lv2_done, 1)
                    part(todo)
                part(todo)
                pe.wait_ge(s_tt_ready, b + 1)
                for t in range(TB):
                    if t == 0:
                        pe.wait_ge(s_a8_masked, b + 1)
                    elif t > 1:
                        pe.wait_ge(s_wu_read, 4 * b + t - 1)
                    for c in range(4):
                        ins = pe.matmul(PS[(3, 1)[t % 2]][:, c * P:(c + 1) * P],
                                        KK[:, t, (2 + c) * P:(3 + c) * P], WV[:, t * P:(t + 1) * P],
                                        start=True, stop=True)
                    ins.then_inc(s_wu_done, 1)
                    part(todo)
                part(todo)
                part(todo)
                pe.wait_ge(s_ys_ready, b + 1)
                pe.wait_ge(s_wu_read, 4 * b + 4)
                for h in range(2):
                    pe.matmul(PS[2 + h][:, :], con_("head_ones"), YS[:, h, :], start=True, stop=True
                              ).then_inc(s_yn_done, 1)
                part(todo)
                if more:
                    head(f)
                part(todo)
                pe.wait_ge(s_o_ready, 2 * b + 2)
                for u in range(2):
                    for t in (2 * u, 2 * u + 1):
                        for h in range(2):
                            ins = pe.matmul(PS[(1, 3)[u]][:, (t % 2) * D:(t % 2 + 1) * D],
                                            Y2[:, h, t * P:(t + 1) * P], WOG[:, h, :],
                                            start=(h == 0), stop=(h == 1))
                    ins.then_inc(s_wo_done, 1)
                part(todo)
                part(todo)

            pe.wait_ge(s_ld_con, 16)
            pe.wait_ge(s_route_a, 2)
            pe.wait_ge(s_ab_ready, B)
            pe.matmul(PS[6][:, 0:256], con_("earlier"), RT[2], start=True, stop=True)
            pe.wait_ge(s_proj_read, 6)
            pe.matmul(PS[7][:, 0:256], ones, RT[2], start=True, stop=True).then_inc(s_counts, 1)
            head(0)
            back(0, True)
            with pe.Fori(1, B - 2) as b:
                back(b, True)
            back(B - 2, True)
            back(B - 1, False)


def constants():
    import numpy as np
    p = np.arange(P)[:, None]
    q = np.arange(P)[None, :]
    same_head = (p // HD == q // HD).astype(np.float32)
    lower = ((p // C == q // C) & (p > q)).astype(np.float32)
    parts = {
        "ident": np.eye(P), "ones": np.ones((P, P)), "head_ones": same_head,
        "head_cols": (p // HD == np.arange(2)[None, :]),
        "neg_upper": -lower.T,
        "minus_2i": -2.0 * np.eye(P),
        "tril_rows": np.tile((np.arange(CORR)[None, :] <= np.arange(B)[:, None]).reshape(1, -1), (P, 1)),
        "earlier": (p < q),
        "rank8": np.tile(E - np.arange(E), (P, 1)),
        "thresholds": np.tile(np.where(np.arange(NT) > 0, P * np.arange(NT), -1), (P, E)),
        "block_ids": np.tile(np.repeat(np.arange(NBLK), E), (P, 1)),
        "not_first": np.tile((np.arange(NT) > 0), (P, E)),
    }
    x1 = np.eye(P) + ((p == q + 1) & (p % 2 == 1))
    parts["first_merge"] = x1.T
    parts["merge"] = np.concatenate([(p == q) | ((p // (2 * s) == q // (2 * s)) & (p % (2 * s) >= s)
                                                 & (q % (2 * s) < s)) for s in LEVELS], 1)
    out = np.zeros((P, CON_W), np.float32)
    for name, (at, w) in CON.items():
        out[:, at:at + w] = parts[name]
    ids = np.concatenate([P * np.arange(NT)[None, :] + p, np.full((P, NBLK), T)], 1).astype(np.int32)
    return out, ids


def kernel(L0_attn_x, L0_attn_Wq, L0_attn_Wk, L0_attn_Wv, L0_attn_Wb, L0_attn_conv_q, L0_attn_conv_k,
           L0_attn_conv_v, L0_attn_g, L0_attn_Wo, L0_ffn_centroids, L0_ffn_ln_g, L0_ffn_ln_b, L0_ffn_w1,
           L0_ffn_b1, L0_ffn_w2, L0_ffn_b2):
    import numpy as np
    import concourse.bacc as bacc
    from concourse.bass_utils import run_bass_kernel_spmd

    a = np.ascontiguousarray
    con, ids = constants()
    by_part = lambda v, n: np.asarray(v).reshape(-1, n, P).transpose(2, 0, 1).reshape(P, -1)
    taps = np.concatenate([np.asarray(w).reshape(2, P, KS).transpose(1, 0, 2).reshape(P, 2 * KS)
                           for w in (L0_attn_conv_k, L0_attn_conv_v, L0_attn_conv_q)], 1)
    cw = np.concatenate([np.asarray(L0_ffn_centroids).T, np.asarray(L0_attn_Wb)], 1)
    prm = np.concatenate([taps, by_part(L0_ffn_ln_g, 2), by_part(L0_ffn_ln_b, 2), by_part(L0_ffn_b1, FC),
                          np.tile(np.asarray(L0_attn_g), 2).reshape(P, 1),
                          cw.reshape(2, P, E + NH).transpose(1, 0, 2).reshape(P, -1)], 1)
    arrays = {
        "x": a(np.asarray(L0_attn_x).reshape(T, D)), "con": con, "ids": ids, "prm": a(prm),
        "wqkv": a(np.concatenate([L0_attn_Wk, L0_attn_Wv, L0_attn_Wq], 1)), "wo": a(L0_attn_Wo),
        "w1": a(L0_ffn_w1), "w2": a(L0_ffn_w2), "b2": a(np.asarray(L0_ffn_b2).reshape(E * D)),
    }
    nc = bacc.Bacc("TRN2", target_bir_lowering=False, num_devices=1)
    aps = {n: nc.dram_tensor(n, v.shape, mybir.dt.from_np(v.dtype), kind="ExternalInput").ap()
           for n, v in arrays.items()}
    out = nc.dram_tensor("out", (T, D), mybir.dt.float32, kind="ExternalOutput").ap()
    block_kernel(nc, **aps, out=out)
    r = run_bass_kernel_spmd(nc, [arrays], core_ids=[0])
    return r.results[0]["out"].reshape(B, L, D)
```
